# Optimizing a Trainium2 kernel written in Bass

```python
import numpy as np
import jax
import jax.numpy as jnp

def _softmax(x, axis=-1):
    return jax.nn.softmax(x, axis=axis)

def _gelu(x):
    return jax.nn.gelu(x, approximate=True)

def _silu(x):
    return jax.nn.silu(x)

def _sigmoid(x):
    return jax.nn.sigmoid(x)

def _layernorm(x, axis=-1, eps=1e-05):
    m = jnp.mean(x, axis=axis, keepdims=True)
    v = jnp.var(x, axis=axis, keepdims=True)
    return (x - m) / jnp.sqrt(v + eps)

def _scatter_add(tgt, idx, src, axis=0):
    return tgt.at[idx].add(src)

def _segment_sum(src, seg, n):
    return jax.ops.segment_sum(src, seg, n)
kernel_name = 'mk_seq_preln_d2_jaxref_r8_e67c14'

def setup_inputs(seed: int=0):
    np.random.seed(seed)
    _w = jnp.asarray

    def _L0_attn_setup():
        import jax, jax.numpy as jnp
        import numpy as np
        HEADS, DK, DV = (16, 16, 64)
        EPS = 1e-12

        def l2norm(t):
            n = jnp.linalg.norm(t, axis=-1, keepdims=True)
            return t / jnp.maximum(n, EPS)

        def tanh_norm(t):
            n = jnp.linalg.norm(t, axis=-1, keepdims=True)
            return jnp.tanh(n) * (t / jnp.maximum(n, EPS))

        def split_heads(x, h):
            b, n, hd = x.shape
            return x.reshape(b, n, h, hd // h).transpose(0, 2, 1, 3)
        key = jax.random.key(seed)
        k1, k2, k3, k4 = jax.random.split(key, 4)
        b, n, dim = (2, 256, 128)
        tokens = jax.random.normal(k1, (b, n, dim), dtype=jnp.float32)
        Wq = jax.random.normal(k2, (dim, DK * HEADS), dtype=jnp.float32) * 0.02
        Wkv = jax.random.normal(k3, (dim, (DK + DV) * HEADS), dtype=jnp.float32) * 0.02
        Wout = jax.random.normal(k4, (DV * HEADS, dim), dtype=jnp.float32) * 0.02
        return {'tokens': tokens, 'Wq': Wq, 'Wkv': Wkv, 'Wout': Wout}
    _L0_attn_in = _L0_attn_setup()

    def _L0_ffn_setup():
        import jax, jax.numpy as jnp
        import numpy as np
        DIM = 128
        HIDDEN = 384
        SCALE = 1.0 / 127.0

        def _dequant(w_int, dtype):
            return w_int.astype(dtype) * jnp.asarray(SCALE, dtype)
        key = jax.random.key(seed)
        k_x, k_g, k_u, k_d = jax.random.split(key, 4)
        x = jax.random.normal(k_x, (4, 256, DIM), dtype=jnp.float32)
        w_gate = jax.random.randint(k_g, (HIDDEN, DIM), -127, 128, dtype=jnp.int32)
        w_up = jax.random.randint(k_u, (HIDDEN, DIM), -127, 128, dtype=jnp.int32)
        w_down = jax.random.randint(k_d, (DIM, HIDDEN), -127, 128, dtype=jnp.int32)
        return {'x': x, 'w_gate': w_gate, 'w_up': w_up, 'w_down': w_down}
    _L0_ffn_in = _L0_ffn_setup()

    def _L1_attn_setup():
        import jax, jax.numpy as jnp
        import numpy as np
        import math
        D_MODEL = 128
        LAYER_ID = 6
        NUM_LAYERS = 12
        B, T = (8, 256)
        MIN_P = -1e+38

        def _init_params():
            C = D_MODEL
            r01 = LAYER_ID / (NUM_LAYERS - 1)
            r1a0 = 1.0 - LAYER_ID / NUM_LAYERS
            h = np.arange(C, dtype=np.float32)
            decay_speed = -5.0 + 8.0 * (h / (C - 1)) ** (0.7 + 1.3 * r01)
            zigzag = ((np.arange(C) + 1) % 3 - 1).astype(np.float32) * 0.5
            U = np.float32(math.log(0.3)) + zigzag
            xx = (np.arange(C, dtype=np.float32) / C).reshape(1, 1, C)
            tmk = xx ** r1a0
            tmv = xx ** r1a0 + 0.3 * r01
            tmr = xx ** (0.5 * r1a0)
            return (jnp.asarray(decay_speed), jnp.asarray(U), jnp.asarray(tmk, jnp.float32), jnp.asarray(tmv, jnp.float32), jnp.asarray(tmr, jnp.float32))

        def _wkv(W, U, k, v):
            w = -jnp.exp(W)
            Bb, Tt, Cc = k.shape
            aa0 = jnp.zeros((Bb, Cc), k.dtype)
            bb0 = jnp.zeros((Bb, Cc), k.dtype)
            pp0 = jnp.full((Bb, Cc), MIN_P, k.dtype)

            def step(carry, kv_t):
                aa, bb, pp = carry
                kt, vt = kv_t
                ww = U + kt
                p = jnp.maximum(pp, ww)
                e1 = jnp.exp(pp - p)
                e2 = jnp.exp(ww - p)
                y = (e1 * aa + e2 * vt) / (e1 * bb + e2)
                ww2 = pp + w
                p2 = jnp.maximum(ww2, kt)
                e1b = jnp.exp(ww2 - p2)
                e2b = jnp.exp(kt - p2)
                return ((e1b * aa + e2b * vt, e1b * bb + e2b, p2), y)
            kT = jnp.swapaxes(k, 0, 1)
            vT = jnp.swapaxes(v, 0, 1)
            _, yT = jax.lax.scan(step, (aa0, bb0, pp0), (kT, vT))
            return jnp.swapaxes(yT, 0, 1)

        def _reference_tuple_inner(x, W, U, time_mix_k, time_mix_v, time_mix_r, Wk, Wv, Wr, Wo):
            xs = jnp.pad(x, ((0, 0), (1, 0), (0, 0)))[:, :-1]
            xk = x * time_mix_k + xs * (1.0 - time_mix_k)
            xv = x * time_mix_v + xs * (1.0 - time_mix_v)
            xr = x * time_mix_r + xs * (1.0 - time_mix_r)
            K = jnp.einsum('btc,dc->btd', xk, Wk)
            V = jnp.einsum('btc,dc->btd', xv, Wv)
            R = jnp.einsum('btc,dc->btd', xr, Wr)
            wkv = _wkv(W, U, K, V)
            hidden = jax.lax.stop_gradient(wkv[:, -1, :])
            rwkv = jax.nn.sigmoid(R) * wkv
            output = jnp.einsum('btc,dc->btd', rwkv, Wo)
            return (output, hidden)
        key = jax.random.key(seed)
        k0, k1, k2, k3, k4 = jax.random.split(key, 5)
        W, U, tmk, tmv, tmr = _init_params()
        C = D_MODEL
        s = 1.0 / math.sqrt(C)
        return {'x': jax.random.normal(k0, (B, T, C), jnp.float32), 'W': W, 'U': U, 'time_mix_k': tmk, 'time_mix_v': tmv, 'time_mix_r': tmr, 'Wk': jax.random.normal(k1, (C, C), jnp.float32) * s, 'Wv': jax.random.normal(k2, (C, C), jnp.float32) * s, 'Wr': jax.random.normal(k3, (C, C), jnp.float32) * s, 'Wo': jax.random.normal(k4, (C, C), jnp.float32) * s}
    _L1_attn_in = _L1_attn_setup()

    def _L1_ffn_setup():
        import math
        import jax, jax.numpy as jnp
        import numpy as np
        D_MODEL = 128
        D_HIDDEN = 512
        N_EXPERTS = 8
        TOP_K = 2
        CAPACITY_FACTOR = 1.25
        key = jax.random.key(seed)
        ks = jax.random.split(key, 8)
        s = 0.02
        x = jax.random.normal(ks[0], (4, 256, D_MODEL), dtype=jnp.float32)
        router_w = jax.random.normal(ks[1], (D_MODEL, N_EXPERTS), dtype=jnp.float32) * s
        router_b = jnp.zeros((N_EXPERTS,), dtype=jnp.float32)
        w1 = jax.random.normal(ks[2], (N_EXPERTS, D_MODEL, D_HIDDEN), dtype=jnp.float32) * s
        b1 = jnp.zeros((N_EXPERTS, D_HIDDEN), dtype=jnp.float32)
        w2 = jax.random.normal(ks[3], (N_EXPERTS, D_HIDDEN, D_MODEL), dtype=jnp.float32) * s
        b2 = jnp.zeros((N_EXPERTS, D_MODEL), dtype=jnp.float32)
        return {'x': x, 'router_w': router_w, 'router_b': router_b, 'w1': w1, 'b1': b1, 'w2': w2, 'b2': b2}
    _L1_ffn_in = _L1_ffn_setup()
    _d = {'L0_attn_tokens': _L0_attn_in['tokens'], 'L0_attn_Wq': _L0_attn_in['Wq'], 'L0_attn_Wkv': _L0_attn_in['Wkv'], 'L0_attn_Wout': _L0_attn_in['Wout'], 'L0_ffn_w_gate': _L0_ffn_in['w_gate'], 'L0_ffn_w_up': _L0_ffn_in['w_up'], 'L0_ffn_w_down': _L0_ffn_in['w_down'], 'L1_attn_W': _L1_attn_in['W'], 'L1_attn_U': _L1_attn_in['U'], 'L1_attn_time_mix_k': _L1_attn_in['time_mix_k'], 'L1_attn_time_mix_v': _L1_attn_in['time_mix_v'], 'L1_attn_time_mix_r': _L1_attn_in['time_mix_r'], 'L1_attn_Wk': _L1_attn_in['Wk'], 'L1_attn_Wv': _L1_attn_in['Wv'], 'L1_attn_Wr': _L1_attn_in['Wr'], 'L1_attn_Wo': _L1_attn_in['Wo'], 'L1_ffn_router_w': _L1_ffn_in['router_w'], 'L1_ffn_router_b': _L1_ffn_in['router_b'], 'L1_ffn_w1': _L1_ffn_in['w1'], 'L1_ffn_b1': _L1_ffn_in['b1'], 'L1_ffn_w2': _L1_ffn_in['w2'], 'L1_ffn_b2': _L1_ffn_in['b2']}
    _x0 = _d['L0_attn_tokens']
    _d['L0_attn_tokens'] = jax.random.normal(jax.random.fold_in(jax.random.key(seed), 1), (8, 256, 128), dtype=_x0.dtype)
    del _x0
    return _d

def reference(L0_attn_tokens, L0_attn_Wq, L0_attn_Wkv, L0_attn_Wout, L0_ffn_w_gate, L0_ffn_w_up, L0_ffn_w_down, L1_attn_W, L1_attn_U, L1_attn_time_mix_k, L1_attn_time_mix_v, L1_attn_time_mix_r, L1_attn_Wk, L1_attn_Wv, L1_attn_Wr, L1_attn_Wo, L1_ffn_router_w, L1_ffn_router_b, L1_ffn_w1, L1_ffn_b1, L1_ffn_w2, L1_ffn_b2):

    def _L0_attn_ref(tokens, Wq, Wkv, Wout):
        import jax, jax.numpy as jnp
        import numpy as np
        HEADS, DK, DV = (16, 16, 64)
        EPS = 1e-12

        def l2norm(t):
            n = jnp.linalg.norm(t, axis=-1, keepdims=True)
            return t / jnp.maximum(n, EPS)

        def tanh_norm(t):
            n = jnp.linalg.norm(t, axis=-1, keepdims=True)
            return jnp.tanh(n) * (t / jnp.maximum(n, EPS))

        def split_heads(x, h):
            b, n, hd = x.shape
            return x.reshape(b, n, h, hd // h).transpose(0, 2, 1, 3)
        q = split_heads(tokens @ Wq, HEADS)
        kv = split_heads(tokens @ Wkv, HEADS)
        k, v = (kv[..., :DK], kv[..., DK:])
        q, k, v = (l2norm(q), l2norm(k), l2norm(v))
        sim = jnp.einsum('bhid,bhjd->bhij', q, k)
        attn = jnp.square(jax.nn.relu(sim))
        out = jnp.einsum('bhij,bhjd->bhid', attn, v)
        out = tanh_norm(out)
        b, h, n, d = out.shape
        out = out.transpose(0, 2, 1, 3).reshape(b, n, h * d)
        return out @ Wout

    def _L0_ffn_ref(x, w_gate, w_up, w_down):
        import jax, jax.numpy as jnp
        import numpy as np
        DIM = 128
        HIDDEN = 384
        SCALE = 1.0 / 127.0

        def _dequant(w_int, dtype):
            return w_int.astype(dtype) * jnp.asarray(SCALE, dtype)
        wg = _dequant(w_gate, x.dtype)
        wu = _dequant(w_up, x.dtype)
        wd = _dequant(w_down, x.dtype)
        gate = jnp.einsum('bsd,hd->bsh', x, wg)
        up = jnp.einsum('bsd,hd->bsh', x, wu)
        h = jax.nn.silu(gate) * up
        return jnp.einsum('bsh,dh->bsd', h, wd)

    def _L1_attn_ref(x, W, U, time_mix_k, time_mix_v, time_mix_r, Wk, Wv, Wr, Wo):
        import jax, jax.numpy as jnp
        import numpy as np
        import math
        D_MODEL = 128
        LAYER_ID = 6
        NUM_LAYERS = 12
        B, T = (8, 256)
        MIN_P = -1e+38

        def _init_params():
            C = D_MODEL
            r01 = LAYER_ID / (NUM_LAYERS - 1)
            r1a0 = 1.0 - LAYER_ID / NUM_LAYERS
            h = np.arange(C, dtype=np.float32)
            decay_speed = -5.0 + 8.0 * (h / (C - 1)) ** (0.7 + 1.3 * r01)
            zigzag = ((np.arange(C) + 1) % 3 - 1).astype(np.float32) * 0.5
            U = np.float32(math.log(0.3)) + zigzag
            xx = (np.arange(C, dtype=np.float32) / C).reshape(1, 1, C)
            tmk = xx ** r1a0
            tmv = xx ** r1a0 + 0.3 * r01
            tmr = xx ** (0.5 * r1a0)
            return (jnp.asarray(decay_speed), jnp.asarray(U), jnp.asarray(tmk, jnp.float32), jnp.asarray(tmv, jnp.float32), jnp.asarray(tmr, jnp.float32))

        def _wkv(W, U, k, v):
            w = -jnp.exp(W)
            Bb, Tt, Cc = k.shape
            aa0 = jnp.zeros((Bb, Cc), k.dtype)
            bb0 = jnp.zeros((Bb, Cc), k.dtype)
            pp0 = jnp.full((Bb, Cc), MIN_P, k.dtype)

            def step(carry, kv_t):
                aa, bb, pp = carry
                kt, vt = kv_t
                ww = U + kt
                p = jnp.maximum(pp, ww)
                e1 = jnp.exp(pp - p)
                e2 = jnp.exp(ww - p)
                y = (e1 * aa + e2 * vt) / (e1 * bb + e2)
                ww2 = pp + w
                p2 = jnp.maximum(ww2, kt)
                e1b = jnp.exp(ww2 - p2)
                e2b = jnp.exp(kt - p2)
                return ((e1b * aa + e2b * vt, e1b * bb + e2b, p2), y)
            kT = jnp.swapaxes(k, 0, 1)
            vT = jnp.swapaxes(v, 0, 1)
            _, yT = jax.lax.scan(step, (aa0, bb0, pp0), (kT, vT))
            return jnp.swapaxes(yT, 0, 1)

        def _reference_tuple_inner(x, W, U, time_mix_k, time_mix_v, time_mix_r, Wk, Wv, Wr, Wo):
            xs = jnp.pad(x, ((0, 0), (1, 0), (0, 0)))[:, :-1]
            xk = x * time_mix_k + xs * (1.0 - time_mix_k)
            xv = x * time_mix_v + xs * (1.0 - time_mix_v)
            xr = x * time_mix_r + xs * (1.0 - time_mix_r)
            K = jnp.einsum('btc,dc->btd', xk, Wk)
            V = jnp.einsum('btc,dc->btd', xv, Wv)
            R = jnp.einsum('btc,dc->btd', xr, Wr)
            wkv = _wkv(W, U, K, V)
            hidden = jax.lax.stop_gradient(wkv[:, -1, :])
            rwkv = jax.nn.sigmoid(R) * wkv
            output = jnp.einsum('btc,dc->btd', rwkv, Wo)
            return (output, hidden)
        return _reference_tuple_inner(x, W, U, time_mix_k, time_mix_v, time_mix_r, Wk, Wv, Wr, Wo)[0]

    def _L1_ffn_ref(x, router_w, router_b, w1, b1, w2, b2):
        import math
        import jax, jax.numpy as jnp
        import numpy as np
        D_MODEL = 128
        D_HIDDEN = 512
        N_EXPERTS = 8
        TOP_K = 2
        CAPACITY_FACTOR = 1.25
        B, T, D = x.shape
        N = B * T
        E = N_EXPERTS
        capacity = max(1, math.ceil(N / E * CAPACITY_FACTOR))
        x_flat = x.reshape(N, D)
        logits = x_flat.astype(jnp.float32) @ router_w + router_b
        gates = jax.nn.softmax(logits, axis=-1)
        _, topk_idx = jax.lax.top_k(gates, TOP_K)
        expert_mask = jax.nn.one_hot(topk_idx, E, dtype=jnp.int32).sum(1)
        pos = jnp.cumsum(expert_mask, axis=0) - 1
        expert_mask = expert_mask * (pos < capacity)
        valid = expert_mask > 0
        pos_c = jnp.where(valid, pos, capacity)
        e_idx = jnp.broadcast_to(jnp.arange(E), (N, E))
        dispatched = x_flat[:, None, :] * valid[:, :, None].astype(x.dtype)
        buf = jnp.zeros((E, capacity + 1, D), x.dtype).at[e_idx.ravel(), pos_c.ravel()].add(dispatched.reshape(N * E, D))
        buf = buf[:, :capacity]
        h = jax.nn.gelu(jnp.einsum('ecd,edh->ech', buf, w1) + b1[:, None, :], approximate=False)
        out = jnp.einsum('ech,ehd->ecd', h, w2) + b2[:, None, :]
        pos_g = jnp.minimum(pos_c, capacity - 1)
        gathered = out[e_idx, pos_g]
        weights = (gates * valid).astype(x.dtype)
        y = jnp.einsum('ned,ne->nd', gathered, weights)
        return y.reshape(B, T, D)
    x = L0_attn_tokens
    x = x + _L0_attn_ref(_layernorm(x, axis=-1), L0_attn_Wq, L0_attn_Wkv, L0_attn_Wout)
    x = x + _L0_ffn_ref(_layernorm(x, axis=-1), L0_ffn_w_gate, L0_ffn_w_up, L0_ffn_w_down)
    x = x + _L1_attn_ref(_layernorm(x, axis=-1), L1_attn_W, L1_attn_U, L1_attn_time_mix_k, L1_attn_time_mix_v, L1_attn_time_mix_r, L1_attn_Wk, L1_attn_Wv, L1_attn_Wr, L1_attn_Wo)
    x = x + _L1_ffn_ref(_layernorm(x, axis=-1), L1_ffn_router_w, L1_ffn_router_b, L1_ffn_w1, L1_ffn_b1, L1_ffn_w2, L1_ffn_b2)
    return x

_drawn_inputs = setup_inputs


def setup_inputs(seed=0):
    import zlib

    import numpy as np

    out = dict(_drawn_inputs(seed))
    spreads = {'L1_ffn_router_b': (0.0, 2.0), 'L1_ffn_b1': (0.0, 2.0), 'L1_ffn_b2': (0.0, 2.0)}
    factors = {'L1_attn_W': 8.0,
     'L1_attn_U': 8.0,
     'L1_attn_time_mix_k': 8.0,
     'L1_attn_time_mix_v': 8.0,
     'L1_attn_time_mix_r': 8.0,
     'L1_attn_Wk': 8.0,
     'L1_attn_Wv': 8.0,
     'L1_attn_Wr': 8.0,
     'L1_attn_Wo': 8.0,
     'L1_ffn_router_w': 64.0,
     'L1_ffn_w1': 64.0,
     'L1_ffn_w2': 64.0}
    for name, (base, spread) in spreads.items():
        noise = np.random.default_rng([zlib.crc32(name.encode()), seed]).standard_normal(out[name].shape)
        drawn = base * np.exp(spread * noise) if base else spread * noise
        out[name] = jnp.asarray(drawn.astype(out[name].dtype))
    for name, factor in factors.items():
        out[name] = (out[name] * factor).astype(out[name].dtype)
    return out
```

```python
from contextlib import ExitStack

import concourse.bass as bass
from concourse import mybir

F32 = mybir.dt.float32
BF16 = mybir.dt.bfloat16
I32 = mybir.dt.int32
U32 = mybir.dt.uint32
ALU = mybir.AluOpType
ACT = mybir.ActivationFunctionType
AX = mybir.AxisListType

P = 128
BATCH, T = 8, 256
TOKENS = BATCH * T
TILES = TOKENS // P
TPB = T // P
LN_EPS = 1e-5

HEADS, DK, DV = 16, 16, 64
PAIRS = HEADS // 2
NORM_FLOOR = 1e-24
RSQRT_MAGIC = float(0x5F3759DF)

Q_PART = (0, 0, 1, 1, 0, 2)
K_PART = (0, 1, 0, 1, 2, 0)
COMBOS = len(Q_PART)


class At:

    def __init__(self, i, c):
        self.i, self.c, self.par = i, c, c % 2

    def __add__(self, n):
        return At(self.i, self.c + n)

    def count(self, per, k=0):
        return self.i * (2 * per) + (self.c * per + k)

    def half(self, per, k=0):
        return self.i * per + (self.c // 2 * per + k)


class Chain:

    def __init__(self, eng, sem, base=0):
        self.eng, self.sem, self.base, self.n = eng, sem, base, 0

    def done(self, ins):
        ins.then_inc(self.sem, 1)
        self.n += 1
        return self

    def wait(self):
        self.eng.wait_ge(self.sem, self.base + self.n)

    def __call__(self, ins):
        self.done(ins)
        self.wait()


def rsqrt(nc, link, y, x, a, yi, xi):
    v = nc.vector
    link(v.tensor_scalar(yi, xi, 1, None, ALU.arith_shift_right))
    link(v.tensor_scalar(yi, yi, -1.0, RSQRT_MAGIC, ALU.mult, ALU.add))
    for _ in range(3):
        link(v.scalar_tensor_tensor(a, y, -0.5, y, ALU.mult, ALU.mult))
        link(v.tensor_tensor(a, a, x, ALU.mult))
        link(v.scalar_tensor_tensor(y, a, 1.5, y, ALU.add, ALU.mult))


def attention_phase(nc, x_in, Wq, Wkv, Wout, ident_in, pair_ones_in, sel_in, parts, x_res, sem_of, load_x=True):
    with ExitStack() as ctx:
        def sb(name, shape, dt=F32):
            return ctx.enter_context(nc.sbuf_tensor("at_" + name, shape, dt))

        def bank(name):
            return ctx.enter_context(nc.psum_tensor("at_" + name, [P, 512], F32))

        sem = sem_of("at")
        QK, V = 2 * HEADS * DK, HEADS * DV
        w_qk = sb("w_qk", [P, QK])
        w_v = sb("w_v", [P, V])
        w_out = sb("w_out", [P, PAIRS, P])
        ident = sb("ident", [P, P])
        pair_ones = sb("pair_ones", [P, 2])
        sel_f32 = sb("sel_f32", [3 * HEADS, PAIRS, P])
        sel = sb("sel", [3 * HEADS, PAIRS, P], BF16)
        ident16 = sb("ident16", [P, P], BF16)
        f_parts = sb("f_parts", [P, TPB, P], BF16)
        f_rest = sb("f_rest", [P, TPB, HEADS])
        fT = sb("fT", [3 * HEADS, T], BF16)
        stats = sb("stats", [P, TILES, 6])
        mv = sb("mv", [P, TILES, 2])
        rstd = sb("rstd", [P, TILES])
        ln_var = sb("ln_var", [P, TILES])
        xn = [sb(f"xn{i}", [P, TPB, P]) for i in range(2)]
        xnT = sb("xnT", [P, T])
        qk_raw = [sb(f"qk_raw{i}", [P, TPB, QK]) for i in range(2)]
        v_raw = [sb(f"v_raw{i}", [P, TPB, V]) for i in range(2)]
        sq = sb("sq", [P, TPB, QK + V])
        small = {n: sb("nr_" + n, [P, 64]) for n in ("x", "y", "a", "n2", "n", "th", "f")}
        part = [[sb(f"part{i}{j}", [P, 4, T], BF16) for j in range(3)] for i in range(2)]
        rest = sb("rest", [P, 4, T])
        q_stack = [sb(f"q_stack{i}", [COMBOS * DK, HEADS, T], BF16) for i in range(2)]
        k_stack = [sb(f"k_stack{i}", [COMBOS * DK, HEADS, T], BF16) for i in range(2)]
        attn = [sb(f"attn{i}", [P, TPB, T]) for i in range(4)]
        ob = [sb(f"ob{i}", [P, PAIRS, T]) for i in range(2)]
        rv = sb("rv", [P, 32])
        inv_n = sb("inv_n", [P, 32])
        osq = sb("osq", [P, PAIRS, T])

        sim = [bank(f"sim{i}") for i in range(4)]
        av = [bank(f"av{i}") for i in range(2)]
        misc = [bank(f"misc{i}") for i in range(2)]

        x_loaded = [sem(f"x_loaded{i}") for i in range(4)]
        w_loaded = sem("w_loaded")
        xn_ready = sem("xn_ready")
        tx_done, xT_ready = sem("tx_done"), sem("xT_ready")
        proj_done, qkv_ready = sem("proj_done"), sem("qkv_ready")
        sq_qk_ready, sq_v_ready = sem("sq_qk_ready"), sem("sq_v_ready")
        qkn_ready, rv_ready, vn_ready = sem("qkn_ready"), sem("rv_ready"), sem("vn_ready")
        tqk_done = sem("tqk_done")
        p1_ready, rest_ready, p2_ready, p3_ready = sem("p1_ready"), sem("rest_ready"), sem("p2_ready"), sem("p3_ready")
        parts_out = [sem(f"parts_out{i}") for i in range(2)]
        stack_ready = [sem(f"stack_ready{i}") for i in range(2)]
        sim_done, av_done = sem("sim_done"), sem("av_done")
        relu_even, relu_odd = sem("relu_even"), sem("relu_odd")
        attn_even, attn_odd = sem("attn_even"), sem("attn_odd")
        ob_ready, osq_ready = sem("ob_ready"), sem("osq_ready")
        n2_done, n2_read, n_ready, tanh_ready, f_ready = (
            sem("n2_done"), sem("n2_read"), sem("n_ready"), sem("tanh_ready"), sem("f_ready"))
        consts_ready, fT_done, fT_ready = sem("consts_ready"), sem("fT_done"), sem("fT_ready")
        bc_done, on_ready = sem("bc_done"), sem("on_ready")
        out_done, x1_ready = sem("out_done"), sem("x1_ready")
        chain_sems = [sem(f"dve_chain{i}") for i in range(5)]

        block = ctx.enter_context(nc.Block())
        x_tiles = x_in.rearrange("b t d -> (b t) d").rearrange("(a p) d -> p a d", p=P)
        xr = x_res[:, :].rearrange("p (a d) -> p a d", a=TILES)
        kv_view = Wkv.rearrange("p (h e) -> p h e", h=HEADS)
        Q4 = TILES // 4

        @block.sync
        def _(sp):
            if load_x:
                for n in range(4):
                    sp.dma_start(xr[:, n * Q4:(n + 1) * Q4, :], x_tiles[:, n * Q4:(n + 1) * Q4, :]).then_inc(x_loaded[n], 16)

            def stack(b):
                for j, ready in enumerate((p1_ready, p2_ready, p3_ready)):
                    sp.wait_ge(ready, b.count(2, 2))
                    sp.dma_start(parts[b.par, j].rearrange("(a p) t -> p a t", p=P),
                                 part[b.par][j][:, :, :]).then_inc(parts_out[b.par], 16)
                sp.wait_ge(parts_out[b.par], b.half(48, 48))
                for c in range(COMBOS):
                    for s, tile, j in ((0, q_stack, Q_PART[c]), (1, k_stack, K_PART[c])):
                        src = parts[b.par, j, s * 256:(s + 1) * 256, :].rearrange("(h d) t -> d h t", d=DK)
                        sp.dma_start(tile[b.par][c * DK:(c + 1) * DK, :, :], src).then_inc(stack_ready[b.par], 16)

            stack(At(0, 0))
            stack(At(0, 1))
            with sp.Fori(0, 3) as i:
                for c in (1, 2):
                    stack(At(i, c) + 1)

        @block.tensor
        def _(pe):
            mm = nc.tensor.matmul

            def transpose_x(b):
                pe.wait_ge(xn_ready, b.count(1, 1))
                for t in range(TPB):
                    last = nc.tensor.transpose(misc[0][:, t * P:(t + 1) * P], xn[b.par][:, t, :], ident[:, :])
                last.then_inc(tx_done, 1)

            def project(b, j, after=None):
                if j == 0:
                    pe.wait_ge(xT_ready, b.count(1, 1))
                elif j >= 2:
                    pe.wait_ge(qkv_ready, b.count(6, j - 1))
                t = j if j < 2 else (j - 2) // 2
                w = w_qk[:, :] if j < 2 else w_v[:, (j % 2) * 512:(j % 2 + 1) * 512]
                mm(misc[j % 2][:, :], xnT[:, t * P:(t + 1) * P], w, start=True, stop=True).then_inc(proj_done, 1)

            def transpose_qk(b, factors_before=False):
                pe.wait_ge(qkn_ready, b.count(1, 1))
                for s in range(2):
                    pe.wait_ge(qkv_ready, b.count(6, 5 + s))
                    if s and factors_before:
                        pe.wait_ge(fT_ready, b.count(1, -1))
                    for g in range(2):
                        for t in range(TPB):
                            last = nc.tensor.transpose(
                                misc[s][:, g * T + t * P:g * T + (t + 1) * P],
                                qk_raw[b.par][:, t, s * 256 + g * P:s * 256 + (g + 1) * P], ident[:, :])
                    last.then_inc(tqk_done, 1)

            def scores(b, s, first):
                if s == 0:
                    pe.wait_ge(stack_ready[b.par], b.half(192, 192))
                for h in (2 * s, 2 * s + 1):
                    if not (first and h < 4):
                        pe.wait_ge(relu_odd if h % 2 else relu_even, b.count(8, s - 1))
                    for j in range(TPB):
                        last = mm(sim[h % 4][:, j * T:(j + 1) * T], k_stack[b.par][:, h, j * P:(j + 1) * P],
                                  q_stack[b.par][:, h, :], start=True, stop=True)
                    last.then_inc(sim_done, 1)

            def values(b, s, first):
                pe.wait_ge(vn_ready, b.count(4, s // 2 + 1))
                pe.wait_ge(attn_even, b.count(8, s + 1))
                pe.wait_ge(attn_odd, b.count(8, s + 1))
                if not (first and s < 2):
                    pe.wait_ge(ob_ready, b.count(8, s - 1))
                for j in range(TPB):
                    for e in range(2):
                        h = 2 * s + e
                        last = mm(av[s % 2][e * DV:(e + 1) * DV, 0:T], v_raw[b.par][:, j, h * DV:(h + 1) * DV],
                                  attn[h % 4][:, j, :], start=j == 0, stop=j == TPB - 1)
                last.then_inc(av_done, 1)

            def norms(b):
                pe.wait_ge(osq_ready, b.count(8, 8))
                pe.wait_ge(x1_ready, b.count(2))
                for s in range(PAIRS):
                    for t in range(TPB):
                        last = mm(misc[1][:, t * HEADS + 2 * s:t * HEADS + 2 * s + 2],
                                  osq[:, s, t * P:(t + 1) * P], pair_ones[:, :], start=True, stop=True)
                last.then_inc(n2_done, 1)

            def transpose_factors(b, tail):
                pe.wait_ge(f_ready, b.count(1, 1))
                if tail:
                    pe.wait_ge(n2_read, b.count(1, 1))
                else:
                    pe.wait_ge(qkv_ready, (b + 2).count(6, 6))
                for t in range(TPB):
                    last = nc.tensor.transpose(
                        misc[1][:, :].bitcast(BF16)[:, t * P:(t + 1) * P],
                        f_parts[:, t, :], ident16[:, :])
                last.then_inc(fT_done, 1)

            def spread(b, j, tail):
                if j == 0:
                    pe.wait_ge(fT_ready, b.count(1, 1))
                if j >= 2:
                    pe.wait_ge(on_ready, b.count(4, j - 1))
                elif tail:
                    pe.wait_ge(x1_ready, b.count(2))
                else:
                    pe.wait_ge(rest_ready, (b + 2).count(2, j + 1))
                for e in range(2):
                    last = mm(misc[j % 2][:, e * T:(e + 1) * T], sel[:, 2 * j + e, :], fT[:, :],
                              start=True, stop=True)
                last.then_inc(bc_done, 1)

            def output(b):
                for t in range(TPB):
                    pe.wait_ge(on_ready, b.count(4, 4))
                    for s in range(PAIRS):
                        last = mm(misc[t][:, 0:P], ob[b.par][:, s, t * P:(t + 1) * P], w_out[:, s, :],
                                  start=s == 0, stop=s == PAIRS - 1)
                    last.then_inc(out_done, 1)

            def body(b, first=False, last=False):
                for s in range(PAIRS):
                    if s < PAIRS - 1:
                        scores(b, s + 1, first)
                    values(b, s, first)
                    if not last:
                        if s == 0:
                            if not first:
                                pe.wait_ge(x1_ready, b.count(2, -2))
                            transpose_x(b + 1)
                        if s == 1:
                            if not first:
                                norms(b + -1)
                            project(b + 1, 0)
                            if not first:
                                pe.wait_ge(n2_read, b.count(1))
                            project(b + 1, 1)
                        if s in (2, 3):
                            project(b + 1, 2 * s - 2)
                            project(b + 1, 2 * s - 1)
                        if s == 4:
                            if not first:
                                transpose_factors(b + -1, False)
                            transpose_qk(b + 1, not first)
                    elif s == 1:
                        norms(b + -1)
                    if not first:
                        if last and s == 4:
                            transpose_factors(b + -1, True)
                        if s == 4:
                            spread(b + -1, 0, last)
                        if s == 5:
                            spread(b + -1, 1, last)
                            spread(b + -1, 2, last)
                        if s == 6:
                            spread(b + -1, 3, last)
                        if s == 7:
                            output(b + -1)
                if not last:
                    scores(b + 1, 0, False)

            pe.wait_ge(w_loaded, 16 * 7)
            pe.wait_ge(consts_ready, 3)
            b0 = At(0, 0)
            transpose_x(b0)
            for j in range(6):
                project(b0, j)
            transpose_qk(b0)
            scores(b0, 0, True)
            body(b0, first=True)
            body(At(0, 1))
            with pe.Fori(0, 2) as i:
                for c in (2, 3):
                    body(At(i, c))
            body(At(0, 6))
            body(At(0, 7), last=True)
            b7 = At(0, 7)
            norms(b7)
            transpose_factors(b7, True)
            for j in range(4):
                spread(b7, j, True)
            output(b7)

        @block.scalar
        def _(act):
            def w_load(dst, src):
                act.dma_start(dst, src).then_inc(w_loaded, 16)

            w_load(ident[:, :], ident_in)
            w_load(w_qk[:, 0:256], Wq)
            w_load(w_qk[:, 256:512].rearrange("p (h d) -> p h d", h=HEADS), kv_view[:, :, 0:DK])
            w_load(w_v[:, :].rearrange("p (h d) -> p h d", h=HEADS), kv_view[:, :, DK:DK + DV])
            w_load(w_out[:, :, :], Wout.rearrange("(s p) n -> p s n", p=P))
            w_load(pair_ones[:, :], pair_ones_in)
            w_load(sel_f32[:, :, :], sel_in)

            def copy_xT(b):
                act.wait_ge(tx_done, b.count(1, 1))
                nc.scalar.copy(xnT[:, :], misc[0][:, 0:T]).then_inc(xT_ready, 1)

            def copy_qkv(b, j):
                act.wait_ge(proj_done, b.count(6, j + 1))
                t = j if j < 2 else (j - 2) // 2
                dst = qk_raw[b.par][:, t, :] if j < 2 else v_raw[b.par][:, t, (j % 2) * 512:(j % 2 + 1) * 512]
                nc.scalar.copy(dst, misc[j % 2][:, :]).then_inc(qkv_ready, 1)

            def part1(b):
                for s in range(2):
                    act.wait_ge(tqk_done, b.count(2, s + 1))
                    nc.scalar.copy(part[b.par][0][:, 2 * s:2 * s + 2, :],
                                   misc[s][:, :].rearrange("p (g t) -> p g t", g=2)).then_inc(p1_ready, 1)

            def part2(b):
                for s in range(2):
                    act.wait_ge(rest_ready, b.count(2, s + 1))
                    nc.scalar.copy(part[b.par][1][:, 2 * s:2 * s + 2, :], rest[:, 2 * s:2 * s + 2, :]).then_inc(p2_ready, 1)

            def copy_ob(b, s):
                act.wait_ge(av_done, b.count(8, s + 1))
                nc.scalar.copy(ob[b.par][:, s, :], av[s % 2][:, 0:T]).then_inc(ob_ready, 1)

            def tanh(b):
                act.wait_ge(n_ready, b.count(1, 1))
                nc.scalar.activation(small["th"][:, 0:32], small["n"][:, 0:32], ACT.Tanh).then_inc(tanh_ready, 1)

            def copy_fT(b):
                act.wait_ge(fT_done, b.count(1, 1))
                nc.scalar.copy(fT[:, :], misc[1][0:3 * HEADS, :].bitcast(BF16)[:, 0:T]).then_inc(fT_ready, 1)

            def body(b, first=False, last=False):
                for s in range(PAIRS):
                    act.wait_ge(sim_done, b.count(16, 2 * s + 1))
                    if not (first and s < 2):
                        act.wait_ge(av_done, b.count(8, s - 1))
                    a = attn[2 * s % 4][:, :, :].rearrange("p j t -> p (j t)")
                    nc.scalar.activation(a, sim[2 * s % 4][:, :], ACT.Relu).then_inc(relu_even, 1)
                    act.wait_ge(relu_odd, b.count(8, s + 1))
                    a = attn[(2 * s + 1) % 4][:, :, :]
                    nc.scalar.activation(a, a, ACT.Square).then_inc(attn_odd, 1)
                    if s == 1 and not first:
                        act.wait_ge(x1_ready, b.count(2, -2))
                    if s:
                        copy_ob(b, s - 1)
                    if s == 4 and not first:
                        copy_fT(b + -1)
                    if not last:
                        if s == 0:
                            copy_xT(b + 1)
                        if s in (1, 2, 3):
                            copy_qkv(b + 1, 2 * s - 2)
                            copy_qkv(b + 1, 2 * s - 1)
                        if s == 4:
                            part1(b + 1)
                        if s == 5:
                            part2(b + 1)
                    if s == 1 and not first:
                        tanh(b + -1)
                copy_ob(b, PAIRS - 1)

            b0 = At(0, 0)
            copy_xT(b0)
            for j in range(6):
                copy_qkv(b0, j)
            part1(b0)
            part2(b0)
            body(b0, first=True)
            body(At(0, 1))
            with act.Fori(0, 2) as i:
                for c in (2, 3):
                    body(At(i, c))
            body(At(0, 6))
            body(At(0, 7), last=True)
            tanh(At(0, 7))
            copy_fT(At(0, 7))

        @block.vector
        def _(dve):
            v = nc.vector

            def normalize_x(b):
                for t in range(TPB):
                    at = b.count(TPB, t)
                    last = v.tensor_scalar(xn[b.par][:, t, :], x_res[:, bass.ds(at * P, P)],
                                           mv[:, :, :].rearrange("p a c -> p (a c)")[:, bass.ds(at * 2, 1)],
                                           rstd[:, bass.ds(at, 1)], ALU.subtract, ALU.mult)
                last.then_inc(xn_ready, 1)

            def sized(n):
                return {k: t[:, 0:n] for k, t in small.items()}

            def newton(link, n):
                s = sized(n)
                rsqrt(nc, link, s["y"], s["x"], s["a"], s["y"].bitcast(I32), s["x"].bitcast(I32))

            def normalize_qk(b, link):
                dve.wait_ge(sq_qk_ready, b.count(2, 2))
                n = TPB * 2 * HEADS
                for t in range(TPB):
                    last = v.reduce_sum(small["x"][:, t * 32:(t + 1) * 32],
                                        sq[:, t, 0:QK].rearrange("p (h d) -> p h d", d=DK), AX.X)
                    link.done(last)
                link.wait()
                link(v.tensor_scalar(small["x"][:, 0:n], small["x"][:, 0:n], NORM_FLOOR, None, ALU.max))
                newton(link, n)
                for t in range(TPB):
                    q = qk_raw[b.par][:, t, :].rearrange("p (h d) -> p h d", d=DK)
                    y = small["y"][:, t * 32:(t + 1) * 32].unsqueeze(2).to_broadcast([P, 2 * HEADS, DK])
                    last = v.tensor_tensor(q, q, y, ALU.mult)
                last.then_inc(qkn_ready, 1)

            def norms_v(b, link):
                dve.wait_ge(sq_v_ready, b.count(2, 2))
                n = TPB * HEADS
                for t in range(TPB):
                    last = v.reduce_sum(small["x"][:, t * HEADS:(t + 1) * HEADS],
                                        sq[:, t, QK:QK + V].rearrange("p (h d) -> p h d", d=DV), AX.X)
                    link.done(last)
                link.wait()
                link(v.tensor_scalar(small["x"][:, 0:n], small["x"][:, 0:n], NORM_FLOOR, None, ALU.max))
                newton(link, n)
                dve.wait_ge(vn_ready, b.count(4))
                v.tensor_copy(rv[:, :], small["y"][:, 0:n]).then_inc(rv_ready, 1)

            def factors(b, link):
                dve.wait_ge(n2_done, b.count(1, 1))
                s = sized(32)
                v.tensor_copy(s["n2"], misc[1][:, 0:32]).then_inc(n2_read, 1)
                dve.wait_ge(n2_read, b.count(1, 1))
                link(v.tensor_scalar(s["x"], s["n2"], NORM_FLOOR, None, ALU.max))
                newton(link, 32)
                v.tensor_tensor(s["n"], s["n2"], s["y"], ALU.mult).then_inc(n_ready, 1)
                link(v.tensor_copy(inv_n[:, :], s["y"]))

            def f_part(c):
                return f_parts[:, :, c * HEADS:(c + 1) * HEADS]

            def tanh_factor(b, link):
                dve.wait_ge(tanh_ready, b.count(1, 1))
                f = small["f"][:, 0:32]
                f3 = f.rearrange("p (t h) -> p t h", t=TPB)
                link(v.tensor_tensor(f, small["th"][:, 0:32], inv_n[:, :], ALU.mult))
                link(v.tensor_copy(f_part(0), f3))
                link(v.tensor_tensor(f_rest[:, :, :], f3, f_part(0), ALU.subtract))
                link(v.tensor_copy(f_part(1), f_rest[:, :, :]))
                v.tensor_tensor(f_part(2), f_rest[:, :, :], f_part(1),
                                ALU.subtract).then_inc(f_ready, 1)

            def split_rest(b):
                for s in range(2):
                    dve.wait_ge(p1_ready, b.count(2, s + 1))
                    v.tensor_tensor(rest[:, 2 * s:2 * s + 2, :], misc[s][:, :].rearrange("p (g t) -> p g t", g=2),
                                    part[b.par][0][:, 2 * s:2 * s + 2, :], ALU.subtract).then_inc(rest_ready, 1)

            def part3(b):
                for s in range(2):
                    dve.wait_ge(p2_ready, b.count(2, s + 1))
                    v.tensor_tensor(part[b.par][2][:, 2 * s:2 * s + 2, :], rest[:, 2 * s:2 * s + 2, :],
                                    part[b.par][1][:, 2 * s:2 * s + 2, :], ALU.subtract).then_inc(p3_ready, 1)

            def scale_ob(b, j):
                dve.wait_ge(bc_done, b.count(4, j + 1))
                o = ob[b.par][:, 2 * j:2 * j + 2, :]
                v.tensor_tensor(o, o, misc[j % 2][:, :].rearrange("p (g t) -> p g t", g=2),
                                ALU.mult).then_inc(on_ready, 1)

            def residual(b):
                for t in range(TPB):
                    dve.wait_ge(out_done, b.count(2, t + 1))
                    x = x_res[:, bass.ds(b.count(TPB, t) * P, P)]
                    v.tensor_tensor(x, x, misc[t][:, 0:P], ALU.add).then_inc(x1_ready, 1)

            def body(b, link, first=False, last=False):
                if not last:
                    normalize_x(b + 1)
                for s in range(PAIRS):
                    dve.wait_ge(sim_done, b.count(16, 2 * s + 2))
                    if not (first and s < 2):
                        dve.wait_ge(av_done, b.count(8, s - 1))
                    a = attn[(2 * s + 1) % 4][:, :, :].rearrange("p j t -> p (j t)")
                    v.tensor_scalar(a, sim[(2 * s + 1) % 4][:, :], 0.0, None, ALU.max).then_inc(relu_odd, 1)
                    dve.wait_ge(relu_even, b.count(8, s + 1))
                    a = attn[2 * s % 4][:, :, :]
                    v.tensor_tensor(a, a, a, ALU.mult).then_inc(attn_even, 1)
                    if not first:
                        if s == 1:
                            factors(b + -1, link)
                        if s == 2:
                            tanh_factor(b + -1, link)
                    if not last:
                        if s == 3:
                            normalize_qk(b + 1, link)
                        if s == 4:
                            split_rest(b + 1)
                        if s == 5:
                            part3(b + 1)
                        if s == 6:
                            norms_v(b + 1, link)
                    if not first:
                        if s == 4:
                            scale_ob(b + -1, 0)
                        if s == 5:
                            scale_ob(b + -1, 1)
                            scale_ob(b + -1, 2)
                        if s == 6:
                            scale_ob(b + -1, 3)
                        if s == 7:
                            residual(b + -1)

            link = Chain(dve, chain_sems[0])
            for a in range(TILES):
                if load_x and a % Q4 == 0:
                    dve.wait_ge(x_loaded[a // Q4], 16)
                link.done(v.bn_stats(stats[:, a, :], xr[:, a, :]))
            link.wait()
            for a in range(TILES):
                link.done(v.bn_aggr(mv[:, a, :], stats[:, a, :]))
            link.wait()
            link(v.tensor_scalar(ln_var[:, :], mv[:, :, 1], LN_EPS, None, ALU.add))
            rsqrt(nc, link, rstd[:, :], ln_var[:, :], small["a"][:, 0:TILES], rstd[:, :].bitcast(I32), ln_var[:, :].bitcast(I32))
            dve.wait_ge(consts_ready, 1)
            b0 = At(0, 0)
            normalize_x(b0)
            normalize_qk(b0, link)
            split_rest(b0)
            part3(b0)
            norms_v(b0, link)
            body(b0, Chain(dve, chain_sems[1]), first=True)
            body(At(0, 1), Chain(dve, chain_sems[2]))
            per = CHAIN_PER_BODY
            with dve.Fori(0, 2) as i:
                for c in (2, 3):
                    link = Chain(dve, chain_sems[3], i * (2 * per) + (c - 2) * per)
                    body(At(i, c), link)
                    assert link.n == per, link.n
            link = Chain(dve, chain_sems[4])
            body(At(0, 6), link)
            body(At(0, 7), link, last=True)
            b7 = At(0, 7)
            factors(b7, link)
            tanh_factor(b7, link)
            for j in range(4):
                scale_ob(b7, j)
            residual(b7)

        @block.gpsimd
        def _(pool):
            g = nc.gpsimd
            pool.wait_ge(w_loaded, 16 * 7)
            g.memset(f_parts[:, :, :], 0.0).then_inc(consts_ready, 1)
            g.tensor_copy(ident16[:, :], ident[:, :]).then_inc(consts_ready, 1)
            g.tensor_copy(sel[:, :, :], sel_f32[:, :, :]).then_inc(consts_ready, 1)

            def square_qk(b):
                for t in range(TPB):
                    pool.wait_ge(qkv_ready, b.count(6, t + 1))
                    q = qk_raw[b.par][:, t, :]
                    g.tensor_tensor(sq[:, t, 0:QK], q, q, ALU.mult).then_inc(sq_qk_ready, 1)

            def square_v(b, t):
                pool.wait_ge(qkv_ready, b.count(6, 2 * t + 4))
                x = v_raw[b.par][:, t, :]
                g.tensor_tensor(sq[:, t, QK:QK + V], x, x, ALU.mult).then_inc(sq_v_ready, 1)

            def scale_v(b, n):
                pool.wait_ge(rv_ready, b.count(1, 1))
                for t in range(TPB):
                    x = v_raw[b.par][:, t, n * 256:(n + 1) * 256].rearrange("p (h d) -> p h d", d=DV)
                    r = rv[:, t * HEADS + 4 * n:t * HEADS + 4 * n + 4].unsqueeze(2).to_broadcast([P, 4, DV])
                    last = g.tensor_tensor(x, x, r, ALU.mult)
                last.then_inc(vn_ready, 1)

            def square_ob(b, s):
                pool.wait_ge(ob_ready, b.count(8, s + 1))
                o = ob[b.par][:, s, :]
                g.tensor_tensor(osq[:, s, :], o, o, ALU.mult).then_inc(osq_ready, 1)

            def body(b, first=False, last=False):
                for s in range(PAIRS):
                    if s == 0 and not first:
                        square_ob(b + -1, PAIRS - 1)
                    if not last:
                        if s == 1:
                            square_qk(b + 1)
                        if s in (3, 4):
                            square_v(b + 1, s - 3)
                        if s == 7:
                            for n in range(4):
                                scale_v(b + 1, n)
                    if s == 1 and not first:
                        pool.wait_ge(n2_done, b.count(1))
                    if s:
                        square_ob(b, s - 1)

            b0 = At(0, 0)
            square_qk(b0)
            square_v(b0, 0)
            square_v(b0, 1)
            for n in range(4):
                scale_v(b0, n)
            body(b0, first=True)
            body(At(0, 1))
            with pool.Fori(0, 2) as i:
                for c in (2, 3):
                    body(At(i, c))
            body(At(0, 6))
            body(At(0, 7), last=True)
            square_ob(At(0, 7), PAIRS - 1)


CHAIN_PER_BODY = 4 + 2 + 1 + 11 + 2 + 1 + 11 + 1 + 11 + 1


CHUNKS = 4
TPC = TILES // CHUNKS
CW = TPC * P
HIDDEN = 384
HB = HIDDEN // P
INT_SCALE = 1.0 / 127.0


def layernorm_chunk(nc, dve, link, x_res, at, t, xn, ready):
    v = nc.vector
    for a in range(TPC):
        link.done(v.bn_stats(t["stats"][:, a, :], x_res[:, bass.ds(at + a * P, P)]))
    link.wait()
    for a in range(TPC):
        link.done(v.bn_aggr(t["mv"][:, a, :], t["stats"][:, a, :]))
    link.wait()
    link(v.tensor_scalar(t["var"][:, :], t["mv"][:, :, 1], LN_EPS, None, ALU.add))
    rsqrt(nc, link, t["rstd"][:, :], t["var"][:, :], t["a"][:, :], t["rstd"][:, :].bitcast(I32), t["var"][:, :].bitcast(I32))
    for a in range(TPC):
        last = v.tensor_scalar(xn[:, a, :], x_res[:, bass.ds(at + a * P, P)], t["mv"][:, a, 0:1],
                               t["rstd"][:, a:a + 1], ALU.subtract, ALU.mult)
    last.then_inc(ready, 1)


LN_CHAIN = 2 * TPC + 1 + 11


def ln_tiles(sb):
    return {"stats": sb("ln_stats", [P, TPC, 6]), "mv": sb("ln_mv", [P, TPC, 2]), "var": sb("ln_var2", [P, TPC]),
            "rstd": sb("ln_rstd", [P, TPC]), "a": sb("ln_a", [P, TPC])}


def ffn_phase(nc, w_gate_t, w_up_t, w_down_t, ident_in, x_res, sem_of):
    with ExitStack() as ctx:
        def sb(name, shape, dt=F32):
            return ctx.enter_context(nc.sbuf_tensor("ff_" + name, shape, dt))

        def bank(name):
            return ctx.enter_context(nc.psum_tensor("ff_" + name, [P, 512], F32))

        sem = sem_of("ff")
        w_int = sb("w_int", [P, 3, HIDDEN], I32)
        w_gu = sb("w_gu", [P, 2, HIDDEN])
        w_dn = sb("w_dn", [P, HB, P])
        ident = sb("ident", [P, P])
        ln = ln_tiles(sb)
        xn = [sb(f"xn{i}", [P, TPC, P]) for i in range(2)]
        xnT = [sb(f"xnT{i}", [P, CW]) for i in range(2)]
        silu = [sb(f"silu{i}", [P, CW]) for i in range(2)]
        h = [sb(f"h{i}", [P, HB, CW]) for i in range(2)]
        xt_bank = bank("xt")
        g_bank = [bank(f"g{i}") for i in range(2)]
        u_bank = [bank(f"u{i}") for i in range(2)]
        y_bank = bank("y")
        w_loaded, w_ready = sem("w_loaded"), sem("w_ready")
        xn_ready, tx_done, xT_ready = sem("xn_ready"), sem("tx_done"), sem("xT_ready")
        gate_done, up_done, silu_ready, h_ready = sem("gate_done"), sem("up_done"), sem("silu_ready"), sem("h_ready")
        down_done, x_ready = sem("down_done"), sem("x_ready")
        chain = [sem(f"chain{i}") for i in range(3)]
        block = ctx.enter_context(nc.Block())

        @block.sync
        def _(sp):
            sp.dma_start(w_int[:, 0, :], w_gate_t).then_inc(w_loaded, 16)
            sp.dma_start(w_int[:, 1, :], w_up_t).then_inc(w_loaded, 16)
            sp.dma_start(w_int[:, 2, :].rearrange("p (k d) -> p k d", k=HB),
                         w_down_t.rearrange("(k p) d -> p k d", p=P)).then_inc(w_loaded, 16)
            sp.dma_start(ident[:, :], ident_in).then_inc(w_loaded, 16)

        @block.gpsimd
        def _(pool):
            pool.wait_ge(w_loaded, 64)
            nc.gpsimd.tensor_scalar(w_gu[:, :, :], w_int[:, 0:2, :], INT_SCALE, None, ALU.mult).then_inc(w_ready, 1)
            nc.gpsimd.tensor_scalar(w_dn[:, :, :].rearrange("p k d -> p (k d)"), w_int[:, 2, :], INT_SCALE, None,
                                    ALU.mult).then_inc(w_ready, 1)

        @block.tensor
        def _(pe):
            mm = nc.tensor.matmul

            def transpose_x(c):
                pe.wait_ge(xn_ready, c.count(1, 1))
                pe.wait_ge(xT_ready, c.count(1))
                for a in range(TPC):
                    last = nc.tensor.transpose(xt_bank[:, a * P:(a + 1) * P], xn[c.par][:, a, :], ident[:, :])
                last.then_inc(tx_done, 1)

            def body(c, first=False, last=False):
                pe.wait_ge(xT_ready, c.count(1, 1))
                for k in range(HB):
                    n = (c.par * HB + k) % 2
                    if not (first and k < 2):
                        pe.wait_ge(h_ready, c.count(HB, k - 1))
                    mm(g_bank[n][:, :], w_gu[:, 0, k * P:(k + 1) * P], xnT[c.par][:, :], start=True, stop=True).then_inc(gate_done, 1)
                    mm(u_bank[n][:, :], w_gu[:, 1, k * P:(k + 1) * P], xnT[c.par][:, :], start=True, stop=True).then_inc(up_done, 1)
                    if k == 1 and not last:
                        transpose_x(c + 1)
                pe.wait_ge(x_ready, c.count(1))
                pe.wait_ge(h_ready, c.count(HB, HB))
                for a in range(TPC):
                    for k in range(HB):
                        done = mm(y_bank[:, a * P:(a + 1) * P], h[c.par][:, k, a * P:(a + 1) * P], w_dn[:, k, :],
                                  start=k == 0, stop=k == HB - 1)
                done.then_inc(down_done, 1)

            pe.wait_ge(w_ready, 2)
            transpose_x(At(0, 0))
            body(At(0, 0), first=True)
            for c in (1, 2):
                body(At(0, c))
            body(At(0, 3), last=True)

        @block.scalar
        def _(act):
            def copy_xT(c):
                act.wait_ge(tx_done, c.count(1, 1))
                nc.scalar.copy(xnT[c.par][:, :], xt_bank[:, :]).then_inc(xT_ready, 1)

            def body(c, first=False, last=False):
                for k in range(HB):
                    n = (c.par * HB + k) % 2
                    act.wait_ge(gate_done, c.count(HB, k + 1))
                    if not (first and k < 2):
                        act.wait_ge(h_ready, c.count(HB, k - 1))
                    nc.scalar.activation(silu[n][:, :], g_bank[n][:, :], ACT.Silu).then_inc(silu_ready, 1)
                    if k == 1 and not last:
                        copy_xT(c + 1)

            copy_xT(At(0, 0))
            body(At(0, 0), first=True)
            for c in (1, 2):
                body(At(0, c))
            body(At(0, 3), last=True)

        @block.vector
        def _(dve):
            v = nc.vector

            def body(c, link, first=False, last=False):
                if not last:
                    n = c + 1
                    layernorm_chunk(nc, dve, link, x_res, n.count(CW), ln, xn[n.par], xn_ready)
                for k in range(HB):
                    n = (c.par * HB + k) % 2
                    dve.wait_ge(silu_ready, c.count(HB, k + 1))
                    dve.wait_ge(up_done, c.count(HB, k + 1))
                    v.tensor_tensor(h[c.par][:, k, :], silu[n][:, :], u_bank[n][:, :], ALU.mult).then_inc(h_ready, 1)
                dve.wait_ge(down_done, c.count(1, 1))
                x = x_res[:, bass.ds(c.count(CW), CW)]
                v.tensor_tensor(x, x, y_bank[:, :], ALU.add).then_inc(x_ready, 1)

            link = Chain(dve, chain[0])
            layernorm_chunk(nc, dve, link, x_res, 0, ln, xn[0], xn_ready)
            body(At(0, 0), link, first=True)
            link = Chain(dve, chain[1])
            for c in (1, 2):
                body(At(0, c), link)
            body(At(0, 3), Chain(dve, chain[2]), last=True)


MIN_P = -1e38
MIX = ("k", "v", "r")


def wkv_phase(nc, W, U, mixes, weights_t, ident_in, x_res, sem_of):
    with ExitStack() as ctx:
        def sb(name, shape, dt=F32):
            return ctx.enter_context(nc.sbuf_tensor("wk_" + name, shape, dt))

        def bank(name):
            return ctx.enter_context(nc.psum_tensor("wk_" + name, [P, 512], F32))

        sem = sem_of("wk")
        NB = CW // T
        w = {m: sb("w_" + m, [P, P]) for m in ("k", "v", "r", "o")}
        ident = sb("ident", [P, P])
        cols = sb("cols", [P, 5])
        decay = sb("decay", [P, 2])
        keep = sb("keep", [P, 3])
        ln = ln_tiles(sb)
        xn = [sb(f"xn{i}", [P, TPC, P]) for i in range(2)]
        xT = [sb(f"xT{i}", [P, NB, T + 1]) for i in range(2)]
        mixed = {m: sb("mixed_" + m, [P, NB, T]) for m in MIX}
        scratch = sb("scratch", [P, NB, T])
        V = sb("V", [P, NB, T])
        R = sb("R", [P, NB, T])
        pp = sb("pp", [P, NB, T + 1])
        aa = sb("aa", [P, NB, T + 1])
        bb = sb("bb", [P, NB, T + 1])
        names = ("d1", "d2", "g1", "g2", "e1", "e2", "e1b", "e2b", "ev", "t1", "t2", "t3", "den")
        e = {n: sb(n, [P, NB, T]) for n in names}
        rw = [sb(f"rw{i}", [P, NB, T]) for i in range(2)]
        xt_bank, k_bank, v_bank, r_bank, y_bank = bank("xt"), bank("k"), bank("v"), bank("r"), bank("y")
        w_loaded, consts, xn_ready, tx_done, xT_ready = (
            sem("w_loaded"), sem("consts"), sem("xn_ready"), sem("tx_done"), sem("xT_ready"))
        mixed_ready, proj_done, k_used, v_copied, er_ready = (
            sem("mixed_ready"), sem("proj_done"), sem("k_used"), sem("v_copied"), sem("er_ready"))
        d_ready, e_ready, sums_ready, prods_ready = sem("d_ready"), sem("e_ready"), sem("sums_ready"), sem("prods_ready")
        rw_ready, out_done, x_ready, decay_ready = sem("rw_ready"), sem("out_done"), sem("x_ready"), sem("decay_ready")
        chain = [sem(f"chain{i}") for i in range(3)]
        pool_chain, act_chain = sem("pool_chain"), sem("act_chain")
        block = ctx.enter_context(nc.Block())

        @block.sync
        def _(sp):
            for n, col in enumerate((W, U, *mixes)):
                sp.dma_start(cols[:, n:n + 1], col).then_inc(w_loaded, 16)
            for m, src in zip(("k", "v", "r", "o"), weights_t):
                sp.dma_start(w[m][:, :], src).then_inc(w_loaded, 16)
            sp.dma_start(ident[:, :], ident_in).then_inc(w_loaded, 16)

        @block.gpsimd
        def _(pool):
            g = nc.gpsimd
            g.memset(pp[:, :, 0:1], MIN_P).then_inc(consts, 1)
            g.memset(aa[:, :, 0:1], 0.0).then_inc(consts, 1)
            g.memset(bb[:, :, 0:1], 0.0).then_inc(consts, 1)
            for i in range(2):
                g.memset(xT[i][:, :, 0:1], 0.0).then_inc(consts, 1)
            pool.wait_ge(w_loaded, 160)
            g.tensor_scalar(keep[:, :], cols[:, 2:5], -1.0, 1.0, ALU.mult, ALU.add).then_inc(consts, 1)
            pool.wait_ge(decay_ready, 1)
            g.tensor_scalar(decay[:, 1:2], decay[:, 0:1], -1.0, None, ALU.mult).then_inc(consts, 1)

            def body(c):
                pool.wait_ge(e_ready, c.count(4, 3))
                pool.wait_ge(sums_ready, c.count(2, 1))
                g.tensor_tensor(e["t1"][:, :, :], e["e1"][:, :, :], aa[:, :, 0:T], ALU.mult).then_inc(prods_ready, 1)
                pool.wait_ge(sums_ready, c.count(2, 2))
                g.tensor_tensor(e["t3"][:, :, :], e["e1"][:, :, :], bb[:, :, 0:T], ALU.mult).then_inc(prods_ready, 1)

            with pool.Fori(0, 2) as i:
                for c in (0, 1):
                    body(At(i, c))

        @block.tensor
        def _(pe):
            mm = nc.tensor.matmul

            def transpose_x(c):
                pe.wait_ge(xn_ready, c.count(1, 1))
                pe.wait_ge(xT_ready, c.count(1))
                for a in range(TPC):
                    last = nc.tensor.transpose(xt_bank[:, a * P:(a + 1) * P], xn[c.par][:, a, :], ident[:, :])
                last.then_inc(tx_done, 1)

            def body(c, last=False):
                for n, (m, dst) in enumerate((("k", k_bank), ("v", v_bank), ("r", r_bank))):
                    pe.wait_ge(mixed_ready, c.count(3, n + 1))
                    if m == "k":
                        pe.wait_ge(d_ready, c.count(4))
                    mm(dst[:, :], w[m][:, :], mixed[m][:, :, :].rearrange("p b t -> p (b t)"),
                       start=True, stop=True).then_inc(proj_done, 1)
                if not last:
                    transpose_x(c + 1)
                pe.wait_ge(rw_ready, c.count(1, 1))
                pe.wait_ge(x_ready, c.count(1))
                r = rw[c.par][:, :, :].rearrange("p b t -> p (b t)")
                for a in range(TPC):
                    done = mm(y_bank[:, a * P:(a + 1) * P], r[:, a * P:(a + 1) * P], w["o"][:, :], start=True, stop=True)
                done.then_inc(out_done, 1)

            pe.wait_ge(w_loaded, 160)
            transpose_x(At(0, 0))
            body(At(0, 0))
            for c in (1, 2):
                body(At(0, c))
            body(At(0, 3), last=True)

        @block.scalar
        def _(act):
            def copy_xT(c):
                act.wait_ge(tx_done, c.count(1, 1))
                nc.scalar.copy(xT[c.par][:, :, 1:T + 1], xt_bank[:, :].rearrange("p (b t) -> p b t", b=NB)).then_inc(xT_ready, 1)

            def exp(c, dst, src, scale=1.0):
                nc.scalar.activation(dst[:, :, :], src[:, :, :], ACT.Exp, scale=scale).then_inc(e_ready, 1)

            def body(c, last=False):
                view = lambda b: b[:, :].rearrange("p (b t) -> p b t", b=NB)
                act.wait_ge(proj_done, c.count(3, 2))
                act.wait_ge(rw_ready, c.count(1))
                nc.scalar.copy(V[:, :, :], view(v_bank)).then_inc(v_copied, 1)
                for n, (dst, src) in enumerate((("e1b", "g1"), ("e2b", "g2"), ("e1", "d1"), ("e2", "d2"))):
                    act.wait_ge(d_ready, c.count(4, n + 1))
                    exp(c, e[dst], e[src])
                act.wait_ge(proj_done, c.count(3, 3))
                nc.scalar.activation(R[:, :, :], view(r_bank), ACT.Sigmoid).then_inc(er_ready, 1)
                if not last:
                    copy_xT(c + 1)

            act.wait_ge(w_loaded, 160)
            nc.scalar.activation(decay[:, 0:1], cols[:, 0:1], ACT.Exp).then_inc(decay_ready, 1)
            act.wait_ge(consts, 7)
            copy_xT(At(0, 0))
            body(At(0, 0))
            for c in (1, 2):
                body(At(0, c))
            body(At(0, 3), last=True)

        @block.vector
        def _(dve):
            v = nc.vector

            def mix(c, link):
                dve.wait_ge(xT_ready, c.count(1, 1))
                for n, m in enumerate(MIX):
                    link(v.tensor_scalar(scratch[:, :, :], xT[c.par][:, :, 0:T], keep[:, n:n + 1], None, ALU.mult))
                    v.scalar_tensor_tensor(mixed[m][:, :, :], xT[c.par][:, :, 1:T + 1], cols[:, 2 + n:3 + n],
                                           scratch[:, :, :], ALU.mult, ALU.add).then_inc(mixed_ready, 1)
                    dve.wait_ge(mixed_ready, c.count(3, n + 1))

            def body(c, link, last=False):
                mix(c, link)
                K = k_bank[:, :].rearrange("p (b t) -> p b t", b=NB)
                now, nxt = pp[:, :, 0:T], pp[:, :, 1:T + 1]
                dve.wait_ge(proj_done, c.count(3, 1))
                for b in range(NB):
                    link.done(v.tensor_tensor_scan(pp[:, b, 1:T + 1], decay[:, 1:2].to_broadcast([P, T]), K[:, b, :],
                                                   MIN_P, ALU.add, ALU.max))
                link.wait()
                v.scalar_tensor_tensor(e["g1"][:, :, :], now, decay[:, 1:2], nxt, ALU.add, ALU.subtract).then_inc(d_ready, 1)
                v.tensor_tensor(e["g2"][:, :, :], K, nxt, ALU.subtract).then_inc(d_ready, 1)
                link(v.scalar_tensor_tensor(e["t2"][:, :, :], K, cols[:, 1:2], now, ALU.add, ALU.subtract))
                v.tensor_scalar(e["d1"][:, :, :], e["t2"][:, :, :], -1.0, 0.0, ALU.mult, ALU.min).then_inc(d_ready, 1)
                v.tensor_scalar(e["d2"][:, :, :], e["t2"][:, :, :], 0.0, None, ALU.min).then_inc(d_ready, 1)
                dve.wait_ge(d_ready, c.count(4, 4))
                dve.wait_ge(e_ready, c.count(4, 2))
                dve.wait_ge(v_copied, c.count(1, 1))
                link(v.tensor_tensor(e["ev"][:, :, :], e["e2b"][:, :, :], V[:, :, :], ALU.mult))
                for src, dst in (("ev", aa), ("e2b", bb)):
                    for b in range(NB):
                        done = v.tensor_tensor_scan(dst[:, b, 1:T + 1], e["e1b"][:, b, :], e[src][:, b, :],
                                                    0.0, ALU.mult, ALU.add)
                        if b < NB - 1:
                            link.done(done)
                    done.then_inc(sums_ready, 1)
                if not last:
                    n = c + 1
                    layernorm_chunk(nc, dve, link, x_res, n.count(CW), ln, xn[n.par], xn_ready)
                dve.wait_ge(e_ready, c.count(4, 4))
                link(v.tensor_tensor(e["t2"][:, :, :], e["e2"][:, :, :], V[:, :, :], ALU.mult))
                dve.wait_ge(prods_ready, c.count(2, 1))
                link(v.tensor_tensor(e["t2"][:, :, :], e["t2"][:, :, :], e["t1"][:, :, :], ALU.add))
                dve.wait_ge(prods_ready, c.count(2, 2))
                link(v.tensor_tensor(e["den"][:, :, :], e["t3"][:, :, :], e["e2"][:, :, :], ALU.add))
                link(v.reciprocal(e["den"][:, :, :], e["den"][:, :, :]))
                link(v.tensor_tensor(e["t2"][:, :, :], e["t2"][:, :, :], e["den"][:, :, :], ALU.mult))
                dve.wait_ge(er_ready, c.count(1, 1))
                v.tensor_tensor(rw[c.par][:, :, :], e["t2"][:, :, :], R[:, :, :], ALU.mult).then_inc(rw_ready, 1)
                dve.wait_ge(out_done, c.count(1, 1))
                x = x_res[:, bass.ds(c.count(CW), CW)]
                v.tensor_tensor(x, x, y_bank[:, :], ALU.add).then_inc(x_ready, 1)

            PER = 3 + NB + 1 + 1 + 2 * (NB - 1) + LN_CHAIN + 5
            dve.wait_ge(consts, 7)
            link = Chain(dve, chain[0])
            layernorm_chunk(nc, dve, link, x_res, 0, ln, xn[0], xn_ready)
            body(At(0, 0), link)
            link = Chain(dve, chain[1])
            for c in (1, 2):
                body(At(0, c), link)
            body(At(0, 3), Chain(dve, chain[2]), last=True)


EXPERTS, EXPERT_HIDDEN, CAPACITY = 8, 512, 320
SLOTS = EXPERTS * CAPACITY
KB = EXPERT_HIDDEN // P
SLOT_TILES = ((0, 128), (128, 128), (256, 64))
FAR = 1e6


def moe_consts(np):
    return {
        "iota": np.tile(np.arange(EXPERTS, dtype=np.float32), (P, 1)),
        "tri": np.triu(np.ones((P, P), np.float32)),
    }


def moe_phase(nc, a, out, x_res, sem_of):
    with ExitStack() as ctx:
        def sb(name, shape, dt=F32):
            return ctx.enter_context(nc.sbuf_tensor("mo_" + name, shape, dt))

        def bank(name):
            return ctx.enter_context(nc.psum_tensor("mo_" + name, [P, 512], F32))

        sem = sem_of("mo")
        slots = nc.dram_tensor("mo_slots", [SLOTS, P], F32).ap()
        answers = nc.dram_tensor("mo_answers", [SLOTS, P], F32).ap()
        N = TILES * EXPERTS
        ident, tri32 = sb("ident", [P, P]), sb("tri32", [P, P])
        tri, ones = sb("tri", [P, P], BF16), sb("ones", [P, P], BF16)
        iota, far_iota = sb("iota", [P, EXPERTS]), sb("far_iota", [P, EXPERTS])
        zero = sb("zero", [P, SLOTS // P * P])
        rw, rb = sb("rw", [P, EXPERTS]), sb("rb", [P, EXPERTS])
        b1_rows, b1 = sb("b1_rows", [EXPERTS * KB, P]), sb("b1", [P, EXPERTS * KB])
        b2 = sb("b2", [P, EXPERTS * P])
        ln = ln_tiles(sb)
        xn = sb("xn", [P, TILES, P])
        xT = [sb(f"xT{i}", [P, CW]) for i in range(2)]
        wide = lambda n, dt=F32: sb(n, [P, TILES, EXPERTS], dt)
        gates, eq, cand, masked, prod, pos, total, before = (
            wide(n) for n in ("gates", "eq", "cand", "masked", "prod", "pos", "total", "before"))
        zeros = wide("zeros")
        mask = wide("mask", BF16)
        hot = [wide(f"hot{k}") for k in range(2)]
        per_token = lambda n, dt=F32: sb(n, [P, TILES], dt)
        top, denom = per_token("top"), per_token("denom")
        gate, expert, place, valid, weight, tmp = (
            [per_token(f"{n}{k}") for k in range(2)] for n in ("gate", "expert", "place", "valid", "weight", "tmp"))
        put = [per_token(f"put{k}", U32) for k in range(2)]
        get = [per_token(f"get{k}", U32) for k in range(2)]
        w1 = [sb(f"w1_{i}", [P, EXPERT_HIDDEN]) for i in range(2)]
        w2 = [sb(f"w2_{i}", [P, KB, P]) for i in range(2)]
        xe = [sb(f"xe{i}", [P, 3, P]) for i in range(2)]
        xeT = [sb(f"xeT{i}", [P, CAPACITY]) for i in range(2)]
        hT = [sb(f"hT{i}", [P, KB, CAPACITY]) for i in range(2)]
        ye = [sb(f"ye{i}", [P, 3, P]) for i in range(2)]
        got = sb("got", [P, 2, TILES, P])
        xt_bank, route_bank = bank("xt"), bank("route")
        h_bank = [bank(f"h{k}") for k in range(KB)]
        y_bank = [bank(f"y{i}") for i in range(2)]

        consts_loaded, consts_ready, zeroed = sem("consts_loaded"), sem("consts_ready"), sem("zeroed")
        xn_ready, tx_done, xT_ready, logits_done = sem("xn_ready"), sem("tx_done"), sem("xT_ready"), sem("logits_done")
        shifted, exp_ready, mask_ready, counts_done, counts_read = (
            sem("shifted"), sem("exp_ready"), sem("mask_ready"), sem("counts_done"), sem("counts_read"))
        b1_done, b1_ready = sem("b1_done"), sem("b1_ready")
        routed, scattered, gathered = sem("routed"), sem("scattered"), [sem(f"gathered{t}") for t in range(TILES)]
        w_loaded = [sem(f"w_loaded{i}") for i in range(2)]
        xe_loaded = [sem(f"xe_loaded{i}") for i in range(2)]
        te_done, xeT_ready, up_done, gelu_ready, down_done, ye_ready = (
            sem("te_done"), sem("xeT_ready"), sem("up_done"), sem("gelu_ready"), sem("down_done"), sem("ye_ready"))
        ye_out = [sem(f"ye_out{i}") for i in range(2)]
        y_ready, stored = sem("y_ready"), sem("stored")
        chain = sem("chain")
        CONSTS = 16 * 7
        block = ctx.enter_context(nc.Block())
        out_tiles = out.rearrange("(a p) d -> p a d", p=P)

        @block.sync
        def _(sp):
            for dst, src in ((ident[:, :], a["c_ident"]), (tri32[:, :], a["tri"]), (iota[:, :], a["iota"]),
                             (rw[:, :], a["router_w"]), (rb[:, :], a["router_b"].partition_broadcast(P)),
                             (b1_rows[:, :], a["b1"].rearrange("e (k p) -> (e k) p", p=P)),
                             (b2[:, :], a["b2"].rearrange("e d -> (e d)").partition_broadcast(P))):
                sp.dma_start(dst, src).then_inc(consts_loaded, 16)
            sp.wait_ge(consts_ready, 1)
            sp.dma_start(slots.rearrange("(p a) d -> p (a d)", p=P), zero[:, :]).then_inc(zeroed, 16)

            def load_w(e):
                sp.dma_start(w1[e.par][:, :], a["w1"][bass.ds(e.count(1), 1), :, :].rearrange("e p h -> (e p) h")).then_inc(w_loaded[e.par], 16)
                sp.dma_start(w2[e.par][:, :, :], a["w2"][bass.ds(e.count(1), 1), :, :].rearrange("e (k p) d -> p (e k) d", p=P)).then_inc(w_loaded[e.par], 16)

            def load_x(e):
                at = e.count(CAPACITY)
                sp.dma_start(xe[e.par][:, 0:2, :], slots[bass.ds(at, 256), :].rearrange("(a p) d -> p a d", p=P)).then_inc(xe_loaded[e.par], 16)
                sp.dma_start(xe[e.par][0:64, 2, :], slots[bass.ds(at + 256, 64), :]).then_inc(xe_loaded[e.par], 16)

            def store_y(e):
                at = e.count(CAPACITY)
                sp.wait_ge(ye_ready, e.count(1, 1))
                sp.dma_start(answers[bass.ds(at, 256), :].rearrange("(a p) d -> p a d", p=P), ye[e.par][:, 0:2, :]).then_inc(ye_out[e.par], 16)
                sp.dma_start(answers[bass.ds(at + 256, 64), :], ye[e.par][0:64, 2, :]).then_inc(ye_out[e.par], 16)

            def body(e, last=False):
                if not last:
                    sp.wait_ge(down_done, e.count(1))
                    load_w(e + 1)
                    load_x(e + 1)
                store_y(e)

            load_w(At(0, 0))
            sp.wait_ge(scattered, 16 * 2 * TILES)
            load_x(At(0, 0))
            body(At(0, 0))
            body(At(0, 1))
            with sp.Fori(0, 2) as i:
                for c in (2, 3):
                    body(At(i, c))
            body(At(0, 6))
            body(At(0, 7), last=True)
            for c in range(CHUNKS):
                sp.wait_ge(y_ready, c + 1)
                sp.dma_start(out_tiles[:, c * TPC:(c + 1) * TPC, :],
                             x_res[:, c * CW:(c + 1) * CW].rearrange("p (a d) -> p a d", a=TPC)).then_inc(stored, 16)
            sp.wait_ge(stored, 16 * CHUNKS)

        @block.gpsimd
        def _(pool):
            g = nc.gpsimd
            g.memset(zero[:, :], 0.0).then_inc(consts_ready, 1)
            g.memset(ones[:, :], 1.0).then_inc(consts_ready, 1)
            g.memset(zeros[:, :, :], 0.0).then_inc(consts_ready, 1)
            pool.wait_ge(consts_loaded, CONSTS)
            g.tensor_copy(tri[:, :], tri32[:, :]).then_inc(consts_ready, 1)
            g.tensor_scalar(far_iota[:, :], iota[:, :], float(EXPERTS), None, ALU.add).then_inc(consts_ready, 1)
            pool.wait_ge(zeroed, 16)
            pool.wait_ge(routed, 1)
            for t in range(TILES):
                for k in range(2):
                    g.indirect_dma_start(slots, bass.IndirectOffsetOnAxis(put[k][:, t:t + 1], 0), xn[:, t, :], None,
                                         bounds_check=SLOTS - 1, oob_is_err=False).then_inc(scattered, 16)
            for i in range(2):
                pool.wait_ge(ye_out[i], 32 * (EXPERTS // 2))
            for t in range(TILES):
                for k in range(2):
                    g.indirect_dma_start(got[:, k, t, :], None, answers, bass.IndirectOffsetOnAxis(get[k][:, t:t + 1], 0),
                                         bounds_check=SLOTS - 1, oob_is_err=False).then_inc(gathered[t], 16)

        @block.tensor
        def _(pe):
            mm = nc.tensor.matmul
            pe.wait_ge(consts_loaded, CONSTS)
            for c in range(CHUNKS):
                pe.wait_ge(xn_ready, c + 1)
                pe.wait_ge(xT_ready, c)
                for n in range(TPC):
                    last = nc.tensor.transpose(xt_bank[:, n * P:(n + 1) * P], xn[:, c * TPC + n, :], ident[:, :])
                last.then_inc(tx_done, 1)
                pe.wait_ge(xT_ready, c + 1)
                for n in range(TPC):
                    t = c * TPC + n
                    last = mm(route_bank[:, t * EXPERTS:(t + 1) * EXPERTS], xT[c % 2][:, n * P:(n + 1) * P], rw[:, :],
                              start=True, stop=True)
            last.then_inc(logits_done, 1)
            nc.tensor.transpose(h_bank[0][:, 0:EXPERTS * KB], b1_rows[:, :], ident[0:EXPERTS * KB, 0:EXPERTS * KB]).then_inc(b1_done, 1)
            pe.wait_ge(mask_ready, 1)
            pe.wait_ge(consts_ready, 5)
            flat = mask[:, :, :].rearrange("p t e -> p (t e)")
            mm(route_bank[:, 128:128 + N], tri[:, :], flat, start=True, stop=True)
            mm(route_bank[:, 256:256 + N], ones[:, :], flat, start=True, stop=True).then_inc(counts_done, 1)

            def transpose_e(e):
                pe.wait_ge(xe_loaded[e.par], e.half(32, 32))
                pe.wait_ge(xeT_ready, e.count(1))
                for n, (at, rows) in enumerate(SLOT_TILES):
                    last = nc.tensor.transpose(xt_bank[:, at:at + rows], xe[e.par][0:rows, n, :], ident[0:rows, 0:rows])
                last.then_inc(te_done, 1)

            def body(e, first=False, last=False):
                pe.wait_ge(xeT_ready, e.count(1, 1))
                pe.wait_ge(w_loaded[e.par], e.half(32, 32))
                for k in range(KB):
                    if not first:
                        pe.wait_ge(gelu_ready, e.count(KB, k - KB + 1))
                    mm(h_bank[k][:, 0:CAPACITY], w1[e.par][:, k * P:(k + 1) * P], xeT[e.par][:, :],
                       start=True, stop=True).then_inc(up_done, 1)
                if not last:
                    transpose_e(e + 1)
                if not first:
                    pe.wait_ge(ye_ready, e.count(1, -1))
                pe.wait_ge(gelu_ready, e.count(KB, KB))
                for n, (at, rows) in enumerate(SLOT_TILES):
                    for k in range(KB):
                        done = mm(y_bank[e.par][0:rows, n * P:(n + 1) * P], hT[e.par][:, k, at:at + rows], w2[e.par][:, k, :],
                                  start=k == 0, stop=k == KB - 1)
                done.then_inc(down_done, 1)

            pe.wait_ge(b1_ready, 1)
            transpose_e(At(0, 0))
            body(At(0, 0), first=True)
            body(At(0, 1))
            with pe.Fori(0, 2) as i:
                for c in (2, 3):
                    body(At(i, c))
            body(At(0, 6))
            body(At(0, 7), last=True)

        @block.scalar
        def _(act):
            for c in range(CHUNKS):
                act.wait_ge(tx_done, c + 1)
                nc.scalar.copy(xT[c % 2][:, :], xt_bank[:, :]).then_inc(xT_ready, 1)
            act.wait_ge(b1_done, 1)
            nc.scalar.copy(b1[:, :], h_bank[0][:, 0:EXPERTS * KB]).then_inc(b1_ready, 1)
            act.wait_ge(b1_ready, 1)
            act.wait_ge(shifted, 1)
            nc.scalar.activation(gates[:, :, :], gates[:, :, :], ACT.Exp).then_inc(exp_ready, 1)

            def copy_xeT(e):
                act.wait_ge(te_done, e.count(1, 1))
                nc.scalar.copy(xeT[e.par][:, :], xt_bank[:, 0:CAPACITY]).then_inc(xeT_ready, 1)

            def body(e, last=False):
                for k in range(KB):
                    act.wait_ge(up_done, e.count(KB, k + 1))
                    nc.scalar.activation(hT[e.par][:, k, :], h_bank[k][:, 0:CAPACITY], ACT.Gelu,
                                         bias=b1[:, bass.ds(e.count(KB, k), 1)]).then_inc(gelu_ready, 1)
                if not last:
                    copy_xeT(e + 1)

            copy_xeT(At(0, 0))
            body(At(0, 0))
            body(At(0, 1))
            with act.Fori(0, 2) as i:
                for c in (2, 3):
                    body(At(i, c))
            body(At(0, 6))
            body(At(0, 7), last=True)

        @block.vector
        def _(dve):
            v = nc.vector
            link = Chain(dve, chain)
            for c in range(CHUNKS):
                layernorm_chunk(nc, dve, link, x_res, c * CW, ln, xn[:, c * TPC:(c + 1) * TPC, :], xn_ready)
            dve.wait_ge(logits_done, 1)
            shape = [P, TILES, EXPERTS]
            each = lambda t: t[:, :].unsqueeze(1).to_broadcast(shape)
            every = lambda t: t[:, :].unsqueeze(2).to_broadcast(shape)
            full = lambda t: t[:, :, :]
            tt = v.tensor_tensor
            link(tt(full(gates), route_bank[:, 0:N].rearrange("p (t e) -> p t e", e=EXPERTS), each(rb), ALU.add))
            link(v.reduce_max(top[:, :], full(gates), AX.X))
            tt(full(gates), full(gates), every(top), ALU.subtract).then_inc(shifted, 1)
            dve.wait_ge(exp_ready, 1)
            link(v.reduce_sum(denom[:, :], full(gates), AX.X))
            link(v.reciprocal(denom[:, :], denom[:, :]))
            link(tt(full(gates), full(gates), every(denom), ALU.mult))
            dve.wait_ge(consts_ready, 5)
            source = gates
            for k in range(2):
                link(v.reduce_max(gate[k][:, :], full(source), AX.X))
                link(tt(full(eq), full(source), every(gate[k]), ALU.is_equal))
                link(v.scalar_tensor_tensor(full(cand), full(eq), -float(EXPERTS), each(far_iota), ALU.mult, ALU.add))
                link(v.tensor_reduce(expert[k][:, :], full(cand), AX.X, ALU.min))
                link(tt(full(hot[k]), each(iota), every(expert[k]), ALU.is_equal))
                if k == 0:
                    link(v.scalar_tensor_tensor(full(masked), full(hot[0]), -2.0, full(gates), ALU.mult, ALU.add))
                    source = masked
            tt(full(mask), full(hot[0]), full(hot[1]), ALU.add).then_inc(mask_ready, 1)
            dve.wait_ge(counts_done, 1)
            view = lambda n: route_bank[:, n:n + N].rearrange("p (t e) -> p t e", e=EXPERTS)
            link(v.tensor_copy(full(total), view(256)))
            for e in range(EXPERTS):
                link.done(v.tensor_tensor_scan(before[:, :, e], total[:, :, e], zeros[:, :, e], 0.0, ALU.add, ALU.add))
            link.wait()
            link(tt(full(before), full(before), full(total), ALU.subtract))
            link(tt(full(pos), view(128), full(before), ALU.add))
            for k in range(2):
                link(tt(full(prod), full(hot[k]), full(pos), ALU.mult))
                link(v.reduce_sum(place[k][:, :], full(prod), AX.X))
                link(v.tensor_scalar(place[k][:, :], place[k][:, :], -1.0, None, ALU.add))
                link(v.tensor_scalar(valid[k][:, :], place[k][:, :], float(CAPACITY), None, ALU.is_lt))
                link(tt(weight[k][:, :], gate[k][:, :], valid[k][:, :], ALU.mult))
                link(v.scalar_tensor_tensor(tmp[0][:, :], expert[k][:, :], float(CAPACITY), place[k][:, :], ALU.mult, ALU.add))
                link(v.tensor_scalar(tmp[1][:, :], valid[k][:, :], -FAR, FAR, ALU.mult, ALU.add))
                link(tt(put[k][:, :], tmp[0][:, :], tmp[1][:, :], ALU.add))
                link(v.tensor_scalar(place[k][:, :], place[k][:, :], float(CAPACITY - 1), None, ALU.min))
                link(v.scalar_tensor_tensor(get[k][:, :], expert[k][:, :], float(CAPACITY), place[k][:, :], ALU.mult, ALU.add))
            dve.sem_inc(routed, 1)

            def body(e):
                dve.wait_ge(down_done, e.count(1, 1))
                dve.wait_ge(ye_out[e.par], e.half(32))
                bias = b2[:, bass.ds(e.count(P), P)]
                for n, (_, rows) in enumerate(SLOT_TILES):
                    last = v.tensor_tensor(ye[e.par][0:rows, n, :], y_bank[e.par][0:rows, n * P:(n + 1) * P],
                                           bias[0:rows, :], ALU.add)
                last.then_inc(ye_ready, 1)

            for c in (0, 1):
                body(At(0, c))
            with dve.Fori(0, 3) as i:
                for c in (2, 3):
                    body(At(i, c))

            for t in range(TILES):
                dve.wait_ge(gathered[t], 32)
                x = x_res[:, t * P:(t + 1) * P]
                link(v.scalar_tensor_tensor(x, got[:, 0, t, :], weight[0][:, t:t + 1], x, ALU.mult, ALU.add))
                last = v.scalar_tensor_tensor(x, got[:, 1, t, :], weight[1][:, t:t + 1], x, ALU.mult, ALU.add)
                if t % TPC == TPC - 1:
                    last.then_inc(y_ready, 1)


def attention_consts(np):
    pair_ones = np.zeros((P, 2), np.float32)
    pair_ones[:DV, 0] = pair_ones[DV:, 1] = 1
    sel = np.zeros((3 * HEADS, PAIRS, P), np.float32)
    for part in range(3):
        for h in range(HEADS):
            at = DV * (h % 2)
            sel[part * HEADS + h, h // 2, at:at + DV] = 1
    return {"ident": np.eye(P, dtype=np.float32), "pair_ones": pair_ones, "sel": sel}


def two_layer_program(nc, a, out):
    with ExitStack() as ctx:
        def sem_of(phase):
            return lambda name: ctx.enter_context(nc.semaphore(f"{phase}_{name}"))

        x_res = ctx.enter_context(nc.sbuf_tensor("x_res", [P, TILES * P], F32))
        parts = nc.dram_tensor("parts", [2, 3, 2 * HEADS * DK, T], BF16).ap()
        attention_phase(nc, a["L0_attn_tokens"], a["L0_attn_Wq"], a["L0_attn_Wkv"], a["L0_attn_Wout"],
                        a["ident"], a["pair_ones"], a["sel"], parts, x_res, sem_of)
        ffn_phase(nc, a["L0_ffn_w_gate"], a["L0_ffn_w_up"], a["L0_ffn_w_down"], a["ident"], x_res, sem_of)
        wkv_phase(nc, a["L1_attn_W"], a["L1_attn_U"], [a["L1_attn_time_mix_" + m] for m in "kvr"],
                  [a["L1_attn_W" + m] for m in "kvro"], a["ident"], x_res, sem_of)
        moe = {n: a["L1_ffn_" + n] for n in ("router_w", "router_b", "w1", "b1", "w2", "b2")}
        moe_phase(nc, {**moe, "c_ident": a["ident"], "iota": a["iota"], "tri": a["tri"]}, out, x_res, sem_of)


def kernel(**inputs):
    import numpy as np
    import concourse.bacc as bacc
    from concourse.bass_utils import run_bass_kernel_spmd

    arrays = {}
    for name, a in inputs.items():
        a = np.asarray(a)
        if name.startswith(("L0_ffn_w_", "L1_attn_W")) and a.ndim == 2:
            a = a.T
        elif name.startswith("L1_attn_"):
            a = a.reshape(P, 1)
        arrays[name] = np.ascontiguousarray(a)
    arrays.update(attention_consts(np))
    arrays.update(moe_consts(np))
    nc = bacc.Bacc("TRN2", target_bir_lowering=False, num_devices=1)
    args = {name: nc.dram_tensor("in_" + name, a.shape, mybir.dt.from_np(a.dtype), kind="ExternalInput").ap()
            for name, a in arrays.items()}
    out = nc.dram_tensor("out", [BATCH, T, P], F32, kind="ExternalOutput").ap()
    two_layer_program(nc, args, out.rearrange("b t d -> (b t) d"))
    return run_bass_kernel_spmd(nc, [{"in_" + name: a for name, a in arrays.items()}], core_ids=[0]).results[0]["out"]
```

```python
from contextlib import ExitStack

import concourse.bass as bass
from concourse import mybir

F32 = mybir.dt.float32
BF16 = mybir.dt.bfloat16
I32 = mybir.dt.int32
U32 = mybir.dt.uint32
ALU = mybir.AluOpType
ACT = mybir.ActivationFunctionType
AX = mybir.AxisListType

P = 128
BATCH, T = 8, 256
TOKENS = BATCH * T
TILES = TOKENS // P
TPB = T // P
LN_EPS = 1e-5

HEADS, DK, DV = 16, 16, 64
PAIRS = HEADS // 2
NORM_FLOOR = 1e-24
RSQRT_MAGIC = float(0x5F3759DF)

Q_PART = (0, 0, 1, 1, 0, 2)
K_PART = (0, 1, 0, 1, 2, 0)
COMBOS = len(Q_PART)


class At:

    def __init__(self, i, c):
        self.i, self.c, self.par = i, c, c % 2

    def __add__(self, n):
        return At(self.i, self.c + n)

    def count(self, per, k=0):
        n = self.c * per + k
        return max(n, 0) if isinstance(self.i, int) else self.i * (2 * per) + n

    def half(self, per, k=0):
        return self.i * per + (self.c // 2 * per + k)


class Chain:

    def __init__(self, eng, sem, base=0):
        self.eng, self.sem, self.base, self.n = eng, sem, base, 0

    def done(self, ins):
        ins.then_inc(self.sem, 1)
        self.n += 1
        return self

    def wait(self):
        self.eng.wait_ge(self.sem, self.base + self.n)

    def __call__(self, ins):
        self.done(ins)
        self.wait()


def rsqrt_guess(nc, link, yi, xi):
    link(nc.vector.tensor_scalar(yi, xi, 1, None, ALU.arith_shift_right))
    link(nc.vector.tensor_scalar(yi, yi, -1.0, RSQRT_MAGIC, ALU.mult, ALU.add))


def rsqrt_step(nc, link, y, x, a):
    link(nc.vector.scalar_tensor_tensor(a, y, -0.5, y, ALU.mult, ALU.mult))
    link(nc.vector.tensor_tensor(a, a, x, ALU.mult))
    link(nc.vector.scalar_tensor_tensor(y, a, 1.5, y, ALU.add, ALU.mult))


def rsqrt(nc, link, y, x, a, yi, xi):
    rsqrt_guess(nc, link, yi, xi)
    for _ in range(3):
        rsqrt_step(nc, link, y, x, a)


def attention_phase(nc, x_in, Wq, Wkv, Wout, ident_in, pair_ones_in, head_ones_in, sel_in, parts, x_res, sem_of):
    with ExitStack() as ctx:
        def sb(name, shape, dt=F32):
            return ctx.enter_context(nc.sbuf_tensor("at_" + name, shape, dt))

        def bank(name):
            return ctx.enter_context(nc.psum_tensor("at_" + name, [P, 512], F32))

        sem = sem_of("at")
        QK, V, HQ = 2 * HEADS * DK, HEADS * DV, P // DK
        w_qk = sb("w_qk", [P, QK])
        w_v = sb("w_v", [P, V])
        w_out = sb("w_out", [P, PAIRS, P])
        ident = sb("ident", [P, P])
        pair_ones, head_ones = sb("pair_ones", [P, 2]), sb("head_ones", [P, HQ])
        sel_f32 = sb("sel_f32", [3 * HEADS, PAIRS, P])
        sel = sb("sel", [3 * HEADS, PAIRS, P], BF16)
        ident16 = sb("ident16", [P, P], BF16)
        f_parts = sb("f_parts", [P, TPB, P], BF16)
        f_rest = sb("f_rest", [P, TPB, HEADS])
        fT = sb("fT", [3 * HEADS, T], BF16)
        stats = sb("stats", [P, TILES, 6])
        mv = sb("mv", [P, TILES, 2])
        rstd = sb("rstd", [P, TILES])
        ln_var = sb("ln_var", [P, TILES])
        xn = sb("xn", [P, TPB, P])
        xnT = [sb(f"xnT{i}", [P, T]) for i in range(2)]
        v_raw = [sb(f"v_raw{i}", [P, TPB, V]) for i in range(2)]
        sq_v = sb("sq_v", [P, TPB, V])
        sq_qk = sb("sq_qk", [P, 4, T])
        sums = [sb(f"sums{i}", [P, 96]) for i in range(2)]
        y, a = sb("nr_y", [P, 96]), sb("nr_a", [P, 96])
        fx, fy, fa, fn, th, inv_n = (sb("f_" + n, [P, 32]) for n in ("x", "y", "a", "n", "th", "inv_n"))
        f = sb("f", [P, 32])
        r_qk = [sb(f"r_qk{i}", [P, TPB, 2, HEADS]) for i in range(2)]
        key_factor = [sb(f"key_factor{i}", [P, TPB, HEADS]) for i in range(2)]
        part = [[sb(f"part{i}{j}", [P, 4, T], BF16) for j in range(3)] for i in range(2)]
        rest = sb("rest", [P, 4, T])
        q_stack = [sb(f"q_stack{i}", [COMBOS * DK, HEADS, T], BF16) for i in range(2)]
        k_stack = [sb(f"k_stack{i}", [COMBOS * DK, HEADS, T], BF16) for i in range(2)]
        attn = [sb(f"attn{i}", [P, TPB, T]) for i in range(8)]
        ob = [sb(f"ob{i}", [P, PAIRS, T]) for i in range(2)]
        osq = [sb(f"osq{i}", [P, PAIRS, T]) for i in range(2)]

        sim = [bank(f"sim{i}") for i in range(4)]
        av = [bank(f"av{i}") for i in range(2)]
        misc = even, odd = [bank(f"misc{i}") for i in range(2)]

        x_loaded = [sem(f"x_loaded{i}") for i in range(4)]
        w_loaded, consts_ready = sem("w_loaded"), sem("consts_ready")
        xn_ready, tx_done, xT_ready = sem("xn_ready"), sem("tx_done"), sem("xT_ready")
        qk_done, sq_ready = sem("qk_done"), sem("sq_ready")
        p1_ready, rest_ready, p2_ready, p3_ready = (
            sem("p1_ready"), sem("rest_ready"), sem("p2_ready"), sem("p3_ready"))
        ssq_done, ssq_read = sem("ssq_done"), sem("ssq_read")
        v_done, v_ready = sem("v_done"), sem("v_ready")
        vsum_ready = sem("vsum_ready")
        v_odd_ready = sem("v_odd_ready")
        key_factor_ready = sem("key_factor_ready")
        parts_out = [sem(f"parts_out{i}") for i in range(2)]
        stack_ready = [sem(f"stack_ready{i}") for i in range(2)]
        sim_done, relu_ready = sem("sim_done"), sem("relu_ready")
        attn_even, attn_odd = sem("attn_even"), sem("attn_odd")
        av_done, ob_ready, osq_ready = sem("av_done"), sem("ob_ready"), sem("osq_ready")
        norms_done, norms_read, n_ready, tanh_ready, f_ready = (
            sem("norms_done"), sem("norms_read"), sem("n_ready"), sem("tanh_ready"), sem("f_ready"))
        fT_done, fT_ready = sem("fT_done"), sem("fT_ready")
        bc_done, on_ready = sem("bc_done"), sem("on_ready")
        out_done, x1_ready = sem("out_done"), sem("x1_ready")
        chain_sems = [sem(f"dve_chain{i}") for i in range(5)]

        block = ctx.enter_context(nc.Block())
        x_tiles = x_in.rearrange("b t d -> (b t) d").rearrange("(a p) d -> p a d", p=P)
        xr = x_res[:, :].rearrange("p (a d) -> p a d", a=TILES)
        kv_view = Wkv.rearrange("p (h e) -> p h e", h=HEADS)
        Q4 = TILES // 4
        STACKED = 16 * 2 * COMBOS

        @block.sync
        def _(sp):
            for n in range(4):
                sp.dma_start(xr[:, n * Q4:(n + 1) * Q4, :], x_tiles[:, n * Q4:(n + 1) * Q4, :]).then_inc(x_loaded[n], 16)

            def stack(b):
                sp.wait_ge(p3_ready, b.count(2, 2))
                for j in range(3):
                    sp.dma_start(parts[b.par, j].rearrange("(a p) t -> p a t", p=P),
                                 part[b.par][j][:, :, :]).then_inc(parts_out[b.par], 16)
                sp.wait_ge(parts_out[b.par], b.half(48, 48))
                for c in range(COMBOS):
                    for s, tile, j in ((0, q_stack, Q_PART[c]), (1, k_stack, K_PART[c])):
                        src = parts[b.par, j, s * 256:(s + 1) * 256, :].rearrange("(h d) t -> d h t", d=DK)
                        sp.dma_start(tile[b.par][c * DK:(c + 1) * DK, :, :], src).then_inc(stack_ready[b.par], 16)

            stack(At(0, 0))
            stack(At(0, 1))
            with sp.Fori(0, 3) as i:
                for c in (2, 3):
                    stack(At(i, c))

        @block.tensor
        def _(pe):
            mm = nc.tensor.matmul

            def transpose_x(b, bank):
                pe.wait_ge(xn_ready, b.count(1, 1))
                for t in range(TPB):
                    last = nc.tensor.transpose(bank[:, t * P:(t + 1) * P], xn[:, t, :], ident[:, :])
                last.then_inc(tx_done, 1)

            def project_qk(b, s, bank):
                pe.wait_ge(xT_ready, b.count(1, 1))
                for g in range(2):
                    at = s * 256 + g * P
                    last = mm(bank[:, g * T:(g + 1) * T], w_qk[:, at:at + P], xnT[b.par][:, :], start=True, stop=True)
                last.then_inc(qk_done, 1)

            def project_v(b, j, bank):
                pe.wait_ge(xT_ready, b.count(1, 1))
                t, half = j // 2, j % 2
                mm(bank[:, :], xnT[b.par][:, t * P:(t + 1) * P], w_v[:, half * 512:(half + 1) * 512],
                   start=True, stop=True).then_inc(v_done, 1)

            def sum_qk(b, bank):
                pe.wait_ge(sq_ready, b.count(2, 2))
                for t in range(TPB):
                    for g in range(4):
                        at = t * 2 * HEADS + g * HQ
                        last = mm(bank[:, at:at + HQ], sq_qk[:, g, t * P:(t + 1) * P], head_ones[:, :], start=True, stop=True)
                last.then_inc(ssq_done, 1)

            def scores(b, s):
                if s == 0:
                    pe.wait_ge(stack_ready[b.par], b.half(STACKED, STACKED))
                for e in range(2):
                    h = 2 * s + e
                    pe.wait_ge(relu_ready, b.count(16, h - 3))
                    for j in range(TPB):
                        last = mm(sim[h % 4][:, j * T:(j + 1) * T], k_stack[b.par][:, h, j * P:(j + 1) * P],
                                  q_stack[b.par][:, h, :], start=True, stop=True)
                    last.then_inc(sim_done, 1)

            def values(b, s):
                pe.wait_ge(attn_even, b.count(8, s + 1))
                pe.wait_ge(attn_odd, b.count(8, s + 1))
                if s in (0, 4):
                    pe.wait_ge(v_odd_ready, b.count(2, s // 4 + 1))
                pe.wait_ge(ob_ready, b.count(8, s - 1))
                for j in range(TPB):
                    for e in range(2):
                        h = 2 * s + e
                        last = mm(av[s % 2][e * DV:(e + 1) * DV, 0:T], v_raw[b.par][:, j, h * DV:(h + 1) * DV],
                                  attn[h % 8][:, j, :], start=j == 0, stop=j == TPB - 1)
                last.then_inc(av_done, 1)

            def norms(b, bank):
                pe.wait_ge(osq_ready, b.count(8, 8))
                for s in range(PAIRS):
                    for t in range(TPB):
                        at = t * HEADS + 2 * s
                        last = mm(bank[:, at:at + 2], osq[b.par][:, s, t * P:(t + 1) * P], pair_ones[:, :], start=True, stop=True)
                last.then_inc(norms_done, 1)

            def transpose_factors(b, bank):
                pe.wait_ge(f_ready, b.count(1, 1))
                for t in range(TPB):
                    last = nc.tensor.transpose(bank[:, :].bitcast(BF16)[:, t * P:(t + 1) * P], f_parts[:, t, :], ident16[:, :])
                last.then_inc(fT_done, 1)

            def spread(b, j, bank):
                pe.wait_ge(fT_ready, b.count(1, 1))
                for e in range(2):
                    last = mm(bank[:, e * T:(e + 1) * T], sel[:, 2 * j + e, :], fT[:, :], start=True, stop=True)
                last.then_inc(bc_done, 1)

            def output(b, bank):
                pe.wait_ge(on_ready, b.count(4, 4))
                for t in range(TPB):
                    for s in range(PAIRS):
                        last = mm(bank[:, t * P:(t + 1) * P], ob[b.par][:, s, t * P:(t + 1) * P], w_out[:, s, :],
                                  start=s == 0, stop=s == PAIRS - 1)
                last.then_inc(out_done, 1)

            def body(b, qk=True, v=True, old=True, older=True):
                for s in range(PAIRS):
                    if s < PAIRS - 2:
                        scores(b, s + 2)
                    elif v:
                        scores(b + 1, s + 2 - PAIRS)
                    if s:
                        values(b, s - 1)
                    elif old:
                        values(b + -1, PAIRS - 1)
                    if s == 0 and v:
                        pe.wait_ge(on_ready, b.count(4, -4 - 1))
                        project_v(b + 1, 0, even)
                    if s == 1:
                        if older:
                            output(b + -2, odd)
                        if v:
                            pe.wait_ge(v_ready, b.count(4, 4 + 1))
                            project_v(b + 1, 1, even)
                    if s == 2:
                        if old:
                            pe.wait_ge(x1_ready, b.count(1, -1))
                            norms(b + -1, odd)
                        if qk:
                            pe.wait_ge(v_ready, b.count(4, 4 + 2))
                            transpose_x(b + 2, even)
                    if s == 3:
                        if v:
                            pe.wait_ge(norms_read, b.count(1))
                            project_v(b + 1, 2, odd)
                        if qk:
                            project_qk(b + 2, 0, even)
                    if s == 4:
                        if v:
                            pe.wait_ge(v_ready, b.count(4, 4 + 3))
                            project_v(b + 1, 3, odd)
                        if qk:
                            pe.wait_ge(rest_ready, b.count(2, 4 + 1))
                            project_qk(b + 2, 1, even)
                    if s == 5:
                        if qk:
                            pe.wait_ge(v_ready, b.count(4, 4 + 4))
                            sum_qk(b + 2, odd)
                        if old:
                            if qk:
                                pe.wait_ge(rest_ready, b.count(2, 4 + 2))
                            elif v:
                                pe.wait_ge(v_ready, b.count(4, 4 + 2))
                            else:
                                pe.wait_ge(on_ready, b.count(4, -4 - 1))
                            transpose_factors(b + -1, even)
                    if s == 6 and old:
                        pe.wait_ge(fT_ready, b.count(1))
                        spread(b + -1, 0, even)
                        if qk:
                            pe.wait_ge(ssq_read, b.count(1, 2 + 1))
                        elif v:
                            pe.wait_ge(v_ready, b.count(4, 4 + 4))
                        else:
                            pe.wait_ge(norms_read, b.count(1))
                        spread(b + -1, 1, odd)
                    if s == 7 and old:
                        pe.wait_ge(on_ready, b.count(4, -4 + 1))
                        spread(b + -1, 2, even)
                        pe.wait_ge(on_ready, b.count(4, -4 + 2))
                        spread(b + -1, 3, odd)

            def tail(b):
                values(b, PAIRS - 1)
                output(b + -1, odd)
                norms(b, even)
                pe.wait_ge(x1_ready, b.count(1))
                transpose_factors(b, odd)
                pe.wait_ge(norms_read, b.count(1, 1))
                spread(b, 0, even)
                spread(b, 1, odd)
                for j in (2, 3):
                    pe.wait_ge(on_ready, b.count(4, j - 1))
                    spread(b, j, misc[j % 2])
                output(b, odd)

            def first_qk(b, bank_waits):
                (even, x_free), (odd, k_free) = bank_waits
                pe.wait_ge(*x_free)
                transpose_x(b, even)
                pe.wait_ge(xT_ready, b.count(1, 1))
                project_qk(b, 0, even)
                pe.wait_ge(*k_free)
                project_qk(b, 1, odd)
                pe.wait_ge(sq_ready, b.count(2, 1))
                pe.wait_ge(rest_ready, b.count(2, 1))
                sum_qk(b, even)

            pe.wait_ge(w_loaded, 16 * 8)
            b0, b1 = At(0, 0), At(0, 1)
            first_qk(b0, ((misc[0], (consts_ready, 3)), (misc[1], (consts_ready, 3))))
            project_v_banks = (misc[1], misc[0])
            pe.wait_ge(rest_ready, 2)
            pe.wait_ge(sq_ready, 2)
            project_v(b0, 0, project_v_banks[0])
            pe.wait_ge(ssq_read, 1)
            project_v(b0, 1, project_v_banks[1])
            pe.wait_ge(v_ready, 1)
            project_v(b0, 2, project_v_banks[0])
            pe.wait_ge(v_ready, 2)
            project_v(b0, 3, project_v_banks[1])
            first_qk(b1, ((misc[0], (v_ready, 4)), (misc[1], (v_ready, 3))))
            scores(b0, 0)
            scores(b0, 1)
            pe.wait_ge(ssq_read, 2)
            pe.wait_ge(rest_ready, 4)
            body(b0, old=False, older=False)
            body(b1, older=False)
            with pe.Fori(0, 2) as i:
                for c in (2, 3):
                    body(At(i, c))
            body(At(0, 6), qk=False)
            body(At(0, 7), qk=False, v=False)
            tail(At(0, 7))

        @block.scalar
        def _(act):
            def w_load(dst, src):
                act.dma_start(dst, src).then_inc(w_loaded, 16)

            w_load(ident[:, :], ident_in)
            w_load(w_qk[:, 0:256], Wq)
            w_load(w_qk[:, 256:512].rearrange("p (h d) -> p h d", h=HEADS), kv_view[:, :, 0:DK])
            w_load(w_v[:, :].rearrange("p (h d) -> p h d", h=HEADS), kv_view[:, :, DK:DK + DV])
            w_load(head_ones[:, :], head_ones_in)
            w_load(w_out[:, :, :], Wout.rearrange("(s p) n -> p s n", p=P))
            w_load(pair_ones[:, :], pair_ones_in)
            w_load(sel_f32[:, :, :], sel_in)

            def copy_xT(b, bank):
                act.wait_ge(tx_done, b.count(1, 1))
                act.wait_ge(v_done, b.count(4, -4))
                nc.scalar.copy(xnT[b.par][:, :], bank[:, 0:T]).then_inc(xT_ready, 1)

            def copy_v(b, j, bank):
                act.wait_ge(v_done, b.count(4, j + 1))
                act.wait_ge(av_done, b.count(8, -8))
                act.wait_ge(vsum_ready, b.count(2, j // 2 - 1))
                t, half = j // 2, slice(j % 2 * 512, (j % 2 + 1) * 512)
                nc.scalar.copy(v_raw[b.par][:, t, half], bank[:, :])
                nc.scalar.activation(sq_v[:, t, half], bank[:, :], ACT.Square).then_inc(v_ready, 1)

            def square_and_part1(b, s, bank):
                act.wait_ge(qk_done, b.count(2, s + 1))
                act.wait_ge(ssq_done, b.count(1))
                at = slice(2 * s, 2 * s + 2)
                two = bank[:, :].rearrange("p (g t) -> p g t", g=2)
                nc.scalar.activation(sq_qk[:, at, :], two, ACT.Square).then_inc(sq_ready, 1)
                act.wait_ge(parts_out[b.par], b.half(48))
                nc.scalar.copy(part[b.par][0][:, at, :], two).then_inc(p1_ready, 1)

            def part2(b, s):
                at = slice(2 * s, 2 * s + 2)
                act.wait_ge(rest_ready, b.count(2, s + 1))
                nc.scalar.copy(part[b.par][1][:, at, :], rest[:, at, :]).then_inc(p2_ready, 1)

            def relu(b, s):
                act.wait_ge(av_done, b.count(8, s - 3))
                for h in (2 * s, 2 * s + 1):
                    act.wait_ge(sim_done, b.count(16, h + 1))
                    nc.scalar.activation(attn[h % 8][:, :, :].rearrange("p j t -> p (j t)"), sim[h % 4][:, :],
                                         ACT.Relu).then_inc(relu_ready, 1)

            def copy_ob(b, s):
                act.wait_ge(av_done, b.count(8, s + 1))
                if s == 0:
                    act.wait_ge(out_done, b.count(1, -1))
                nc.scalar.copy(ob[b.par][:, s, :], av[s % 2][:, 0:T]).then_inc(ob_ready, 1)

            def tanh(b):
                act.wait_ge(n_ready, b.count(1, 1))
                nc.scalar.activation(th[:, :], fn[:, :], ACT.Tanh).then_inc(tanh_ready, 1)

            def copy_fT(b, bank):
                act.wait_ge(fT_done, b.count(1, 1))
                act.wait_ge(bc_done, b.count(4))
                nc.scalar.copy(fT[:, :], bank[0:3 * HEADS, :].bitcast(BF16)[:, 0:T]).then_inc(fT_ready, 1)

            def body(b, qk=True, v=True, old=True):
                for s in range(PAIRS):
                    if s < PAIRS - 1:
                        relu(b, s + 1)
                    elif v:
                        relu(b + 1, 0)
                    if s > 1:
                        copy_ob(b, s - 2)
                    elif old:
                        copy_ob(b + -1, PAIRS + s - 2)
                    if s in (0, 1) and v:
                        copy_v(b + 1, s, even)
                    if s == 2 and qk:
                        copy_xT(b + 2, even)
                    if s in (3, 4):
                        if s == 4 and old:
                            tanh(b + -1)
                        if v:
                            copy_v(b + 1, s - 1, odd)
                        if qk:
                            square_and_part1(b + 2, s - 3, even)
                    if s == 5 and old:
                        copy_fT(b + -1, even)
                    if s in (5, 6) and qk:
                        part2(b + 2, s - 5)

            b0, b1 = At(0, 0), At(0, 1)
            copy_xT(b0, misc[0])
            for s in range(2):
                square_and_part1(b0, s, misc[s])
            part2(b0, 0)
            part2(b0, 1)
            for j in range(4):
                copy_v(b0, j, misc[(j + 1) % 2])
            copy_xT(b1, misc[0])
            for s in range(2):
                square_and_part1(b1, s, misc[s])
            relu(b0, 0)
            part2(b1, 0)
            part2(b1, 1)
            body(b0, old=False)
            body(b1)
            with act.Fori(0, 2) as i:
                for c in (2, 3):
                    body(At(i, c))
            body(At(0, 6), qk=False)
            body(At(0, 7), qk=False, v=False)
            copy_ob(At(0, 7), PAIRS - 2)
            copy_ob(At(0, 7), PAIRS - 1)
            tanh(At(0, 7))
            copy_fT(At(0, 7), odd)

        @block.vector
        def _(dve):
            v = nc.vector

            def normalize_x(b):
                dve.wait_ge(tx_done, b.count(1))
                for t in range(TPB):
                    at = b.count(TPB, t)
                    last = v.tensor_scalar(xn[:, t, :], x_res[:, bass.ds(at * P, P)],
                                           mv[:, :, :].rearrange("p a c -> p (a c)")[:, bass.ds(at * 2, 1)],
                                           rstd[:, bass.ds(at, 1)], ALU.subtract, ALU.mult)
                last.then_inc(xn_ready, 1)

            def split_rest(b, s, bank):
                at = slice(2 * s, 2 * s + 2)
                dve.wait_ge(p1_ready, b.count(2, s + 1))
                dve.wait_ge(p3_ready, b.count(2))
                v.tensor_tensor(rest[:, at, :], bank[:, :].rearrange("p (g t) -> p g t", g=2),
                                part[b.par][0][:, at, :], ALU.subtract).then_inc(rest_ready, 1)

            def read_sums(b, bank, link):
                dve.wait_ge(ssq_done, b.count(1, 1))
                v.tensor_scalar(sums[b.par][:, 0:64], bank[:, 0:64], NORM_FLOOR, None, ALU.max).then_inc(ssq_read, 1)
                dve.wait_ge(ssq_read, b.count(1, 1))

            def reduce_v(b, t):
                dve.wait_ge(v_ready, b.count(4, 2 * t + 2))
                at = 64 + t * HEADS
                v.reduce_sum(sums[b.par][:, at:at + HEADS], sq_v[:, t, :].rearrange("p (h d) -> p h d", d=DV),
                             AX.X).then_inc(vsum_ready, 1)

            def start_inverse_norms(b, link):
                dve.wait_ge(vsum_ready, b.count(2, 2))
                x = sums[b.par]
                link(v.tensor_scalar(x[:, 64:96], x[:, 64:96], NORM_FLOOR, None, ALU.max))
                rsqrt_guess(nc, link, y[:, :].bitcast(I32), x[:, :].bitcast(I32))
                rsqrt_step(nc, link, y[:, :], x[:, :], a[:, :])

            def end_inverse_norms(b, link):
                for _ in range(2):
                    rsqrt_step(nc, link, y[:, :], sums[b.par][:, :], a[:, :])
                flat = r_qk[b.par][:, :, :, :].rearrange("p t k h -> p (t k h)")
                link(v.tensor_tensor(flat, y[:, 0:64], y[:, 0:64], ALU.mult))

            def make_key_factor(b, link):
                v.tensor_tensor(key_factor[b.par][:, :, :], r_qk[b.par][:, :, 1, :],
                                y[:, 64:96].rearrange("p (t h) -> p t h", t=TPB), ALU.mult).then_inc(key_factor_ready, 1)
                dve.wait_ge(key_factor_ready, b.count(1, 1))

            def square(b, s):
                h = 2 * s
                dve.wait_ge(relu_ready, b.count(16, h + 1))
                for j in range(TPB):
                    r = attn[h % 8][:, j, :]
                    last = v.scalar_tensor_tensor(r, r, key_factor[b.par][:, j, h:h + 1], r, ALU.mult, ALU.mult)
                last.then_inc(attn_even, 1)

            def read_norms(b, bank, link):
                dve.wait_ge(norms_done, b.count(1, 1))
                r = r_qk[b.par][:, :, 0, :]
                n3 = fn[:, :].rearrange("p (t h) -> p t h", t=TPB)
                v.tensor_tensor(n3, bank[:, 0:32].rearrange("p (t h) -> p t h", t=TPB), r, ALU.mult).then_inc(norms_read, 1)
                dve.wait_ge(norms_read, b.count(1, 1))
                link(v.tensor_tensor(n3, n3, r, ALU.mult))
                link(v.tensor_scalar(fx[:, :], fn[:, :], NORM_FLOOR, None, ALU.max))
                rsqrt_guess(nc, link, fy[:, :].bitcast(I32), fx[:, :].bitcast(I32))

            def factors(b, link):
                for _ in range(3):
                    rsqrt_step(nc, link, fy[:, :], fx[:, :], fa[:, :])
                v.tensor_tensor(fn[:, :], fn[:, :], fy[:, :], ALU.mult).then_inc(n_ready, 1)
                link(v.tensor_tensor(inv_n[:, :].rearrange("p (t h) -> p t h", t=TPB),
                                     fy[:, :].rearrange("p (t h) -> p t h", t=TPB), r_qk[b.par][:, :, 0, :], ALU.mult))

            def f_part(c):
                return f_parts[:, :, c * HEADS:(c + 1) * HEADS]

            def tanh_factor(b, link):
                dve.wait_ge(tanh_ready, b.count(1, 1))
                dve.wait_ge(fT_done, b.count(1))
                f3 = f[:, :].rearrange("p (t h) -> p t h", t=TPB)
                link(v.tensor_tensor(f[:, :], th[:, :], inv_n[:, :], ALU.mult))
                link(v.tensor_copy(f_part(0), f3))
                link(v.tensor_tensor(f_rest[:, :, :], f3, f_part(0), ALU.subtract))
                link(v.tensor_copy(f_part(1), f_rest[:, :, :]))
                v.tensor_tensor(f_part(2), f_rest[:, :, :], f_part(1), ALU.subtract).then_inc(f_ready, 1)

            def scale_ob(b, j, bank):
                dve.wait_ge(bc_done, b.count(4, j + 1))
                o = ob[b.par][:, 2 * j:2 * j + 2, :]
                v.tensor_tensor(o, o, bank[:, :].rearrange("p (g t) -> p g t", g=2), ALU.mult).then_inc(on_ready, 1)

            def residual(b, bank):
                dve.wait_ge(out_done, b.count(1, 1))
                at = x_res[:, bass.ds(b.count(T), T)]
                v.tensor_tensor(at, at, bank[:, 0:T], ALU.add).then_inc(x1_ready, 1)

            def body(b, link, qk=True, v=True, old=True, older=True):
                for s in range(PAIRS):
                    if s < PAIRS - 1:
                        square(b, s + 1)
                    if s == 0:
                        if older:
                            scale_ob(b + -2, 3, odd)
                        if qk:
                            normalize_x(b + 2)
                    if s == 1 and older:
                        residual(b + -2, odd)
                    if s == 2:
                        if old:
                            read_norms(b + -1, odd, link)
                        if v:
                            reduce_v(b + 1, 0)
                    if s == 3 and old:
                        factors(b + -1, link)
                    if s == 4:
                        if qk:
                            split_rest(b + 2, 0, even)
                        if old:
                            tanh_factor(b + -1, link)
                    if s == 5:
                        if qk:
                            split_rest(b + 2, 1, even)
                        if v:
                            reduce_v(b + 1, 1)
                    if s == 6:
                        if qk:
                            read_sums(b + 2, odd, link)
                        if old:
                            scale_ob(b + -1, 0, even)
                        if v:
                            start_inverse_norms(b + 1, link)
                    if s == 7:
                        if old:
                            scale_ob(b + -1, 1, odd)
                        if v:
                            end_inverse_norms(b + 1, link)
                            make_key_factor(b + 1, link)
                        if old:
                            scale_ob(b + -1, 2, even)
                        if v:
                            square(b + 1, 0)

            link = Chain(dve, chain_sems[0])
            for t in range(TILES):
                if t % Q4 == 0:
                    dve.wait_ge(x_loaded[t // Q4], 16)
                link.done(v.bn_stats(stats[:, t, :], xr[:, t, :]))
            link.wait()
            for t in range(TILES):
                link.done(v.bn_aggr(mv[:, t, :], stats[:, t, :]))
            link.wait()
            link(v.tensor_scalar(ln_var[:, :], mv[:, :, 1], LN_EPS, None, ALU.add))
            rsqrt(nc, link, rstd[:, :], ln_var[:, :], a[:, 0:TILES], rstd[:, :].bitcast(I32), ln_var[:, :].bitcast(I32))
            dve.wait_ge(consts_ready, 1)
            b0, b1 = At(0, 0), At(0, 1)
            normalize_x(b0)
            split_rest(b0, 0, misc[0])
            split_rest(b0, 1, misc[1])
            read_sums(b0, misc[0], link)
            normalize_x(b1)
            reduce_v(b0, 0)
            reduce_v(b0, 1)
            start_inverse_norms(b0, link)
            end_inverse_norms(b0, link)
            make_key_factor(b0, link)
            split_rest(b1, 0, misc[0])
            split_rest(b1, 1, misc[1])
            read_sums(b1, misc[0], link)
            square(b0, 0)
            body(b0, Chain(dve, chain_sems[1]), old=False, older=False)
            body(b1, Chain(dve, chain_sems[2]), older=False)
            with dve.Fori(0, 2) as i:
                for c in (2, 3):
                    link = Chain(dve, chain_sems[3], i * (2 * CHAIN_PER_BODY) + (c - 2) * CHAIN_PER_BODY)
                    body(At(i, c), link)
                    assert link.n == CHAIN_PER_BODY, link.n
            link = Chain(dve, chain_sems[4])
            body(At(0, 6), link, qk=False)
            b7 = At(0, 7)
            body(b7, link, qk=False, v=False)
            scale_ob(At(0, 6), 3, odd)
            residual(At(0, 6), odd)
            read_norms(b7, even, link)
            factors(b7, link)
            tanh_factor(b7, link)
            for j in range(4):
                scale_ob(b7, j, misc[j % 2])
            residual(b7, odd)

        @block.gpsimd
        def _(pool):
            g = nc.gpsimd
            pool.wait_ge(w_loaded, 16 * 8)
            g.memset(f_parts[:, :, :], 0.0).then_inc(consts_ready, 1)
            g.tensor_copy(ident16[:, :], ident[:, :]).then_inc(consts_ready, 1)
            g.tensor_copy(sel[:, :, :], sel_f32[:, :, :]).then_inc(consts_ready, 1)

            def scale_v(b, half):
                pool.wait_ge(key_factor_ready, b.count(1, 1))
                for t in range(TPB):
                    heads = v_raw[b.par][:, t, :].rearrange("p (s e d) -> p s e d", e=2, d=DV)[:, 4 * half:4 * half + 4, 1, :]
                    factor = key_factor[b.par][:, t, :].rearrange("p (s e) -> p s e", e=2)[:, 4 * half:4 * half + 4, 1]
                    last = g.tensor_tensor(heads, heads, factor.unsqueeze(2).to_broadcast([P, 4, DV]), ALU.mult)
                last.then_inc(v_odd_ready, 1)

            def part3(b, s):
                at = slice(2 * s, 2 * s + 2)
                pool.wait_ge(p2_ready, b.count(2, s + 1))
                g.tensor_tensor(part[b.par][2][:, at, :], rest[:, at, :], part[b.par][1][:, at, :],
                                ALU.subtract).then_inc(p3_ready, 1)

            def square(b, s):
                h = 2 * s + 1
                pool.wait_ge(relu_ready, b.count(16, h + 1))
                r = attn[h % 8][:, :, :]
                g.tensor_tensor(r, r, r, ALU.mult).then_inc(attn_odd, 1)

            def square_ob(b, s):
                pool.wait_ge(ob_ready, b.count(8, s + 1))
                o = ob[b.par][:, s, :]
                g.tensor_tensor(osq[b.par][:, s, :], o, o, ALU.mult).then_inc(osq_ready, 1)

            def body(b, qk=True, v=True, old=True):
                for s in range(PAIRS):
                    if s < PAIRS - 1:
                        square(b, s + 1)
                    elif v:
                        square(b + 1, 0)
                    if s > 1:
                        square_ob(b, s - 2)
                    elif old:
                        square_ob(b + -1, PAIRS + s - 2)
                    if s in (6, 7) and qk:
                        part3(b + 2, s - 6)
                if v:
                    scale_v(b + 1, 0)
                    scale_v(b + 1, 1)

            b0, b1 = At(0, 0), At(0, 1)
            part3(b0, 0)
            part3(b0, 1)
            scale_v(b0, 0)
            scale_v(b0, 1)
            square(b0, 0)
            part3(b1, 0)
            part3(b1, 1)
            body(b0, old=False)
            body(b1)
            with pool.Fori(0, 2) as i:
                for c in (2, 3):
                    body(At(i, c))
            body(At(0, 6), qk=False)
            body(At(0, 7), qk=False, v=False)
            square_ob(At(0, 7), PAIRS - 2)
            square_ob(At(0, 7), PAIRS - 1)


CHAIN_PER_BODY = 2 + 11 + 1 + 4 + 1 + 11 + 1


CHUNKS = 4
TPC = TILES // CHUNKS
CW = TPC * P
HIDDEN = 384
HB = HIDDEN // P
INT_SCALE = 1.0 / 127.0


def layernorm_chunk(nc, dve, link, x_res, at, t, xn, ready):
    v = nc.vector
    for a in range(TPC):
        link.done(v.bn_stats(t["stats"][:, a, :], x_res[:, bass.ds(at + a * P, P)]))
    link.wait()
    for a in range(TPC):
        link.done(v.bn_aggr(t["mv"][:, a, :], t["stats"][:, a, :]))
    link.wait()
    link(v.tensor_scalar(t["var"][:, :], t["mv"][:, :, 1], LN_EPS, None, ALU.add))
    rsqrt(nc, link, t["rstd"][:, :], t["var"][:, :], t["a"][:, :], t["rstd"][:, :].bitcast(I32), t["var"][:, :].bitcast(I32))
    for a in range(TPC):
        last = v.tensor_scalar(xn[:, a, :], x_res[:, bass.ds(at + a * P, P)], t["mv"][:, a, 0:1],
                               t["rstd"][:, a:a + 1], ALU.subtract, ALU.mult)
    last.then_inc(ready, 1)


LN_CHAIN = 2 * TPC + 1 + 11


def ln_tiles(sb):
    return {"stats": sb("ln_stats", [P, TPC, 6]), "mv": sb("ln_mv", [P, TPC, 2]), "var": sb("ln_var2", [P, TPC]),
            "rstd": sb("ln_rstd", [P, TPC]), "a": sb("ln_a", [P, TPC])}


def ffn_phase(nc, w_gate_t, w_up_t, w_down_t, ident_in, x_res, sem_of):
    with ExitStack() as ctx:
        def sb(name, shape, dt=F32):
            return ctx.enter_context(nc.sbuf_tensor("ff_" + name, shape, dt))

        def bank(name):
            return ctx.enter_context(nc.psum_tensor("ff_" + name, [P, 512], F32))

        sem = sem_of("ff")
        w_int = sb("w_int", [P, 3, HIDDEN], I32)
        w_gu = sb("w_gu", [P, 2, HIDDEN])
        w_dn = sb("w_dn", [P, HB, P])
        ident = sb("ident", [P, P])
        ln = ln_tiles(sb)
        xn = [sb(f"xn{i}", [P, TPC, P]) for i in range(2)]
        xnT = [sb(f"xnT{i}", [P, CW]) for i in range(2)]
        silu = [sb(f"silu{i}", [P, CW]) for i in range(2)]
        h = [sb(f"h{i}", [P, HB, CW]) for i in range(2)]
        xt_bank = bank("xt")
        g_bank = [bank(f"g{i}") for i in range(2)]
        u_bank = [bank(f"u{i}") for i in range(2)]
        y_bank = bank("y")
        w_loaded, w_ready = sem("w_loaded"), sem("w_ready")
        xn_ready, tx_done, xT_ready = sem("xn_ready"), sem("tx_done"), sem("xT_ready")
        gate_done, up_done, silu_ready, h_ready = sem("gate_done"), sem("up_done"), sem("silu_ready"), sem("h_ready")
        down_done, x_ready = sem("down_done"), sem("x_ready")
        chain = [sem(f"chain{i}") for i in range(3)]
        block = ctx.enter_context(nc.Block())

        @block.sync
        def _(sp):
            sp.dma_start(w_int[:, 0, :], w_gate_t).then_inc(w_loaded, 16)
            sp.dma_start(w_int[:, 1, :], w_up_t).then_inc(w_loaded, 16)
            sp.dma_start(w_int[:, 2, :].rearrange("p (k d) -> p k d", k=HB),
                         w_down_t.rearrange("(k p) d -> p k d", p=P)).then_inc(w_loaded, 16)
            sp.dma_start(ident[:, :], ident_in).then_inc(w_loaded, 16)

        @block.gpsimd
        def _(pool):
            pool.wait_ge(w_loaded, 64)
            nc.gpsimd.tensor_scalar(w_gu[:, :, :], w_int[:, 0:2, :], INT_SCALE, None, ALU.mult).then_inc(w_ready, 1)
            nc.gpsimd.tensor_scalar(w_dn[:, :, :].rearrange("p k d -> p (k d)"), w_int[:, 2, :], INT_SCALE, None,
                                    ALU.mult).then_inc(w_ready, 1)

        @block.tensor
        def _(pe):
            mm = nc.tensor.matmul

            def transpose_x(c):
                pe.wait_ge(xn_ready, c.count(1, 1))
                pe.wait_ge(xT_ready, c.count(1))
                for a in range(TPC):
                    last = nc.tensor.transpose(xt_bank[:, a * P:(a + 1) * P], xn[c.par][:, a, :], ident[:, :])
                last.then_inc(tx_done, 1)

            def body(c, first=False, last=False):
                pe.wait_ge(xT_ready, c.count(1, 1))
                for k in range(HB):
                    n = (c.par * HB + k) % 2
                    if not (first and k < 2):
                        pe.wait_ge(h_ready, c.count(HB, k - 1))
                    mm(g_bank[n][:, :], w_gu[:, 0, k * P:(k + 1) * P], xnT[c.par][:, :], start=True, stop=True).then_inc(gate_done, 1)
                    mm(u_bank[n][:, :], w_gu[:, 1, k * P:(k + 1) * P], xnT[c.par][:, :], start=True, stop=True).then_inc(up_done, 1)
                    if k == 1 and not last:
                        transpose_x(c + 1)
                pe.wait_ge(x_ready, c.count(1))
                pe.wait_ge(h_ready, c.count(HB, HB))
                for a in range(TPC):
                    for k in range(HB):
                        done = mm(y_bank[:, a * P:(a + 1) * P], h[c.par][:, k, a * P:(a + 1) * P], w_dn[:, k, :],
                                  start=k == 0, stop=k == HB - 1)
                done.then_inc(down_done, 1)

            pe.wait_ge(w_ready, 2)
            transpose_x(At(0, 0))
            body(At(0, 0), first=True)
            for c in (1, 2):
                body(At(0, c))
            body(At(0, 3), last=True)

        @block.scalar
        def _(act):
            def copy_xT(c):
                act.wait_ge(tx_done, c.count(1, 1))
                nc.scalar.copy(xnT[c.par][:, :], xt_bank[:, :]).then_inc(xT_ready, 1)

            def body(c, first=False, last=False):
                for k in range(HB):
                    n = (c.par * HB + k) % 2
                    act.wait_ge(gate_done, c.count(HB, k + 1))
                    if not (first and k < 2):
                        act.wait_ge(h_ready, c.count(HB, k - 1))
                    nc.scalar.activation(silu[n][:, :], g_bank[n][:, :], ACT.Silu).then_inc(silu_ready, 1)
                    if k == 1 and not last:
                        copy_xT(c + 1)

            copy_xT(At(0, 0))
            body(At(0, 0), first=True)
            for c in (1, 2):
                body(At(0, c))
            body(At(0, 3), last=True)

        @block.vector
        def _(dve):
            v = nc.vector

            def body(c, link, first=False, last=False):
                if not last:
                    n = c + 1
                    layernorm_chunk(nc, dve, link, x_res, n.count(CW), ln, xn[n.par], xn_ready)
                for k in range(HB):
                    n = (c.par * HB + k) % 2
                    dve.wait_ge(silu_ready, c.count(HB, k + 1))
                    dve.wait_ge(up_done, c.count(HB, k + 1))
                    v.tensor_tensor(h[c.par][:, k, :], silu[n][:, :], u_bank[n][:, :], ALU.mult).then_inc(h_ready, 1)
                dve.wait_ge(down_done, c.count(1, 1))
                x = x_res[:, bass.ds(c.count(CW), CW)]
                v.tensor_tensor(x, x, y_bank[:, :], ALU.add).then_inc(x_ready, 1)

            link = Chain(dve, chain[0])
            layernorm_chunk(nc, dve, link, x_res, 0, ln, xn[0], xn_ready)
            body(At(0, 0), link, first=True)
            link = Chain(dve, chain[1])
            for c in (1, 2):
                body(At(0, c), link)
            body(At(0, 3), Chain(dve, chain[2]), last=True)


MIN_P = -1e38
MIX = ("k", "v", "r")


def wkv_phase(nc, W, U, mixes, weights_t, ident_in, x_res, sem_of):
    with ExitStack() as ctx:
        def sb(name, shape, dt=F32):
            return ctx.enter_context(nc.sbuf_tensor("wk_" + name, shape, dt))

        def bank(name):
            return ctx.enter_context(nc.psum_tensor("wk_" + name, [P, 512], F32))

        sem = sem_of("wk")
        NB = CW // T
        w = {m: sb("w_" + m, [P, P]) for m in ("k", "v", "r", "o")}
        ident = sb("ident", [P, P])
        cols = sb("cols", [P, 5])
        decay = sb("decay", [P, 2])
        keep = sb("keep", [P, 3])
        ln = ln_tiles(sb)
        xn = [sb(f"xn{i}", [P, TPC, P]) for i in range(2)]
        xT = [sb(f"xT{i}", [P, NB, T + 1]) for i in range(2)]
        mixed = {m: sb("mixed_" + m, [P, NB, T]) for m in MIX}
        scratch = sb("scratch", [P, NB, T])
        V = sb("V", [P, NB, T])
        R = sb("R", [P, NB, T])
        pp = sb("pp", [P, NB, T + 1])
        aa = sb("aa", [P, NB, T + 1])
        bb = sb("bb", [P, NB, T + 1])
        names = ("d1", "d2", "g1", "g2", "e1", "e2", "e1b", "e2b", "ev", "t1", "t2", "t3", "den")
        e = {n: sb(n, [P, NB, T]) for n in names}
        rw = [sb(f"rw{i}", [P, NB, T]) for i in range(2)]
        xt_bank, k_bank, v_bank, r_bank, y_bank = bank("xt"), bank("k"), bank("v"), bank("r"), bank("y")
        w_loaded, consts, xn_ready, tx_done, xT_ready = (
            sem("w_loaded"), sem("consts"), sem("xn_ready"), sem("tx_done"), sem("xT_ready"))
        mixed_ready, proj_done, k_used, v_copied, er_ready = (
            sem("mixed_ready"), sem("proj_done"), sem("k_used"), sem("v_copied"), sem("er_ready"))
        d_ready, e_ready, sums_ready, prods_ready = sem("d_ready"), sem("e_ready"), sem("sums_ready"), sem("prods_ready")
        rw_ready, out_done, x_ready, decay_ready = sem("rw_ready"), sem("out_done"), sem("x_ready"), sem("decay_ready")
        chain = [sem(f"chain{i}") for i in range(3)]
        pool_chain, act_chain = sem("pool_chain"), sem("act_chain")
        block = ctx.enter_context(nc.Block())

        @block.sync
        def _(sp):
            for n, col in enumerate((W, U, *mixes)):
                sp.dma_start(cols[:, n:n + 1], col).then_inc(w_loaded, 16)
            for m, src in zip(("k", "v", "r", "o"), weights_t):
                sp.dma_start(w[m][:, :], src).then_inc(w_loaded, 16)
            sp.dma_start(ident[:, :], ident_in).then_inc(w_loaded, 16)

        @block.gpsimd
        def _(pool):
            g = nc.gpsimd
            g.memset(pp[:, :, 0:1], MIN_P).then_inc(consts, 1)
            g.memset(aa[:, :, 0:1], 0.0).then_inc(consts, 1)
            g.memset(bb[:, :, 0:1], 0.0).then_inc(consts, 1)
            for i in range(2):
                g.memset(xT[i][:, :, 0:1], 0.0).then_inc(consts, 1)
            pool.wait_ge(w_loaded, 160)
            g.tensor_scalar(keep[:, :], cols[:, 2:5], -1.0, 1.0, ALU.mult, ALU.add).then_inc(consts, 1)
            pool.wait_ge(decay_ready, 1)
            g.tensor_scalar(decay[:, 1:2], decay[:, 0:1], -1.0, None, ALU.mult).then_inc(consts, 1)

            def body(c):
                pool.wait_ge(e_ready, c.count(4, 3))
                pool.wait_ge(sums_ready, c.count(2, 1))
                g.tensor_tensor(e["t1"][:, :, :], e["e1"][:, :, :], aa[:, :, 0:T], ALU.mult).then_inc(prods_ready, 1)
                pool.wait_ge(sums_ready, c.count(2, 2))
                g.tensor_tensor(e["t3"][:, :, :], e["e1"][:, :, :], bb[:, :, 0:T], ALU.mult).then_inc(prods_ready, 1)

            with pool.Fori(0, 2) as i:
                for c in (0, 1):
                    body(At(i, c))

        @block.tensor
        def _(pe):
            mm = nc.tensor.matmul

            def transpose_x(c):
                pe.wait_ge(xn_ready, c.count(1, 1))
                pe.wait_ge(xT_ready, c.count(1))
                for a in range(TPC):
                    last = nc.tensor.transpose(xt_bank[:, a * P:(a + 1) * P], xn[c.par][:, a, :], ident[:, :])
                last.then_inc(tx_done, 1)

            def body(c, last=False):
                for n, (m, dst) in enumerate((("k", k_bank), ("v", v_bank), ("r", r_bank))):
                    pe.wait_ge(mixed_ready, c.count(3, n + 1))
                    if m == "k":
                        pe.wait_ge(d_ready, c.count(4))
                    mm(dst[:, :], w[m][:, :], mixed[m][:, :, :].rearrange("p b t -> p (b t)"),
                       start=True, stop=True).then_inc(proj_done, 1)
                if not last:
                    transpose_x(c + 1)
                pe.wait_ge(rw_ready, c.count(1, 1))
                pe.wait_ge(x_ready, c.count(1))
                r = rw[c.par][:, :, :].rearrange("p b t -> p (b t)")
                for a in range(TPC):
                    done = mm(y_bank[:, a * P:(a + 1) * P], r[:, a * P:(a + 1) * P], w["o"][:, :], start=True, stop=True)
                done.then_inc(out_done, 1)

            pe.wait_ge(w_loaded, 160)
            transpose_x(At(0, 0))
            body(At(0, 0))
            for c in (1, 2):
                body(At(0, c))
            body(At(0, 3), last=True)

        @block.scalar
        def _(act):
            def copy_xT(c):
                act.wait_ge(tx_done, c.count(1, 1))
                nc.scalar.copy(xT[c.par][:, :, 1:T + 1], xt_bank[:, :].rearrange("p (b t) -> p b t", b=NB)).then_inc(xT_ready, 1)

            def exp(c, dst, src, scale=1.0):
                nc.scalar.activation(dst[:, :, :], src[:, :, :], ACT.Exp, scale=scale).then_inc(e_ready, 1)

            def body(c, last=False):
                view = lambda b: b[:, :].rearrange("p (b t) -> p b t", b=NB)
                act.wait_ge(proj_done, c.count(3, 2))
                act.wait_ge(rw_ready, c.count(1))
                nc.scalar.copy(V[:, :, :], view(v_bank)).then_inc(v_copied, 1)
                for n, (dst, src) in enumerate((("e1b", "g1"), ("e2b", "g2"), ("e1", "d1"), ("e2", "d2"))):
                    act.wait_ge(d_ready, c.count(4, n + 1))
                    exp(c, e[dst], e[src])
                act.wait_ge(proj_done, c.count(3, 3))
                nc.scalar.activation(R[:, :, :], view(r_bank), ACT.Sigmoid).then_inc(er_ready, 1)
                if not last:
                    copy_xT(c + 1)

            act.wait_ge(w_loaded, 160)
            nc.scalar.activation(decay[:, 0:1], cols[:, 0:1], ACT.Exp).then_inc(decay_ready, 1)
            act.wait_ge(consts, 7)
            copy_xT(At(0, 0))
            body(At(0, 0))
            for c in (1, 2):
                body(At(0, c))
            body(At(0, 3), last=True)

        @block.vector
        def _(dve):
            v = nc.vector

            def mix(c, link):
                dve.wait_ge(xT_ready, c.count(1, 1))
                for n, m in enumerate(MIX):
                    link(v.tensor_scalar(scratch[:, :, :], xT[c.par][:, :, 0:T], keep[:, n:n + 1], None, ALU.mult))
                    v.scalar_tensor_tensor(mixed[m][:, :, :], xT[c.par][:, :, 1:T + 1], cols[:, 2 + n:3 + n],
                                           scratch[:, :, :], ALU.mult, ALU.add).then_inc(mixed_ready, 1)
                    dve.wait_ge(mixed_ready, c.count(3, n + 1))

            def body(c, link, last=False):
                mix(c, link)
                K = k_bank[:, :].rearrange("p (b t) -> p b t", b=NB)
                now, nxt = pp[:, :, 0:T], pp[:, :, 1:T + 1]
                dve.wait_ge(proj_done, c.count(3, 1))
                for b in range(NB):
                    link.done(v.tensor_tensor_scan(pp[:, b, 1:T + 1], decay[:, 1:2].to_broadcast([P, T]), K[:, b, :],
                                                   MIN_P, ALU.add, ALU.max))
                link.wait()
                v.scalar_tensor_tensor(e["g1"][:, :, :], now, decay[:, 1:2], nxt, ALU.add, ALU.subtract).then_inc(d_ready, 1)
                v.tensor_tensor(e["g2"][:, :, :], K, nxt, ALU.subtract).then_inc(d_ready, 1)
                link(v.scalar_tensor_tensor(e["t2"][:, :, :], K, cols[:, 1:2], now, ALU.add, ALU.subtract))
                v.tensor_scalar(e["d1"][:, :, :], e["t2"][:, :, :], -1.0, 0.0, ALU.mult, ALU.min).then_inc(d_ready, 1)
                v.tensor_scalar(e["d2"][:, :, :], e["t2"][:, :, :], 0.0, None, ALU.min).then_inc(d_ready, 1)
                dve.wait_ge(d_ready, c.count(4, 4))
                dve.wait_ge(e_ready, c.count(4, 2))
                dve.wait_ge(v_copied, c.count(1, 1))
                link(v.tensor_tensor(e["ev"][:, :, :], e["e2b"][:, :, :], V[:, :, :], ALU.mult))
                for src, dst in (("ev", aa), ("e2b", bb)):
                    for b in range(NB):
                        done = v.tensor_tensor_scan(dst[:, b, 1:T + 1], e["e1b"][:, b, :], e[src][:, b, :],
                                                    0.0, ALU.mult, ALU.add)
                        if b < NB - 1:
                            link.done(done)
                    done.then_inc(sums_ready, 1)
                if not last:
                    n = c + 1
                    layernorm_chunk(nc, dve, link, x_res, n.count(CW), ln, xn[n.par], xn_ready)
                dve.wait_ge(e_ready, c.count(4, 4))
                link(v.tensor_tensor(e["t2"][:, :, :], e["e2"][:, :, :], V[:, :, :], ALU.mult))
                dve.wait_ge(prods_ready, c.count(2, 1))
                link(v.tensor_tensor(e["t2"][:, :, :], e["t2"][:, :, :], e["t1"][:, :, :], ALU.add))
                dve.wait_ge(prods_ready, c.count(2, 2))
                link(v.tensor_tensor(e["den"][:, :, :], e["t3"][:, :, :], e["e2"][:, :, :], ALU.add))
                link(v.reciprocal(e["den"][:, :, :], e["den"][:, :, :]))
                link(v.tensor_tensor(e["t2"][:, :, :], e["t2"][:, :, :], e["den"][:, :, :], ALU.mult))
                dve.wait_ge(er_ready, c.count(1, 1))
                v.tensor_tensor(rw[c.par][:, :, :], e["t2"][:, :, :], R[:, :, :], ALU.mult).then_inc(rw_ready, 1)
                dve.wait_ge(out_done, c.count(1, 1))
                x = x_res[:, bass.ds(c.count(CW), CW)]
                v.tensor_tensor(x, x, y_bank[:, :], ALU.add).then_inc(x_ready, 1)

            PER = 3 + NB + 1 + 1 + 2 * (NB - 1) + LN_CHAIN + 5
            dve.wait_ge(consts, 7)
            link = Chain(dve, chain[0])
            layernorm_chunk(nc, dve, link, x_res, 0, ln, xn[0], xn_ready)
            body(At(0, 0), link)
            link = Chain(dve, chain[1])
            for c in (1, 2):
                body(At(0, c), link)
            body(At(0, 3), Chain(dve, chain[2]), last=True)


EXPERTS, EXPERT_HIDDEN, CAPACITY = 8, 512, 320
SLOTS = EXPERTS * CAPACITY
KB = EXPERT_HIDDEN // P
SLOT_TILES = ((0, 128), (128, 128), (256, 64))
FAR = 1e6


def moe_consts(np):
    return {
        "iota": np.tile(np.arange(EXPERTS, dtype=np.float32), (P, 1)),
        "tri": np.triu(np.ones((P, P), np.float32)),
    }


def moe_phase(nc, a, out, x_res, sem_of):
    with ExitStack() as ctx:
        def sb(name, shape, dt=F32):
            return ctx.enter_context(nc.sbuf_tensor("mo_" + name, shape, dt))

        def bank(name):
            return ctx.enter_context(nc.psum_tensor("mo_" + name, [P, 512], F32))

        sem = sem_of("mo")
        slots = nc.dram_tensor("mo_slots", [SLOTS, P], F32).ap()
        answers = nc.dram_tensor("mo_answers", [SLOTS, P], F32).ap()
        N = TILES * EXPERTS
        ident, tri32 = sb("ident", [P, P]), sb("tri32", [P, P])
        tri, ones = sb("tri", [P, P], BF16), sb("ones", [P, P], BF16)
        iota, far_iota = sb("iota", [P, EXPERTS]), sb("far_iota", [P, EXPERTS])
        zero = sb("zero", [P, SLOTS // P * P])
        rw, rb = sb("rw", [P, EXPERTS]), sb("rb", [P, EXPERTS])
        b1_rows, b1 = sb("b1_rows", [EXPERTS * KB, P]), sb("b1", [P, EXPERTS * KB])
        b2 = sb("b2", [P, EXPERTS * P])
        ln = ln_tiles(sb)
        xn = sb("xn", [P, TILES, P])
        xT = [sb(f"xT{i}", [P, CW]) for i in range(2)]
        wide = lambda n, dt=F32: sb(n, [P, TILES, EXPERTS], dt)
        gates, eq, cand, masked, prod, pos, total, before = (
            wide(n) for n in ("gates", "eq", "cand", "masked", "prod", "pos", "total", "before"))
        zeros = wide("zeros")
        mask = wide("mask", BF16)
        hot = [wide(f"hot{k}") for k in range(2)]
        per_token = lambda n, dt=F32: sb(n, [P, TILES], dt)
        top, denom = per_token("top"), per_token("denom")
        gate, expert, place, valid, weight, tmp = (
            [per_token(f"{n}{k}") for k in range(2)] for n in ("gate", "expert", "place", "valid", "weight", "tmp"))
        put = [per_token(f"put{k}", U32) for k in range(2)]
        get = [per_token(f"get{k}", U32) for k in range(2)]
        w1 = [sb(f"w1_{i}", [P, EXPERT_HIDDEN]) for i in range(2)]
        w2 = [sb(f"w2_{i}", [P, KB, P]) for i in range(2)]
        xe = [sb(f"xe{i}", [P, 3, P]) for i in range(2)]
        xeT = [sb(f"xeT{i}", [P, CAPACITY]) for i in range(2)]
        hT = [sb(f"hT{i}", [P, KB, CAPACITY]) for i in range(2)]
        ye = [sb(f"ye{i}", [P, 3, P]) for i in range(2)]
        got = sb("got", [P, 2, TILES, P])
        xt_bank, route_bank = bank("xt"), bank("route")
        h_bank = [bank(f"h{k}") for k in range(KB)]
        y_bank = [bank(f"y{i}") for i in range(2)]

        consts_loaded, consts_ready, zeroed = sem("consts_loaded"), sem("consts_ready"), sem("zeroed")
        xn_ready, tx_done, xT_ready, logits_done = sem("xn_ready"), sem("tx_done"), sem("xT_ready"), sem("logits_done")
        shifted, exp_ready, mask_ready, counts_done, counts_read = (
            sem("shifted"), sem("exp_ready"), sem("mask_ready"), sem("counts_done"), sem("counts_read"))
        b1_done, b1_ready = sem("b1_done"), sem("b1_ready")
        routed, scattered, gathered = sem("routed"), sem("scattered"), [sem(f"gathered{t}") for t in range(TILES)]
        w_loaded = [sem(f"w_loaded{i}") for i in range(2)]
        xe_loaded = [sem(f"xe_loaded{i}") for i in range(2)]
        te_done, xeT_ready, up_done, gelu_ready, down_done, ye_ready = (
            sem("te_done"), sem("xeT_ready"), sem("up_done"), sem("gelu_ready"), sem("down_done"), sem("ye_ready"))
        ye_out = [sem(f"ye_out{i}") for i in range(2)]
        y_ready, stored = sem("y_ready"), sem("stored")
        chain = sem("chain")
        CONSTS = 16 * 7
        block = ctx.enter_context(nc.Block())
        out_tiles = out.rearrange("(a p) d -> p a d", p=P)

        @block.sync
        def _(sp):
            for dst, src in ((ident[:, :], a["c_ident"]), (tri32[:, :], a["tri"]), (iota[:, :], a["iota"]),
                             (rw[:, :], a["router_w"]), (rb[:, :], a["router_b"].partition_broadcast(P)),
                             (b1_rows[:, :], a["b1"].rearrange("e (k p) -> (e k) p", p=P)),
                             (b2[:, :], a["b2"].rearrange("e d -> (e d)").partition_broadcast(P))):
                sp.dma_start(dst, src).then_inc(consts_loaded, 16)
            sp.wait_ge(consts_ready, 1)
            sp.dma_start(slots.rearrange("(p a) d -> p (a d)", p=P), zero[:, :]).then_inc(zeroed, 16)

            def load_w(e):
                sp.dma_start(w1[e.par][:, :], a["w1"][bass.ds(e.count(1), 1), :, :].rearrange("e p h -> (e p) h")).then_inc(w_loaded[e.par], 16)
                sp.dma_start(w2[e.par][:, :, :], a["w2"][bass.ds(e.count(1), 1), :, :].rearrange("e (k p) d -> p (e k) d", p=P)).then_inc(w_loaded[e.par], 16)

            def load_x(e):
                at = e.count(CAPACITY)
                sp.dma_start(xe[e.par][:, 0:2, :], slots[bass.ds(at, 256), :].rearrange("(a p) d -> p a d", p=P)).then_inc(xe_loaded[e.par], 16)
                sp.dma_start(xe[e.par][0:64, 2, :], slots[bass.ds(at + 256, 64), :]).then_inc(xe_loaded[e.par], 16)

            def store_y(e):
                at = e.count(CAPACITY)
                sp.wait_ge(ye_ready, e.count(1, 1))
                sp.dma_start(answers[bass.ds(at, 256), :].rearrange("(a p) d -> p a d", p=P), ye[e.par][:, 0:2, :]).then_inc(ye_out[e.par], 16)
                sp.dma_start(answers[bass.ds(at + 256, 64), :], ye[e.par][0:64, 2, :]).then_inc(ye_out[e.par], 16)

            def body(e, last=False):
                if not last:
                    sp.wait_ge(down_done, e.count(1))
                    load_w(e + 1)
                    load_x(e + 1)
                store_y(e)

            load_w(At(0, 0))
            sp.wait_ge(scattered, 16 * 2 * TILES)
            load_x(At(0, 0))
            body(At(0, 0))
            body(At(0, 1))
            with sp.Fori(0, 2) as i:
                for c in (2, 3):
                    body(At(i, c))
            body(At(0, 6))
            body(At(0, 7), last=True)
            for c in range(CHUNKS):
                sp.wait_ge(y_ready, c + 1)
                sp.dma_start(out_tiles[:, c * TPC:(c + 1) * TPC, :],
                             x_res[:, c * CW:(c + 1) * CW].rearrange("p (a d) -> p a d", a=TPC)).then_inc(stored, 16)
            sp.wait_ge(stored, 16 * CHUNKS)

        @block.gpsimd
        def _(pool):
            g = nc.gpsimd
            g.memset(zero[:, :], 0.0).then_inc(consts_ready, 1)
            g.memset(ones[:, :], 1.0).then_inc(consts_ready, 1)
            g.memset(zeros[:, :, :], 0.0).then_inc(consts_ready, 1)
            pool.wait_ge(consts_loaded, CONSTS)
            g.tensor_copy(tri[:, :], tri32[:, :]).then_inc(consts_ready, 1)
            g.tensor_scalar(far_iota[:, :], iota[:, :], float(EXPERTS), None, ALU.add).then_inc(consts_ready, 1)
            pool.wait_ge(zeroed, 16)
            pool.wait_ge(routed, 1)
            for t in range(TILES):
                for k in range(2):
                    g.indirect_dma_start(slots, bass.IndirectOffsetOnAxis(put[k][:, t:t + 1], 0), xn[:, t, :], None,
                                         bounds_check=SLOTS - 1, oob_is_err=False).then_inc(scattered, 16)
            for i in range(2):
                pool.wait_ge(ye_out[i], 32 * (EXPERTS // 2))
            for t in range(TILES):
                for k in range(2):
                    g.indirect_dma_start(got[:, k, t, :], None, answers, bass.IndirectOffsetOnAxis(get[k][:, t:t + 1], 0),
                                         bounds_check=SLOTS - 1, oob_is_err=False).then_inc(gathered[t], 16)

        @block.tensor
        def _(pe):
            mm = nc.tensor.matmul
            pe.wait_ge(consts_loaded, CONSTS)
            for c in range(CHUNKS):
                pe.wait_ge(xn_ready, c + 1)
                pe.wait_ge(xT_ready, c)
                for n in range(TPC):
                    last = nc.tensor.transpose(xt_bank[:, n * P:(n + 1) * P], xn[:, c * TPC + n, :], ident[:, :])
                last.then_inc(tx_done, 1)
                pe.wait_ge(xT_ready, c + 1)
                for n in range(TPC):
                    t = c * TPC + n
                    last = mm(route_bank[:, t * EXPERTS:(t + 1) * EXPERTS], xT[c % 2][:, n * P:(n + 1) * P], rw[:, :],
                              start=True, stop=True)
            last.then_inc(logits_done, 1)
            nc.tensor.transpose(h_bank[0][:, 0:EXPERTS * KB], b1_rows[:, :], ident[0:EXPERTS * KB, 0:EXPERTS * KB]).then_inc(b1_done, 1)
            pe.wait_ge(mask_ready, 1)
            pe.wait_ge(consts_ready, 5)
            flat = mask[:, :, :].rearrange("p t e -> p (t e)")
            mm(route_bank[:, 128:128 + N], tri[:, :], flat, start=True, stop=True)
            mm(route_bank[:, 256:256 + N], ones[:, :], flat, start=True, stop=True).then_inc(counts_done, 1)

            def transpose_e(e):
                pe.wait_ge(xe_loaded[e.par], e.half(32, 32))
                pe.wait_ge(xeT_ready, e.count(1))
                for n, (at, rows) in enumerate(SLOT_TILES):
                    last = nc.tensor.transpose(xt_bank[:, at:at + rows], xe[e.par][0:rows, n, :], ident[0:rows, 0:rows])
                last.then_inc(te_done, 1)

            def body(e, first=False, last=False):
                pe.wait_ge(xeT_ready, e.count(1, 1))
                pe.wait_ge(w_loaded[e.par], e.half(32, 32))
                for k in range(KB):
                    if not first:
                        pe.wait_ge(gelu_ready, e.count(KB, k - KB + 1))
                    mm(h_bank[k][:, 0:CAPACITY], w1[e.par][:, k * P:(k + 1) * P], xeT[e.par][:, :],
                       start=True, stop=True).then_inc(up_done, 1)
                if not last:
                    transpose_e(e + 1)
                if not first:
                    pe.wait_ge(ye_ready, e.count(1, -1))
                pe.wait_ge(gelu_ready, e.count(KB, KB))
                for n, (at, rows) in enumerate(SLOT_TILES):
                    for k in range(KB):
                        done = mm(y_bank[e.par][0:rows, n * P:(n + 1) * P], hT[e.par][:, k, at:at + rows], w2[e.par][:, k, :],
                                  start=k == 0, stop=k == KB - 1)
                done.then_inc(down_done, 1)

            pe.wait_ge(b1_ready, 1)
            transpose_e(At(0, 0))
            body(At(0, 0), first=True)
            body(At(0, 1))
            with pe.Fori(0, 2) as i:
                for c in (2, 3):
                    body(At(i, c))
            body(At(0, 6))
            body(At(0, 7), last=True)

        @block.scalar
        def _(act):
            for c in range(CHUNKS):
                act.wait_ge(tx_done, c + 1)
                nc.scalar.copy(xT[c % 2][:, :], xt_bank[:, :]).then_inc(xT_ready, 1)
            act.wait_ge(b1_done, 1)
            nc.scalar.copy(b1[:, :], h_bank[0][:, 0:EXPERTS * KB]).then_inc(b1_ready, 1)
            act.wait_ge(b1_ready, 1)
            act.wait_ge(shifted, 1)
            nc.scalar.activation(gates[:, :, :], gates[:, :, :], ACT.Exp).then_inc(exp_ready, 1)

            def copy_xeT(e):
                act.wait_ge(te_done, e.count(1, 1))
                nc.scalar.copy(xeT[e.par][:, :], xt_bank[:, 0:CAPACITY]).then_inc(xeT_ready, 1)

            def body(e, last=False):
                for k in range(KB):
                    act.wait_ge(up_done, e.count(KB, k + 1))
                    nc.scalar.activation(hT[e.par][:, k, :], h_bank[k][:, 0:CAPACITY], ACT.Gelu,
                                         bias=b1[:, bass.ds(e.count(KB, k), 1)]).then_inc(gelu_ready, 1)
                if not last:
                    copy_xeT(e + 1)

            copy_xeT(At(0, 0))
            body(At(0, 0))
            body(At(0, 1))
            with act.Fori(0, 2) as i:
                for c in (2, 3):
                    body(At(i, c))
            body(At(0, 6))
            body(At(0, 7), last=True)

        @block.vector
        def _(dve):
            v = nc.vector
            link = Chain(dve, chain)
            for c in range(CHUNKS):
                layernorm_chunk(nc, dve, link, x_res, c * CW, ln, xn[:, c * TPC:(c + 1) * TPC, :], xn_ready)
            dve.wait_ge(logits_done, 1)
            shape = [P, TILES, EXPERTS]
            each = lambda t: t[:, :].unsqueeze(1).to_broadcast(shape)
            every = lambda t: t[:, :].unsqueeze(2).to_broadcast(shape)
            full = lambda t: t[:, :, :]
            tt = v.tensor_tensor
            link(tt(full(gates), route_bank[:, 0:N].rearrange("p (t e) -> p t e", e=EXPERTS), each(rb), ALU.add))
            link(v.reduce_max(top[:, :], full(gates), AX.X))
            tt(full(gates), full(gates), every(top), ALU.subtract).then_inc(shifted, 1)
            dve.wait_ge(exp_ready, 1)
            link(v.reduce_sum(denom[:, :], full(gates), AX.X))
            link(v.reciprocal(denom[:, :], denom[:, :]))
            link(tt(full(gates), full(gates), every(denom), ALU.mult))
            dve.wait_ge(consts_ready, 5)
            source = gates
            for k in range(2):
                link(v.reduce_max(gate[k][:, :], full(source), AX.X))
                link(tt(full(eq), full(source), every(gate[k]), ALU.is_equal))
                link(v.scalar_tensor_tensor(full(cand), full(eq), -float(EXPERTS), each(far_iota), ALU.mult, ALU.add))
                link(v.tensor_reduce(expert[k][:, :], full(cand), AX.X, ALU.min))
                link(tt(full(hot[k]), each(iota), every(expert[k]), ALU.is_equal))
                if k == 0:
                    link(v.scalar_tensor_tensor(full(masked), full(hot[0]), -2.0, full(gates), ALU.mult, ALU.add))
                    source = masked
            tt(full(mask), full(hot[0]), full(hot[1]), ALU.add).then_inc(mask_ready, 1)
            dve.wait_ge(counts_done, 1)
            view = lambda n: route_bank[:, n:n + N].rearrange("p (t e) -> p t e", e=EXPERTS)
            link(v.tensor_copy(full(total), view(256)))
            for e in range(EXPERTS):
                link.done(v.tensor_tensor_scan(before[:, :, e], total[:, :, e], zeros[:, :, e], 0.0, ALU.add, ALU.add))
            link.wait()
            link(tt(full(before), full(before), full(total), ALU.subtract))
            link(tt(full(pos), view(128), full(before), ALU.add))
            for k in range(2):
                link(tt(full(prod), full(hot[k]), full(pos), ALU.mult))
                link(v.reduce_sum(place[k][:, :], full(prod), AX.X))
                link(v.tensor_scalar(place[k][:, :], place[k][:, :], -1.0, None, ALU.add))
                link(v.tensor_scalar(valid[k][:, :], place[k][:, :], float(CAPACITY), None, ALU.is_lt))
                link(tt(weight[k][:, :], gate[k][:, :], valid[k][:, :], ALU.mult))
                link(v.scalar_tensor_tensor(tmp[0][:, :], expert[k][:, :], float(CAPACITY), place[k][:, :], ALU.mult, ALU.add))
                link(v.tensor_scalar(tmp[1][:, :], valid[k][:, :], -FAR, FAR, ALU.mult, ALU.add))
                link(tt(put[k][:, :], tmp[0][:, :], tmp[1][:, :], ALU.add))
                link(v.tensor_scalar(place[k][:, :], place[k][:, :], float(CAPACITY - 1), None, ALU.min))
                link(v.scalar_tensor_tensor(get[k][:, :], expert[k][:, :], float(CAPACITY), place[k][:, :], ALU.mult, ALU.add))
            dve.sem_inc(routed, 1)

            def body(e):
                dve.wait_ge(down_done, e.count(1, 1))
                dve.wait_ge(ye_out[e.par], e.half(32))
                bias = b2[:, bass.ds(e.count(P), P)]
                for n, (_, rows) in enumerate(SLOT_TILES):
                    last = v.tensor_tensor(ye[e.par][0:rows, n, :], y_bank[e.par][0:rows, n * P:(n + 1) * P],
                                           bias[0:rows, :], ALU.add)
                last.then_inc(ye_ready, 1)

            for c in (0, 1):
                body(At(0, c))
            with dve.Fori(0, 3) as i:
                for c in (2, 3):
                    body(At(i, c))

            for t in range(TILES):
                dve.wait_ge(gathered[t], 32)
                x = x_res[:, t * P:(t + 1) * P]
                link(v.scalar_tensor_tensor(x, got[:, 0, t, :], weight[0][:, t:t + 1], x, ALU.mult, ALU.add))
                last = v.scalar_tensor_tensor(x, got[:, 1, t, :], weight[1][:, t:t + 1], x, ALU.mult, ALU.add)
                if t % TPC == TPC - 1:
                    last.then_inc(y_ready, 1)


def attention_consts(np):
    pair_ones = np.zeros((P, 2), np.float32)
    pair_ones[:DV, 0] = pair_ones[DV:, 1] = 1
    sel = np.zeros((3 * HEADS, PAIRS, P), np.float32)
    for part in range(3):
        for h in range(HEADS):
            at = DV * (h % 2)
            sel[part * HEADS + h, h // 2, at:at + DV] = 1
    head_ones = np.repeat(np.eye(P // DK, dtype=np.float32), DK, axis=0)
    return {"ident": np.eye(P, dtype=np.float32), "pair_ones": pair_ones, "head_ones": head_ones, "sel": sel}


def two_layer_program(nc, a, out):
    with ExitStack() as ctx:
        def sem_of(phase):
            return lambda name: ctx.enter_context(nc.semaphore(f"{phase}_{name}"))

        x_res = ctx.enter_context(nc.sbuf_tensor("x_res", [P, TILES * P], F32))
        parts = nc.dram_tensor("parts", [2, 3, 2 * HEADS * DK, T], BF16).ap()
        attention_phase(nc, a["L0_attn_tokens"], a["L0_attn_Wq"], a["L0_attn_Wkv"], a["L0_attn_Wout"],
                        a["ident"], a["pair_ones"], a["head_ones"], a["sel"], parts, x_res, sem_of)
        ffn_phase(nc, a["L0_ffn_w_gate"], a["L0_ffn_w_up"], a["L0_ffn_w_down"], a["ident"], x_res, sem_of)
        wkv_phase(nc, a["L1_attn_W"], a["L1_attn_U"], [a["L1_attn_time_mix_" + m] for m in "kvr"],
                  [a["L1_attn_W" + m] for m in "kvro"], a["ident"], x_res, sem_of)
        moe = {n: a["L1_ffn_" + n] for n in ("router_w", "router_b", "w1", "b1", "w2", "b2")}
        moe_phase(nc, {**moe, "c_ident": a["ident"], "iota": a["iota"], "tri": a["tri"]}, out, x_res, sem_of)


def kernel(**inputs):
    import numpy as np
    import concourse.bacc as bacc
    from concourse.bass_utils import run_bass_kernel_spmd

    arrays = {}
    for name, a in inputs.items():
        a = np.asarray(a)
        if name.startswith(("L0_ffn_w_", "L1_attn_W")) and a.ndim == 2:
            a = a.T
        elif name.startswith("L1_attn_"):
            a = a.reshape(P, 1)
        arrays[name] = np.ascontiguousarray(a)
    arrays.update(attention_consts(np))
    arrays.update(moe_consts(np))
    nc = bacc.Bacc("TRN2", target_bir_lowering=False, num_devices=1)
    args = {name: nc.dram_tensor("in_" + name, a.shape, mybir.dt.from_np(a.dtype), kind="ExternalInput").ap()
            for name, a in arrays.items()}
    out = nc.dram_tensor("out", [BATCH, T, P], F32, kind="ExternalOutput").ap()
    two_layer_program(nc, args, out.rearrange("b t d -> (b t) d"))
    return run_bass_kernel_spmd(nc, [{"in_" + name: a for name, a in arrays.items()}], core_ids=[0]).results[0]["out"]
```

```python
from contextlib import ExitStack

import concourse.bass as bass
from concourse import mybir

F32 = mybir.dt.float32
BF16 = mybir.dt.bfloat16
I32 = mybir.dt.int32
U32 = mybir.dt.uint32
ALU = mybir.AluOpType
ACT = mybir.ActivationFunctionType
AX = mybir.AxisListType

P = 128
BATCH, T = 8, 256
TOKENS = BATCH * T
TILES = TOKENS // P
TPB = T // P
LN_EPS = 1e-5

HEADS, DK, DV = 16, 16, 64
PAIRS = HEADS // 2
NORM_FLOOR = 1e-24
RSQRT_MAGIC = float(0x5F3759DF)

Q_PART = (0, 0, 1, 1, 0, 2)
K_PART = (0, 1, 0, 1, 2, 0)
COMBOS = len(Q_PART)


class At:

    def __init__(self, i, c):
        self.i, self.c, self.par = i, c, c % 2

    def __add__(self, n):
        return At(self.i, self.c + n)

    def count(self, per, k=0):
        n = self.c * per + k
        return max(n, 0) if isinstance(self.i, int) else self.i * (2 * per) + n

    def half(self, per, k=0):
        return self.i * per + (self.c // 2 * per + k)


class Chain:

    def __init__(self, eng, sem, base=0):
        self.eng, self.sem, self.base, self.n = eng, sem, base, 0

    def done(self, ins):
        ins.then_inc(self.sem, 1)
        self.n += 1
        return self

    def wait(self):
        self.eng.wait_ge(self.sem, self.base + self.n)

    def __call__(self, ins):
        self.done(ins)
        self.wait()


def rsqrt_guess(nc, link, yi, xi):
    link(nc.vector.tensor_scalar(yi, xi, 1, None, ALU.arith_shift_right))
    link(nc.vector.tensor_scalar(yi, yi, -1.0, RSQRT_MAGIC, ALU.mult, ALU.add))


def rsqrt_step(nc, link, y, x, a):
    link(nc.vector.scalar_tensor_tensor(a, y, -0.5, y, ALU.mult, ALU.mult))
    link(nc.vector.tensor_tensor(a, a, x, ALU.mult))
    link(nc.vector.scalar_tensor_tensor(y, a, 1.5, y, ALU.add, ALU.mult))


def rsqrt(nc, link, y, x, a, yi, xi):
    rsqrt_guess(nc, link, yi, xi)
    for _ in range(3):
        rsqrt_step(nc, link, y, x, a)


def attention_phase(nc, x_in, Wq, Wkv, Wout, ident_in, pick_in, sel_in, parts, x_res, sem_of, load_next, prepare_next, ln_next):
    with ExitStack() as ctx:
        def sb(name, shape, dt=F32):
            return ctx.enter_context(nc.sbuf_tensor("at_" + name, shape, dt))

        def bank(name):
            return ctx.enter_context(nc.psum_tensor("at_" + name, [P, 512], F32))

        sem = sem_of("at")
        QK, V, HQ = 2 * HEADS * DK, HEADS * DV, P // DK
        w_qk = sb("w_qk", [P, QK])
        w_v = sb("w_v", [P, V])
        w_out = sb("w_out", [P, PAIRS, P])
        ident = sb("ident", [P, P])
        pick = sb("pick", [P, 3, 32])
        squares = sb("squares", [P, T])
        sel_f32 = sb("sel_f32", [3 * HEADS, PAIRS, P])
        sel = sb("sel", [3 * HEADS, PAIRS, P], BF16)
        ident16 = sb("ident16", [P, P], BF16)
        f_parts = sb("f_parts", [P, TPB, P], BF16)
        f_rest = sb("f_rest", [P, TPB, HEADS])
        fT = sb("fT", [3 * HEADS, T], BF16)
        stats = sb("stats", [P, TILES, 6])
        mv = sb("mv", [P, TILES, 2])
        rstd = sb("rstd", [P, TILES])
        ln_var = sb("ln_var", [P, TILES])
        xn = sb("xn", [P, TPB, P])
        xnT = [sb(f"xnT{i}", [P, T]) for i in range(2)]
        v_raw = [sb(f"v_raw{i}", [P, TPB, V]) for i in range(2)]
        sq_v = sb("sq_v", [P, TPB, V])
        sq_qk = sb("sq_qk", [P, 4, T])
        sums = [sb(f"sums{i}", [P, 96]) for i in range(2)]
        y, a = sb("nr_y", [P, 96]), sb("nr_a", [P, 96])
        fx, fy, fa, fn, th, inv_n = (sb("f_" + n, [P, 32]) for n in ("x", "y", "a", "n", "th", "inv_n"))
        f = sb("f", [P, 32])
        r_qk = [sb(f"r_qk{i}", [P, TPB, 2, HEADS]) for i in range(2)]
        key_factor = [sb(f"key_factor{i}", [P, TPB, HEADS]) for i in range(2)]
        part = [[sb(f"part{i}{j}", [P, 4, T], BF16) for j in range(3)] for i in range(2)]
        rest = sb("rest", [P, 4, T])
        q_stack = [sb(f"q_stack{i}", [COMBOS * DK, HEADS, T], BF16) for i in range(2)]
        k_stack = [sb(f"k_stack{i}", [COMBOS * DK, HEADS, T], BF16) for i in range(2)]
        attn = [sb(f"attn{i}", [P, TPB, T]) for i in range(8)]
        ob = [sb(f"ob{i}", [P, PAIRS, T]) for i in range(2)]
        osq = [sb(f"osq{i}", [P, PAIRS, T]) for i in range(2)]

        sim = [bank(f"sim{i}") for i in range(4)]
        av = [bank(f"av{i}") for i in range(2)]
        misc = even, odd = [bank(f"misc{i}") for i in range(2)]

        x_loaded = [sem(f"x_loaded{i}") for i in range(4)]
        w_loaded, consts_ready = sem("w_loaded"), sem("consts_ready")
        xn_ready, tx_done, xT_ready = sem("xn_ready"), sem("tx_done"), sem("xT_ready")
        qk_done, sq_ready = sem("qk_done"), sem("sq_ready")
        p1_ready, rest_ready, p2_ready, p3_ready = (
            sem("p1_ready"), sem("rest_ready"), sem("p2_ready"), sem("p3_ready"))
        ns_done, ns_copied, nst_done, ns_read = sem("ns_done"), sem("ns_copied"), sem("nst_done"), sem("ns_read")
        v_done, v_ready = sem("v_done"), sem("v_ready")
        vsum_ready = sem("vsum_ready")
        v_odd_ready = sem("v_odd_ready")
        key_factor_ready = sem("key_factor_ready")
        parts_out = [sem(f"parts_out{i}") for i in range(2)]
        stack_ready = [sem(f"stack_ready{i}") for i in range(2)]
        sim_done, relu_ready = sem("sim_done"), sem("relu_ready")
        attn_even, attn_odd = sem("attn_even"), sem("attn_odd")
        av_done, ob_ready, osq_ready = sem("av_done"), sem("ob_ready"), sem("osq_ready")
        n_ready, tanh_ready, f_ready = sem("n_ready"), sem("tanh_ready"), sem("f_ready")
        fT_done, fT_ready = sem("fT_done"), sem("fT_ready")
        bc_done, on_ready = sem("bc_done"), sem("on_ready")
        out_done, x1_ready = sem("out_done"), sem("x1_ready")
        chain_sems = [sem(f"dve_chain{i}") for i in range(5)]

        block = ctx.enter_context(nc.Block())
        x_tiles = x_in.rearrange("b t d -> (b t) d").rearrange("(a p) d -> p a d", p=P)
        xr = x_res[:, :].rearrange("p (a d) -> p a d", a=TILES)
        kv_view = Wkv.rearrange("p (h e) -> p h e", h=HEADS)
        Q4 = TILES // 4
        STACKED = 16 * 2 * COMBOS

        @block.sync
        def _(sp):
            for n in range(4):
                sp.dma_start(xr[:, n * Q4:(n + 1) * Q4, :], x_tiles[:, n * Q4:(n + 1) * Q4, :]).then_inc(x_loaded[n], 16)

            def stack(b):
                sp.wait_ge(p3_ready, b.count(2, 2))
                for j in range(3):
                    sp.dma_start(parts[b.par, j].rearrange("(a p) t -> p a t", p=P),
                                 part[b.par][j][:, :, :]).then_inc(parts_out[b.par], 16)
                sp.wait_ge(parts_out[b.par], b.half(48, 48))
                for c in range(COMBOS):
                    for s, tile, j in ((0, q_stack, Q_PART[c]), (1, k_stack, K_PART[c])):
                        src = parts[b.par, j, s * 256:(s + 1) * 256, :].rearrange("(h d) t -> d h t", d=DK)
                        sp.dma_start(tile[b.par][c * DK:(c + 1) * DK, :, :], src).then_inc(stack_ready[b.par], 16)

            stack(At(0, 0))
            stack(At(0, 1))
            load_next(sp)
            with sp.Fori(0, 3) as i:
                for c in (2, 3):
                    stack(At(i, c))

        @block.tensor
        def _(pe):
            mm = nc.tensor.matmul

            def transpose_x(b, bank):
                pe.wait_ge(xn_ready, b.count(1, 1))
                for t in range(TPB):
                    last = nc.tensor.transpose(bank[:, t * P:(t + 1) * P], xn[:, t, :], ident[:, :])
                last.then_inc(tx_done, 1)

            def project_qk(b, s, bank):
                pe.wait_ge(xT_ready, b.count(1, 1))
                for g in range(2):
                    at = s * 256 + g * P
                    last = mm(bank[:, g * T:(g + 1) * T], w_qk[:, at:at + P], xnT[b.par][:, :], start=True, stop=True)
                last.then_inc(qk_done, 1)

            def project_v(b, j, bank):
                pe.wait_ge(xT_ready, b.count(1, 1))
                t, half = j // 2, j % 2
                mm(bank[:, :], xnT[b.par][:, t * P:(t + 1) * P], w_v[:, half * 512:(half + 1) * 512],
                   start=True, stop=True).then_inc(v_done, 1)

            def norms(b, bank, old=True, v=True):
                if v:
                    pe.wait_ge(sq_ready, b.count(2, 4))
                if old:
                    pe.wait_ge(osq_ready, b.count(8))
                turns = (0, 1, 2) if old and v else (0, 1) if old else (2,)
                for u in turns:
                    for g in range(4):
                        x = sq_qk[:, g, :] if u == 2 else osq[(b + 1).par][:, 2 * g + u, :]
                        last = mm(bank[32 * g:32 * (g + 1), 0:T], pick[:, u, :], x, start=u == turns[0], stop=u == turns[-1])
                last.then_inc(ns_done, 1)

            def transpose_norms(b, bank):
                pe.wait_ge(ns_copied, b.count(1, 2))
                for t in range(TPB):
                    last = nc.tensor.transpose(bank[:, T + t * P:T + (t + 1) * P], squares[:, t * P:(t + 1) * P], ident[:, :])
                last.then_inc(nst_done, 1)

            def scores(b, s):
                if s == 0:
                    pe.wait_ge(stack_ready[b.par], b.half(STACKED, STACKED))
                for e in range(2):
                    h = 2 * s + e
                    pe.wait_ge(relu_ready, b.count(16, h - 3))
                    for j in range(TPB):
                        last = mm(sim[h % 4][:, j * T:(j + 1) * T], k_stack[b.par][:, h, j * P:(j + 1) * P],
                                  q_stack[b.par][:, h, :], start=True, stop=True)
                    last.then_inc(sim_done, 1)

            def values(b, s):
                pe.wait_ge(attn_even, b.count(8, s + 1))
                pe.wait_ge(attn_odd, b.count(8, s + 1))
                if s in (0, 4):
                    pe.wait_ge(v_odd_ready, b.count(2, s // 4 + 1))
                pe.wait_ge(ob_ready, b.count(8, s - 1))
                for j in range(TPB):
                    for e in range(2):
                        h = 2 * s + e
                        last = mm(av[s % 2][e * DV:(e + 1) * DV, 0:T], v_raw[b.par][:, j, h * DV:(h + 1) * DV],
                                  attn[h % 8][:, j, :], start=j == 0, stop=j == TPB - 1)
                last.then_inc(av_done, 1)

            def transpose_factors(b, bank):
                pe.wait_ge(f_ready, b.count(1, 1))
                for t in range(TPB):
                    last = nc.tensor.transpose(bank[:, :].bitcast(BF16)[:, t * P:(t + 1) * P], f_parts[:, t, :], ident16[:, :])
                last.then_inc(fT_done, 1)

            def spread(b, j, bank):
                pe.wait_ge(fT_ready, b.count(1, 1))
                for e in range(2):
                    last = mm(bank[:, e * T:(e + 1) * T], sel[:, 2 * j + e, :], fT[:, :], start=True, stop=True)
                last.then_inc(bc_done, 1)

            def output(b, bank):
                pe.wait_ge(on_ready, b.count(4, 4))
                for t in range(TPB):
                    for s in range(PAIRS):
                        last = mm(bank[:, t * P:(t + 1) * P], ob[b.par][:, s, t * P:(t + 1) * P], w_out[:, s, :],
                                  start=s == 0, stop=s == PAIRS - 1)
                last.then_inc(out_done, 1)

            def body(b, qk=True, v=True, old=True, older=True):
                for s in range(PAIRS):
                    if s < PAIRS - 2:
                        scores(b, s + 2)
                    elif v:
                        scores(b + 1, s + 2 - PAIRS)
                    if s:
                        values(b, s - 1)
                    elif old:
                        values(b + -1, PAIRS - 1)
                    if s == 0 and older:
                        pe.wait_ge(on_ready, b.count(4, -8 + 1))
                        spread(b + -2, 2, even)
                        pe.wait_ge(on_ready, b.count(4, -8 + 2))
                        spread(b + -2, 3, odd)
                    if s == 1:
                        if v:
                            if older:
                                pe.wait_ge(on_ready, b.count(4, -8 + 3))
                            project_v(b + 1, 0, even)
                        if older:
                            output(b + -2, odd)
                    if s == 2:
                        if older:
                            pe.wait_ge(x1_ready, b.count(1, -1))
                        norms(b, odd, old, v)
                        if v:
                            pe.wait_ge(v_ready, b.count(4, 4 + 1))
                            project_v(b + 1, 1, even)
                    if s == 3:
                        transpose_norms(b, odd)
                        if v:
                            pe.wait_ge(v_ready, b.count(4, 4 + 2))
                            project_v(b + 1, 2, even)
                    if s == 4:
                        if qk:
                            pe.wait_ge(v_ready, b.count(4, 4 + 3))
                            transpose_x(b + 2, even)
                        if v:
                            pe.wait_ge(ns_read, b.count(1, 2))
                            project_v(b + 1, 3, odd)
                    if s == 5 and qk:
                        project_qk(b + 2, 0, even)
                        pe.wait_ge(v_ready, b.count(4, 4 + 4))
                        project_qk(b + 2, 1, odd)
                    if s == 6 and old:
                        if qk:
                            pe.wait_ge(sq_ready, b.count(2, 4 + 1))
                            pe.wait_ge(rest_ready, b.count(2, 4 + 1))
                        elif v:
                            pe.wait_ge(v_ready, b.count(4, 4 + 3))
                        else:
                            pe.wait_ge(on_ready, b.count(4, -8 + 3))
                        transpose_factors(b + -1, even)
                    if s == 7 and old:
                        pe.wait_ge(fT_ready, b.count(1))
                        spread(b + -1, 0, even)
                        if qk:
                            pe.wait_ge(rest_ready, b.count(2, 4 + 2))
                        elif v:
                            pe.wait_ge(v_ready, b.count(4, 4 + 4))
                        else:
                            pe.wait_ge(ns_read, b.count(1, 2))
                        spread(b + -1, 1, odd)

            def tail(b):
                values(b, PAIRS - 1)
                for j in (2, 3):
                    pe.wait_ge(on_ready, b.count(4, -4 + j - 1))
                    spread(b + -1, j, misc[j % 2])
                output(b + -1, odd)
                norms(b + 1, even, True, False)
                transpose_norms(b + 1, even)
                pe.wait_ge(x1_ready, b.count(1))
                transpose_factors(b, odd)
                pe.wait_ge(ns_read, b.count(1, 3))
                spread(b, 0, even)
                spread(b, 1, odd)
                for j in (2, 3):
                    pe.wait_ge(on_ready, b.count(4, j - 1))
                    spread(b, j, misc[j % 2])
                output(b, odd)

            def first_qk(b):
                transpose_x(b, even)
                pe.wait_ge(xT_ready, b.count(1, 1))
                project_qk(b, 0, even)
                project_qk(b, 1, odd)

            pe.wait_ge(w_loaded, 16 * 7)
            b0, b1 = At(0, 0), At(0, 1)
            first_qk(b0)
            pe.wait_ge(rest_ready, 1)
            norms(At(0, -1), even, False, True)
            pe.wait_ge(rest_ready, 2)
            project_v(b0, 0, odd)
            transpose_norms(At(0, -1), even)
            pe.wait_ge(v_ready, 1)
            project_v(b0, 1, odd)
            pe.wait_ge(ns_read, 1)
            project_v(b0, 2, even)
            pe.wait_ge(v_ready, 2)
            project_v(b0, 3, odd)
            pe.wait_ge(v_ready, 4)
            first_qk(b1)
            scores(b0, 0)
            scores(b0, 1)
            pe.wait_ge(rest_ready, 4)
            body(b0, old=False, older=False)
            pe.wait_ge(consts_ready, 3)
            body(b1, older=False)
            with pe.Fori(0, 2) as i:
                for c in (2, 3):
                    body(At(i, c))
            body(At(0, 6), qk=False)
            body(At(0, 7), qk=False, v=False)
            tail(At(0, 7))

        @block.scalar
        def _(act):
            def w_load(dst, src):
                act.dma_start(dst, src).then_inc(w_loaded, 16)

            w_load(ident[:, :], ident_in)
            w_load(w_qk[:, 0:256], Wq)
            w_load(w_qk[:, 256:512].rearrange("p (h d) -> p h d", h=HEADS), kv_view[:, :, 0:DK])
            w_load(w_v[:, :].rearrange("p (h d) -> p h d", h=HEADS), kv_view[:, :, DK:DK + DV])
            w_load(w_out[:, :, :], Wout.rearrange("(s p) n -> p s n", p=P))
            w_load(pick[:, :, :], pick_in)
            w_load(sel_f32[:, :, :], sel_in)

            def copy_xT(b, bank):
                act.wait_ge(tx_done, b.count(1, 1))
                act.wait_ge(v_done, b.count(4, -4))
                nc.scalar.copy(xnT[b.par][:, :], bank[:, 0:T]).then_inc(xT_ready, 1)

            def copy_v(b, j, bank):
                act.wait_ge(v_done, b.count(4, j + 1))
                act.wait_ge(av_done, b.count(8, -8))
                act.wait_ge(vsum_ready, b.count(2, j // 2 - 1))
                t, half = j // 2, slice(j % 2 * 512, (j % 2 + 1) * 512)
                nc.scalar.copy(v_raw[b.par][:, t, half], bank[:, :])
                nc.scalar.activation(sq_v[:, t, half], bank[:, :], ACT.Square).then_inc(v_ready, 1)

            def square_and_part1(b, s, bank):
                act.wait_ge(qk_done, b.count(2, s + 1))
                act.wait_ge(ns_done, b.count(1))
                at = slice(2 * s, 2 * s + 2)
                two = bank[:, :].rearrange("p (g t) -> p g t", g=2)
                nc.scalar.activation(sq_qk[:, at, :], two, ACT.Square).then_inc(sq_ready, 1)
                act.wait_ge(parts_out[b.par], b.half(48))
                nc.scalar.copy(part[b.par][0][:, at, :], two).then_inc(p1_ready, 1)

            def part2(b, s):
                at = slice(2 * s, 2 * s + 2)
                act.wait_ge(rest_ready, b.count(2, s + 1))
                nc.scalar.copy(part[b.par][1][:, at, :], rest[:, at, :]).then_inc(p2_ready, 1)

            def relu(b, s):
                act.wait_ge(av_done, b.count(8, s - 3))
                for h in (2 * s, 2 * s + 1):
                    act.wait_ge(sim_done, b.count(16, h + 1))
                    nc.scalar.activation(attn[h % 8][:, :, :].rearrange("p j t -> p (j t)"), sim[h % 4][:, :],
                                         ACT.Relu).then_inc(relu_ready, 1)

            def copy_ob(b, s):
                act.wait_ge(av_done, b.count(8, s + 1))
                if s == 0:
                    act.wait_ge(out_done, b.count(1, -1))
                nc.scalar.copy(ob[b.par][:, s, :], av[s % 2][:, 0:T]).then_inc(ob_ready, 1)

            def tanh(b):
                act.wait_ge(n_ready, b.count(1, 1))
                nc.scalar.activation(th[:, :], fn[:, :], ACT.Tanh).then_inc(tanh_ready, 1)

            def copy_norms(b, bank):
                act.wait_ge(ns_done, b.count(1, 2))
                act.wait_ge(nst_done, b.count(1, 1))
                nc.scalar.copy(squares[:, :], bank[:, 0:T]).then_inc(ns_copied, 1)

            def copy_fT(b, bank):
                act.wait_ge(fT_done, b.count(1, 1))
                act.wait_ge(bc_done, b.count(4))
                nc.scalar.copy(fT[:, :], bank[0:3 * HEADS, :].bitcast(BF16)[:, 0:T]).then_inc(fT_ready, 1)

            def body(b, qk=True, v=True, old=True):
                for s in range(PAIRS):
                    if s < PAIRS - 1:
                        relu(b, s + 1)
                    elif v:
                        relu(b + 1, 0)
                    if s > 1 and s != 6:
                        copy_ob(b, s - 2)
                    elif s < 2 and old:
                        copy_ob(b + -1, PAIRS + s - 2)
                    if s == 2:
                        copy_norms(b, odd)
                    if s in (1, 2, 3) and v:
                        copy_v(b + 1, s - 1, even)
                    if s == 4:
                        if qk:
                            copy_xT(b + 2, even)
                        if v:
                            copy_v(b + 1, 3, odd)
                    if s == 5:
                        if qk:
                            square_and_part1(b + 2, 0, even)
                            square_and_part1(b + 2, 1, odd)
                        if old:
                            tanh(b + -1)
                        copy_ob(b, 4)
                    if s == 6 and old:
                        copy_fT(b + -1, even)
                    if s == 7 and qk:
                        part2(b + 2, 0)
                        part2(b + 2, 1)

            b0, b1 = At(0, 0), At(0, 1)
            copy_xT(b0, misc[0])
            for s in range(2):
                square_and_part1(b0, s, misc[s])
            copy_norms(At(0, -1), even)
            part2(b0, 0)
            part2(b0, 1)
            for j, bank in enumerate((odd, odd, even, odd)):
                copy_v(b0, j, bank)
            copy_xT(b1, misc[0])
            for s in range(2):
                square_and_part1(b1, s, misc[s])
            relu(b0, 0)
            part2(b1, 0)
            part2(b1, 1)
            body(b0, old=False)
            body(b1)
            with act.Fori(0, 2) as i:
                for c in (2, 3):
                    body(At(i, c))
            body(At(0, 6), qk=False)
            body(At(0, 7), qk=False, v=False)
            copy_ob(At(0, 7), PAIRS - 2)
            copy_ob(At(0, 7), PAIRS - 1)
            copy_norms(At(0, 8), even)
            tanh(At(0, 7))
            copy_fT(At(0, 7), odd)

        @block.vector
        def _(dve):
            v = nc.vector

            def normalize_x(b):
                dve.wait_ge(tx_done, b.count(1))
                for t in range(TPB):
                    at = b.count(TPB, t)
                    last = v.tensor_scalar(xn[:, t, :], x_res[:, bass.ds(at * P, P)],
                                           mv[:, :, :].rearrange("p a c -> p (a c)")[:, bass.ds(at * 2, 1)],
                                           rstd[:, bass.ds(at, 1)], ALU.subtract, ALU.mult)
                last.then_inc(xn_ready, 1)

            def split_rest(b, s, bank):
                at = slice(2 * s, 2 * s + 2)
                dve.wait_ge(p1_ready, b.count(2, s + 1))
                dve.wait_ge(p3_ready, b.count(2))
                v.tensor_tensor(rest[:, at, :], bank[:, :].rearrange("p (g t) -> p g t", g=2),
                                part[b.par][0][:, at, :], ALU.subtract).then_inc(rest_ready, 1)

            def read_norms(b, bank, link, old=True, qk=True):
                dve.wait_ge(nst_done, b.count(1, 2))
                sums_in = bank[:, T:2 * T].rearrange("p (t g c) -> p t g c", t=TPB, g=4)
                n4 = fn[:, :].rearrange("p (t g c) -> p t g c", t=TPB, g=4)
                r4 = r_qk[(b + 1).par][:, :, 0, :].rearrange("p t (g c) -> p t g c", g=4)
                if old:
                    last = v.tensor_tensor(n4, sums_in[:, :, :, 0:4], r4, ALU.mult)
                if old and qk:
                    link.done(last)
                if qk:
                    to = sums[(b + 1).par][:, 0:64].rearrange("p (t g c) -> p t g c", t=TPB, g=4)
                    last = v.tensor_scalar(to, sums_in[:, :, :, 4:12], NORM_FLOOR, None, ALU.max)
                last.then_inc(ns_read, 1)
                dve.wait_ge(ns_read, b.count(1, 2))
                if old:
                    link.wait()
                    link(v.tensor_tensor(n4, n4, r4, ALU.mult))
                    link(v.tensor_scalar(fx[:, :], fn[:, :], NORM_FLOOR, None, ALU.max))
                    rsqrt_guess(nc, link, fy[:, :].bitcast(I32), fx[:, :].bitcast(I32))
                    rsqrt_step(nc, link, fy[:, :], fx[:, :], fa[:, :])

            def reduce_v(b, t):
                dve.wait_ge(v_ready, b.count(4, 2 * t + 2))
                at = 64 + t * HEADS
                v.reduce_sum(sums[b.par][:, at:at + HEADS], sq_v[:, t, :].rearrange("p (h d) -> p h d", d=DV),
                             AX.X).then_inc(vsum_ready, 1)

            def start_inverse_norms(b, link):
                dve.wait_ge(vsum_ready, b.count(2, 2))
                x = sums[b.par]
                link(v.tensor_scalar(x[:, 64:96], x[:, 64:96], NORM_FLOOR, None, ALU.max))
                rsqrt_guess(nc, link, y[:, :].bitcast(I32), x[:, :].bitcast(I32))
                rsqrt_step(nc, link, y[:, :], x[:, :], a[:, :])

            def end_inverse_norms(b, link):
                for _ in range(2):
                    rsqrt_step(nc, link, y[:, :], sums[b.par][:, :], a[:, :])
                flat = r_qk[b.par][:, :, :, :].rearrange("p t k h -> p (t k h)")
                link(v.tensor_tensor(flat, y[:, 0:64], y[:, 0:64], ALU.mult))

            def make_key_factor(b, link):
                v.tensor_tensor(key_factor[b.par][:, :, :], r_qk[b.par][:, :, 1, :],
                                y[:, 64:96].rearrange("p (t h) -> p t h", t=TPB), ALU.mult).then_inc(key_factor_ready, 1)
                dve.wait_ge(key_factor_ready, b.count(1, 1))

            def square(b, s):
                h = 2 * s
                dve.wait_ge(relu_ready, b.count(16, h + 1))
                for j in range(TPB):
                    r = attn[h % 8][:, j, :]
                    last = v.scalar_tensor_tensor(r, r, key_factor[b.par][:, j, h:h + 1], r, ALU.mult, ALU.mult)
                last.then_inc(attn_even, 1)

            def factors(b, link):
                for _ in range(2):
                    rsqrt_step(nc, link, fy[:, :], fx[:, :], fa[:, :])
                v.tensor_tensor(fn[:, :], fn[:, :], fy[:, :], ALU.mult).then_inc(n_ready, 1)
                link(v.tensor_tensor(inv_n[:, :].rearrange("p (t h) -> p t h", t=TPB),
                                     fy[:, :].rearrange("p (t h) -> p t h", t=TPB), r_qk[b.par][:, :, 0, :], ALU.mult))

            def f_part(c):
                return f_parts[:, :, c * HEADS:(c + 1) * HEADS]

            def tanh_factor(b, link):
                dve.wait_ge(tanh_ready, b.count(1, 1))
                dve.wait_ge(fT_done, b.count(1))
                f3 = f[:, :].rearrange("p (t h) -> p t h", t=TPB)
                link(v.tensor_tensor(f[:, :], th[:, :], inv_n[:, :], ALU.mult))
                link(v.tensor_copy(f_part(0), f3))
                link(v.tensor_tensor(f_rest[:, :, :], f3, f_part(0), ALU.subtract))
                link(v.tensor_copy(f_part(1), f_rest[:, :, :]))
                v.tensor_tensor(f_part(2), f_rest[:, :, :], f_part(1), ALU.subtract).then_inc(f_ready, 1)

            def scale_ob(b, j, bank):
                dve.wait_ge(bc_done, b.count(4, j + 1))
                o = ob[b.par][:, 2 * j:2 * j + 2, :]
                v.tensor_tensor(o, o, bank[:, :].rearrange("p (g t) -> p g t", g=2), ALU.mult).then_inc(on_ready, 1)

            def residual(b, bank):
                dve.wait_ge(out_done, b.count(1, 1))
                at = x_res[:, bass.ds(b.count(T), T)]
                v.tensor_tensor(at, at, bank[:, 0:T], ALU.add).then_inc(x1_ready, 1)

            def body(b, link, qk=True, v=True, old=True, older=True):
                for s in range(PAIRS):
                    if s == 0 and older:
                        scale_ob(b + -2, 1, odd)
                    if s < PAIRS - 1:
                        square(b, s + 1)
                    if s == 0 and older:
                        scale_ob(b + -2, 2, even)
                    if s == 1 and older:
                        scale_ob(b + -2, 3, odd)
                    if s == 2:
                        if older:
                            residual(b + -2, odd)
                        if qk:
                            normalize_x(b + 2)
                    if s == 3:
                        if v:
                            reduce_v(b + 1, 0)
                        read_norms(b, odd, link, old, v)
                    if s == 4 and old:
                        factors(b + -1, link)
                    if s == 5:
                        if v:
                            reduce_v(b + 1, 1)
                        if old:
                            tanh_factor(b + -1, link)
                        if qk:
                            split_rest(b + 2, 0, even)
                    if s == 6:
                        if v:
                            start_inverse_norms(b + 1, link)
                        if qk:
                            split_rest(b + 2, 1, odd)
                    if s == 7:
                        if v:
                            end_inverse_norms(b + 1, link)
                            make_key_factor(b + 1, link)
                        if old:
                            scale_ob(b + -1, 0, even)
                        if v:
                            square(b + 1, 0)

            def x_stats(first, end, link):
                for t in range(first, end):
                    if t % Q4 == 0:
                        dve.wait_ge(x_loaded[t // Q4], 16)
                    link.done(v.bn_stats(stats[:, t, :], xr[:, t, :]))
                link.wait()
                for t in range(first, end):
                    link.done(v.bn_aggr(mv[:, t, :], stats[:, t, :]))
                link.wait()
                var, r = ln_var[:, first:end], rstd[:, first:end]
                link(v.tensor_scalar(var, mv[:, first:end, 1], LN_EPS, None, ALU.add))
                rsqrt(nc, link, r, var, a[:, first:end], r.bitcast(I32), var.bitcast(I32))

            link = Chain(dve, chain_sems[0])
            b0, b1 = At(0, 0), At(0, 1)
            x_stats(0, Q4, link)
            normalize_x(b0)
            x_stats(Q4, TILES, link)
            dve.wait_ge(consts_ready, 1)
            split_rest(b0, 0, misc[0])
            split_rest(b0, 1, misc[1])
            read_norms(At(0, -1), even, link, old=False)
            normalize_x(b1)
            reduce_v(b0, 0)
            reduce_v(b0, 1)
            start_inverse_norms(b0, link)
            end_inverse_norms(b0, link)
            make_key_factor(b0, link)
            split_rest(b1, 0, misc[0])
            split_rest(b1, 1, misc[1])
            square(b0, 0)
            body(b0, Chain(dve, chain_sems[1]), old=False, older=False)
            body(b1, Chain(dve, chain_sems[2]), older=False)
            with dve.Fori(0, 2) as i:
                for c in (2, 3):
                    link = Chain(dve, chain_sems[3], i * (2 * CHAIN_PER_BODY) + (c - 2) * CHAIN_PER_BODY)
                    body(At(i, c), link)
                    assert link.n == CHAIN_PER_BODY, link.n
            link = Chain(dve, chain_sems[4])
            body(At(0, 6), link, qk=False)
            b7 = At(0, 7)
            body(b7, link, qk=False, v=False)
            for j in (1, 2, 3):
                scale_ob(At(0, 6), j, misc[j % 2])
            residual(At(0, 6), odd)
            read_norms(At(0, 8), even, link, qk=False)
            factors(b7, link)
            tanh_factor(b7, link)
            for j in range(4):
                scale_ob(b7, j, misc[j % 2])
            dve.wait_ge(x1_ready, BATCH - 1)
            layernorm_stats(nc, link, x_res, ln_next, 0, TILES - TPC)
            residual(b7, odd)

        @block.gpsimd
        def _(pool):
            g = nc.gpsimd
            pool.wait_ge(w_loaded, 16 * 7)
            g.memset(f_parts[:, :, :], 0.0).then_inc(consts_ready, 1)
            g.tensor_copy(ident16[:, :], ident[:, :]).then_inc(consts_ready, 1)
            g.tensor_copy(sel[:, :, :], sel_f32[:, :, :]).then_inc(consts_ready, 1)

            def scale_v(b, half):
                pool.wait_ge(key_factor_ready, b.count(1, 1))
                for t in range(TPB):
                    heads = v_raw[b.par][:, t, :].rearrange("p (s e d) -> p s e d", e=2, d=DV)[:, 4 * half:4 * half + 4, 1, :]
                    factor = key_factor[b.par][:, t, :].rearrange("p (s e) -> p s e", e=2)[:, 4 * half:4 * half + 4, 1]
                    last = g.tensor_tensor(heads, heads, factor.unsqueeze(2).to_broadcast([P, 4, DV]), ALU.mult)
                last.then_inc(v_odd_ready, 1)

            def part3(b, s):
                at = slice(2 * s, 2 * s + 2)
                pool.wait_ge(p2_ready, b.count(2, s + 1))
                g.tensor_tensor(part[b.par][2][:, at, :], rest[:, at, :], part[b.par][1][:, at, :],
                                ALU.subtract).then_inc(p3_ready, 1)

            def square(b, s):
                h = 2 * s + 1
                pool.wait_ge(relu_ready, b.count(16, h + 1))
                r = attn[h % 8][:, :, :]
                g.tensor_tensor(r, r, r, ALU.mult).then_inc(attn_odd, 1)

            def square_ob(b, s):
                pool.wait_ge(ob_ready, b.count(8, s + 1))
                o = ob[b.par][:, s, :]
                g.tensor_tensor(osq[b.par][:, s, :], o, o, ALU.mult).then_inc(osq_ready, 1)

            def body(b, qk=True, v=True, old=True):
                for s in range(PAIRS):
                    if s < PAIRS - 1:
                        square(b, s + 1)
                    elif v:
                        square(b + 1, 0)
                    if s == 4:
                        square_ob(b, 1)
                    if s > 1 and s != 3:
                        square_ob(b, s - 2)
                    elif s < 2 and old:
                        square_ob(b + -1, PAIRS + s - 2)
                    if s in (6, 7) and qk:
                        part3(b + 2, s - 6)
                if v:
                    scale_v(b + 1, 0)
                    scale_v(b + 1, 1)

            b0, b1 = At(0, 0), At(0, 1)
            part3(b0, 0)
            part3(b0, 1)
            scale_v(b0, 0)
            scale_v(b0, 1)
            square(b0, 0)
            part3(b1, 0)
            part3(b1, 1)
            body(b0, old=False)
            body(b1)
            with pool.Fori(0, 2) as i:
                for c in (2, 3):
                    body(At(i, c))
            body(At(0, 6), qk=False)
            body(At(0, 7), qk=False, v=False)
            prepare_next(pool, nc.gpsimd)
            square_ob(At(0, 7), PAIRS - 2)
            square_ob(At(0, 7), PAIRS - 1)


CHAIN_PER_BODY = (1 + 2 + 2 + 3) + (6 + 1) + 4 + (1 + 2 + 3) + (6 + 1)


CHUNKS = 4
TPC = TILES // CHUNKS
CW = TPC * P
HIDDEN = 384
HB = HIDDEN // P
INT_SCALE = 1.0 / 127.0


def layernorm_stats(nc, link, x_res, t, first, end):
    v = nc.vector
    for a in range(first, end):
        link.done(v.bn_stats(t["stats"][:, a, :], x_res[:, a * P:(a + 1) * P]))
    link.wait()
    for a in range(first, end):
        link.done(v.bn_aggr(t["mv"][:, a, :], t["stats"][:, a, :]))
    link.wait()
    var, rstd = t["var"][:, first:end], t["rstd"][:, first:end]
    link(v.tensor_scalar(var, t["mv"][:, first:end, 1], LN_EPS, None, ALU.add))
    rsqrt(nc, link, rstd, var, t["a"][:, first:end], rstd.bitcast(I32), var.bitcast(I32))


def normalize_chunk(nc, x_res, t, c, xn, ready):
    for a in range(TPC):
        n = c * TPC + a
        last = nc.vector.tensor_scalar(xn[:, a, 0:P], x_res[:, n * P:(n + 1) * P], t["mv"][:, n, 0:1],
                                       t["rstd"][:, n:n + 1], ALU.subtract, ALU.mult)
    last.then_inc(ready, 1)


def ln_tiles(sb):
    return {"stats": sb("ln_stats", [P, TILES, 6]), "mv": sb("ln_mv", [P, TILES, 2]), "var": sb("ln_var2", [P, TILES]),
            "rstd": sb("ln_rstd", [P, TILES]), "a": sb("ln_a", [P, TILES])}


class FfnInputs:

    def __init__(self, ctx, nc):
        self.w_int = ctx.enter_context(nc.sbuf_tensor("ff_w_int", [P, 3, HIDDEN], I32))
        self.w_gu = ctx.enter_context(nc.sbuf_tensor("ff_w_gu", [P, 2, HIDDEN], F32))
        self.w_dn = ctx.enter_context(nc.sbuf_tensor("ff_w_dn", [P, HB, P], F32))
        self.ident = ctx.enter_context(nc.sbuf_tensor("ff_ident", [P, P], F32))
        self.loaded, self.w_ready = (ctx.enter_context(nc.semaphore(n)) for n in ("ff_loaded", "ff_w_ready"))

    def load(self, sp, w_gate_t, w_up_t, w_down_t, ident_in):
        sp.dma_start(self.w_int[:, 0, :], w_gate_t).then_inc(self.loaded, 16)
        sp.dma_start(self.w_int[:, 1, :], w_up_t).then_inc(self.loaded, 16)
        sp.dma_start(self.w_int[:, 2, :].rearrange("p (k d) -> p k d", k=HB),
                     w_down_t.rearrange("(k p) d -> p k d", p=P)).then_inc(self.loaded, 16)
        sp.dma_start(self.ident[:, :], ident_in).then_inc(self.loaded, 16)

    def dequantise(self, pool, g):
        pool.wait_ge(self.loaded, 64)
        g.tensor_scalar(self.w_gu[:, :, :], self.w_int[:, 0:2, :], INT_SCALE, None, ALU.mult).then_inc(self.w_ready, 1)
        g.tensor_scalar(self.w_dn[:, :, :].rearrange("p k d -> p (k d)"), self.w_int[:, 2, :], INT_SCALE, None,
                        ALU.mult).then_inc(self.w_ready, 1)


def ffn_phase(nc, inputs, x_res, ln, ln_next, sem_of, load_next, clear_next):
    with ExitStack() as ctx:
        def sb(name, shape, dt=F32):
            return ctx.enter_context(nc.sbuf_tensor("ff_" + name, shape, dt))

        def bank(name):
            return ctx.enter_context(nc.psum_tensor("ff_" + name, [P, 512], F32))

        sem = sem_of("ff")
        ident, w_gu, w_dn, w_ready = inputs.ident, inputs.w_gu, inputs.w_dn, inputs.w_ready
        xn = [sb(f"xn{i}", [P, TPC, P]) for i in range(2)]
        xnT = [sb(f"xnT{i}", [P, CW]) for i in range(2)]
        silu = [sb(f"silu{i}", [P, CW]) for i in range(2)]
        h = [sb(f"h{i}", [P, HB, CW]) for i in range(2)]
        xt_bank = bank("xt")
        g_bank = [bank(f"g{i}") for i in range(2)]
        u_bank = [bank(f"u{i}") for i in range(2)]
        y_bank = bank("y")
        xn_ready, tx_done, xT_ready = sem("xn_ready"), sem("tx_done"), sem("xT_ready")
        gate_done, up_done, silu_ready, h_ready = sem("gate_done"), sem("up_done"), sem("silu_ready"), sem("h_ready")
        down_done, x_ready = sem("down_done"), sem("x_ready")
        chain = [sem(f"chain{i}") for i in range(3)]
        block = ctx.enter_context(nc.Block())

        @block.sync
        def _(sp):
            load_next(sp)

        @block.gpsimd
        def _(pool):
            clear_next(nc.gpsimd)

        @block.tensor
        def _(pe):
            mm = nc.tensor.matmul

            def transpose_x(c):
                pe.wait_ge(xn_ready, c.count(1, 1))
                pe.wait_ge(xT_ready, c.count(1))
                for a in range(TPC):
                    last = nc.tensor.transpose(xt_bank[:, a * P:(a + 1) * P], xn[c.par][:, a, :], ident[:, :])
                last.then_inc(tx_done, 1)

            def gate_and_up(c, k, first=False):
                n = (c.par * HB + k) % 2
                if not first:
                    pe.wait_ge(h_ready, c.count(HB, k - 1))
                mm(g_bank[n][:, :], w_gu[:, 0, k * P:(k + 1) * P], xnT[c.par][:, :], start=True, stop=True).then_inc(gate_done, 1)
                mm(u_bank[n][:, :], w_gu[:, 1, k * P:(k + 1) * P], xnT[c.par][:, :], start=True, stop=True).then_inc(up_done, 1)

            def down(c):
                pe.wait_ge(x_ready, c.count(1))
                pe.wait_ge(h_ready, c.count(HB, HB))
                for a in range(TPC):
                    for k in range(HB):
                        done = mm(y_bank[:, a * P:(a + 1) * P], h[c.par][:, k, a * P:(a + 1) * P], w_dn[:, k, :],
                                  start=k == 0, stop=k == HB - 1)
                done.then_inc(down_done, 1)

            def body(c, first=False, last=False):
                gate_and_up(c, 1, first)
                if not last:
                    transpose_x(c + 1)
                gate_and_up(c, 2)
                if not last:
                    pe.wait_ge(xT_ready, (c + 1).count(1, 1))
                    gate_and_up(c + 1, 0)
                down(c)

            pe.wait_ge(w_ready, 2)
            transpose_x(At(0, 0))
            pe.wait_ge(xT_ready, 1)
            gate_and_up(At(0, 0), 0, first=True)
            body(At(0, 0), first=True)
            for c in (1, 2):
                body(At(0, c))
            body(At(0, 3), last=True)

        @block.scalar
        def _(act):
            def copy_xT(c):
                act.wait_ge(tx_done, c.count(1, 1))
                nc.scalar.copy(xnT[c.par][:, :], xt_bank[:, :]).then_inc(xT_ready, 1)

            def body(c, first=False, last=False):
                for k in range(HB):
                    n = (c.par * HB + k) % 2
                    act.wait_ge(gate_done, c.count(HB, k + 1))
                    if not (first and k < 2):
                        act.wait_ge(h_ready, c.count(HB, k - 1))
                    nc.scalar.activation(silu[n][:, :], g_bank[n][:, :], ACT.Silu).then_inc(silu_ready, 1)
                    if k == 1 and not last:
                        copy_xT(c + 1)

            copy_xT(At(0, 0))
            body(At(0, 0), first=True)
            for c in (1, 2):
                body(At(0, c))
            body(At(0, 3), last=True)

        @block.vector
        def _(dve):
            v = nc.vector

            def next_stats(c, link):
                dve.wait_ge(x_ready, c + 1)
                layernorm_stats(nc, link, x_res, ln_next, c * TPC, (c + 1) * TPC)

            def body(c, link, first=False, last=False):
                if not last:
                    normalize_chunk(nc, x_res, ln, c.c + 1, xn[(c + 1).par], xn_ready)
                for k in range(HB):
                    n = (c.par * HB + k) % 2
                    dve.wait_ge(silu_ready, c.count(HB, k + 1))
                    dve.wait_ge(up_done, c.count(HB, k + 1))
                    v.tensor_tensor(h[c.par][:, k, :], silu[n][:, :], u_bank[n][:, :], ALU.mult).then_inc(h_ready, 1)
                if c.c:
                    next_stats(c.c - 1, link)
                dve.wait_ge(down_done, c.count(1, 1))
                x = x_res[:, bass.ds(c.count(CW), CW)]
                v.tensor_tensor(x, x, y_bank[:, :], ALU.add).then_inc(x_ready, 1)

            link = Chain(dve, chain[0])
            normalize_chunk(nc, x_res, ln, 0, xn[0], xn_ready)
            layernorm_stats(nc, link, x_res, ln, TILES - TPC, TILES)
            body(At(0, 0), link, first=True)
            link = Chain(dve, chain[1])
            for c in (1, 2):
                body(At(0, c), link)
            link = Chain(dve, chain[2])
            body(At(0, 3), link, last=True)


MIN_P = -1e38
RECIPROCAL_MAGIC = float(0x7EF311C3)
MIX = ("k", "v", "r")


class WkvInputs:

    def __init__(self, ctx, nc):
        def sb(name, shape):
            return ctx.enter_context(nc.sbuf_tensor("wk_" + name, shape, F32))

        self.w = {m: sb("w_" + m, [P, P]) for m in ("k", "v", "r", "o")}
        self.ident = sb("ident", [P, P])
        self.cols = sb("cols", [P, 5])
        self.loaded = ctx.enter_context(nc.semaphore("wk_loaded"))

    def load(self, sp, W, U, mixes, weights_t, ident_in):
        for n, col in enumerate((W, U, *mixes)):
            sp.dma_start(self.cols[:, n:n + 1], col).then_inc(self.loaded, 16)
        for m, src in zip(("k", "v", "r", "o"), weights_t):
            sp.dma_start(self.w[m][:, :], src).then_inc(self.loaded, 16)
        sp.dma_start(self.ident[:, :], ident_in).then_inc(self.loaded, 16)


def wkv_phase(nc, inputs, x_res, ln, ln_next, sem_of):
    with ExitStack() as ctx:
        def sb(name, shape, dt=F32):
            return ctx.enter_context(nc.sbuf_tensor("wk_" + name, shape, dt))

        def bank(name):
            return ctx.enter_context(nc.psum_tensor("wk_" + name, [P, 512], F32))

        sem = sem_of("wk")
        NB = CW // T
        w, ident, cols, w_loaded = inputs.w, inputs.ident, inputs.cols, inputs.loaded
        decay = sb("decay", [P, 2])
        keep = sb("keep", [P, 3])
        xn = [sb(f"xn{i}", [P, TPC, P]) for i in range(2)]
        xT = [sb(f"xT{i}", [P, NB, T + 1]) for i in range(2)]
        mixed = {m: sb("mixed_" + m, [P, NB, T]) for m in MIX}
        kept = {m: sb("kept_" + m, [P, NB, T]) for m in MIX}
        V = sb("V", [P, NB, T])
        R = [sb(f"R{i}", [P, NB, T]) for i in range(2)]
        num, den, inv_den = ([sb(f"{n}{i}", [P, NB, T]) for i in range(2)] for n in ("num", "den", "inv_den"))
        newton = sb("newton", [P, NB, T])
        pp = sb("pp", [P, NB, T + 1])
        aa = sb("aa", [P, NB, T + 1])
        bb = sb("bb", [P, NB, T + 1])
        names = ("d1", "d2", "g1", "g2", "e1", "e2", "e1b", "e2b", "ev", "t1", "t2", "t3")
        e = {n: sb(n, [P, NB, T]) for n in names}
        rw = [sb(f"rw{i}", [P, NB, T]) for i in range(2)]
        xt_bank, k_bank, v_bank, r_bank = bank("xt"), bank("k"), bank("v"), bank("r")
        y_bank = [bank(f"y{i}") for i in range(2)]
        consts, xn_ready, tx_done, xT_ready = (
            sem("consts"), sem("xn_ready"), sem("tx_done"), sem("xT_ready"))
        kept_ready, mixed_ready, proj_done, k_used, v_copied, er_ready = (
            sem("kept_ready"), sem("mixed_ready"), sem("proj_done"), sem("k_used"), sem("v_copied"), sem("er_ready"))
        d_ready, relu_ready, e_ready, sums_ready = sem("d_ready"), sem("relu_ready"), sem("e_ready"), sem("sums_ready")
        den_ready, inv_ready = sem("den_ready"), sem("inv_ready")
        rw_ready, out_done, x_ready, decay_ready = sem("rw_ready"), sem("out_done"), sem("x_ready"), sem("decay_ready")
        chain, pool_chain = sem("chain"), sem("pool_chain")
        block = ctx.enter_context(nc.Block())

        @block.gpsimd
        def _(pool):
            g = nc.gpsimd
            g.memset(pp[:, :, 0:1], MIN_P).then_inc(consts, 1)
            g.memset(aa[:, :, 0:1], 0.0).then_inc(consts, 1)
            g.memset(bb[:, :, 0:1], 0.0).then_inc(consts, 1)
            for i in range(2):
                g.memset(xT[i][:, :, 0:1], 0.0).then_inc(consts, 1)
            pool.wait_ge(w_loaded, 160)
            g.tensor_scalar(keep[:, :], cols[:, 2:5], -1.0, 1.0, ALU.mult, ALU.add).then_inc(consts, 1)
            pool.wait_ge(decay_ready, 1)
            g.tensor_scalar(decay[:, 1:2], decay[:, 0:1], -1.0, None, ALU.mult).then_inc(consts, 1)

            def invert(c):
                x, y, a = (t[:, :, :] for t in (den[c.par], inv_den[c.par], newton))
                pool.wait_ge(den_ready, c.count(1, 1))
                pool.wait_ge(rw_ready, c.count(1, -1))
                link(g.tensor_scalar(y.bitcast(I32), x.bitcast(I32), -1.0, RECIPROCAL_MAGIC, ALU.mult, ALU.add))
                for n in range(3):
                    link(g.tensor_tensor(a, x, y, ALU.mult))
                    link(g.tensor_scalar(a, a, -1.0, 2.0, ALU.mult, ALU.add))
                    done = g.tensor_tensor(y, a, y, ALU.mult)
                    if n < 2:
                        link(done)
                done.then_inc(inv_ready, 1)

            link = Chain(pool, pool_chain)
            for c in range(CHUNKS - 1):
                invert(At(0, c))

        @block.tensor
        def _(pe):
            mm = nc.tensor.matmul

            def transpose_x(c):
                pe.wait_ge(xn_ready, c.count(1, 1))
                pe.wait_ge(xT_ready, c.count(1))
                for a in range(TPC):
                    last = nc.tensor.transpose(xt_bank[:, a * P:(a + 1) * P], xn[c.par][:, a, :], ident[:, :])
                last.then_inc(tx_done, 1)

            def project(c):
                for n, (m, dst) in enumerate((("k", k_bank), ("v", v_bank), ("r", r_bank))):
                    pe.wait_ge(mixed_ready, c.count(3, n + 1))
                    if m == "k":
                        pe.wait_ge(d_ready, c.count(3))
                    if m == "v":
                        pe.wait_ge(v_copied, c.count(1))
                    if m == "r":
                        pe.wait_ge(er_ready, c.count(1))
                    mm(dst[:, :], w[m][:, :], mixed[m][:, :, :].rearrange("p b t -> p (b t)"),
                       start=True, stop=True).then_inc(proj_done, 1)

            def output(c):
                pe.wait_ge(rw_ready, c.count(1, 1))
                pe.wait_ge(x_ready, c.count(1, -1))
                r = rw[c.par][:, :, :].rearrange("p b t -> p (b t)")
                for a in range(TPC):
                    done = mm(y_bank[c.par][:, a * P:(a + 1) * P], r[:, a * P:(a + 1) * P], w["o"][:, :], start=True, stop=True)
                done.then_inc(out_done, 1)

            pe.wait_ge(w_loaded, 160)
            transpose_x(At(0, 0))
            project(At(0, 0))
            for c in range(CHUNKS):
                if c < CHUNKS - 1:
                    transpose_x(At(0, c + 1))
                if c < CHUNKS - 1:
                    project(At(0, c + 1))
                if c:
                    output(At(0, c - 1))
            output(At(0, CHUNKS - 1))

        @block.scalar
        def _(act):
            def copy_xT(c):
                act.wait_ge(tx_done, c.count(1, 1))
                nc.scalar.copy(xT[c.par][:, :, 1:T + 1], xt_bank[:, :].rearrange("p (b t) -> p b t", b=NB)).then_inc(xT_ready, 1)

            def keep_last(c):
                act.wait_ge(xT_ready, c.count(1, 1))
                act.wait_ge(consts, 7)
                for n, m in enumerate(MIX):
                    act.wait_ge(mixed_ready, c.count(3, n - 2))
                    nc.scalar.activation(kept[m][:, :, :], xT[c.par][:, :, 0:T], ACT.Copy,
                                         scale=keep[:, n:n + 1]).then_inc(kept_ready, 1)

            def exp(c, dst, src, scale=1.0):
                nc.scalar.activation(dst[:, :, :], src[:, :, :], ACT.Exp, scale=scale).then_inc(e_ready, 1)

            def body(c, last=False):
                view = lambda b: b[:, :].rearrange("p (b t) -> p b t", b=NB)
                act.wait_ge(den_ready, c.count(1))
                act.wait_ge(proj_done, c.count(3, 2))
                nc.scalar.copy(V[:, :, :], view(v_bank)).then_inc(v_copied, 1)
                for n, (dst, src) in enumerate((("e1b", "g1"), ("e2b", "g2"))):
                    act.wait_ge(d_ready, c.count(3, n + 1))
                    exp(c, e[dst], e[src])
                act.wait_ge(d_ready, c.count(3, 3))
                for dst, sign in (("d1", 1.0), ("d2", -1.0)):
                    nc.scalar.activation(e[dst][:, :, :], e["t2"][:, :, :], ACT.Relu, scale=sign).then_inc(relu_ready, 1)
                for n, (dst, src) in enumerate((("e1", "d1"), ("e2", "d2"))):
                    act.wait_ge(relu_ready, c.count(2, n + 1))
                    exp(c, e[dst], e[src], -1.0)
                if not last:
                    copy_xT(c + 1)
                    keep_last(c + 1)
                act.wait_ge(proj_done, c.count(3, 3))
                act.wait_ge(rw_ready, c.count(1, -1))
                nc.scalar.activation(R[c.par][:, :, :], view(r_bank), ACT.Sigmoid).then_inc(er_ready, 1)

            act.wait_ge(w_loaded, 160)
            nc.scalar.activation(decay[:, 0:1], cols[:, 0:1], ACT.Exp).then_inc(decay_ready, 1)
            act.wait_ge(consts, 5)
            copy_xT(At(0, 0))
            keep_last(At(0, 0))
            body(At(0, 0))
            for c in (1, 2):
                body(At(0, c))
            body(At(0, 3), last=True)

        @block.vector
        def _(dve):
            v = nc.vector

            def mix(c):
                for n, m in enumerate(MIX):
                    dve.wait_ge(kept_ready, c.count(3, n + 1))
                    dve.wait_ge(proj_done, c.count(3, n - 2))
                    v.scalar_tensor_tensor(mixed[m][:, :, :], xT[c.par][:, :, 1:T + 1], cols[:, 2 + n:3 + n],
                                           kept[m][:, :, :], ALU.mult, ALU.add).then_inc(mixed_ready, 1)

            def finish(c, link):
                n = num[c.par][:, :, :]
                link(v.tensor_tensor(n, n, inv_den[c.par][:, :, :], ALU.mult))
                dve.wait_ge(er_ready, c.count(1, 1))
                v.tensor_tensor(rw[c.par][:, :, :], n, R[c.par][:, :, :], ALU.mult).then_inc(rw_ready, 1)

            def finish_chunk(c, link):
                dve.wait_ge(inv_ready, c.count(1, 1))
                finish(c, link)

            def total(c, link):
                product = lambda dst, x, y: link.done(v.tensor_tensor(e[dst][:, :, :], x, y, ALU.mult))
                dve.wait_ge(sums_ready, c.count(2, 2))
                dve.wait_ge(e_ready, c.count(4, 4))
                product("t1", e["e1"][:, :, :], aa[:, :, 0:T])
                product("t2", e["e2"][:, :, :], V[:, :, :])
                product("t3", e["e1"][:, :, :], bb[:, :, 0:T])
                link.wait()
                v.tensor_tensor(den[c.par][:, :, :], e["t3"][:, :, :], e["e2"][:, :, :], ALU.add).then_inc(den_ready, 1)
                link.done(v.tensor_tensor(num[c.par][:, :, :], e["t2"][:, :, :], e["t1"][:, :, :], ALU.add))

            def residual(c):
                dve.wait_ge(out_done, c.count(1, 1))
                x = x_res[:, bass.ds(c.count(CW), CW)]
                v.tensor_tensor(x, x, y_bank[c.par][:, :], ALU.add).then_inc(x_ready, 1)

            def body(c, link, last=False):
                K = k_bank[:, :].rearrange("p (b t) -> p b t", b=NB)
                now, nxt = pp[:, :, 0:T], pp[:, :, 1:T + 1]
                dve.wait_ge(proj_done, c.count(3, 1))
                for b in range(NB):
                    link.done(v.tensor_tensor_scan(pp[:, b, 1:T + 1], decay[:, 1:2].to_broadcast([P, T]), K[:, b, :],
                                                   MIN_P, ALU.add, ALU.max))
                link.wait()
                v.scalar_tensor_tensor(e["g1"][:, :, :], now, decay[:, 1:2], nxt, ALU.add, ALU.subtract).then_inc(d_ready, 1)
                v.tensor_tensor(e["g2"][:, :, :], K, nxt, ALU.subtract).then_inc(d_ready, 1)
                v.scalar_tensor_tensor(e["t2"][:, :, :], K, cols[:, 1:2], now, ALU.add, ALU.subtract).then_inc(d_ready, 1)
                if not last:
                    normalize_chunk(nc, x_res, ln, c.c + 1, xn[(c + 1).par], xn_ready)
                if c.c > 1:
                    residual(c + -2)
                dve.wait_ge(d_ready, c.count(3, 3))
                dve.wait_ge(e_ready, c.count(4, 2))
                dve.wait_ge(v_copied, c.count(1, 1))
                link(v.tensor_tensor(e["ev"][:, :, :], e["e2b"][:, :, :], V[:, :, :], ALU.mult))
                for src, dst in (("ev", aa), ("e2b", bb)):
                    for b in range(NB):
                        done = v.tensor_tensor_scan(dst[:, b, 1:T + 1], e["e1b"][:, b, :], e[src][:, b, :],
                                                    0.0, ALU.mult, ALU.add)
                        if b < NB - 1:
                            link.done(done)
                    done.then_inc(sums_ready, 1)
                if not last:
                    mix(c + 1)
                total(c, link)
                if last:
                    dve.wait_ge(den_ready, c.count(1, 1))
                    link(v.reciprocal(inv_den[c.par][:, :, :], den[c.par][:, :, :]))
                if c.c:
                    finish_chunk(c + -1, link)

            link = Chain(dve, chain)
            normalize_chunk(nc, x_res, ln, 0, xn[0], xn_ready)
            layernorm_stats(nc, link, x_res, ln, TILES - TPC, TILES)
            mix(At(0, 0))
            dve.wait_ge(consts, 7)
            for c in range(CHUNKS):
                body(At(0, c), link, last=c == CHUNKS - 1)
            finish(At(0, CHUNKS - 1), link)
            dve.wait_ge(x_ready, CHUNKS - 2)
            layernorm_stats(nc, link, x_res, ln_next, 0, 2 * TPC)
            residual(At(0, CHUNKS - 2))
            residual(At(0, CHUNKS - 1))


EXPERTS, EXPERT_HIDDEN, CAPACITY = 8, 512, 320
SLOTS = EXPERTS * CAPACITY
KB = EXPERT_HIDDEN // P
SLOT_TILES = ((0, 128), (128, 128), (256, 64))
GROUP = 4
GROUPS = SLOTS // P // GROUP
ROW = P + 2 * EXPERTS
FAR = 1e6


def moe_consts(np):
    tokens = np.arange(TILES, dtype=np.float32) * P + np.arange(P, dtype=np.float32)[:, None]
    return {
        "iota": np.tile(np.arange(EXPERTS, dtype=np.float32), (P, 1)),
        "tri": np.triu(np.ones((P, P), np.float32)),
        "tokens": tokens,
    }


class MoeInputs:

    def __init__(self, ctx, nc):
        def sb(name, shape):
            return ctx.enter_context(nc.sbuf_tensor("mo_" + name, shape, F32))

        self.ident, self.tri32 = sb("ident", [P, P]), sb("tri32", [P, P])
        self.iota, self.tokens = sb("iota", [P, EXPERTS]), sb("tokens", [P, TILES])
        self.rw, self.rb = sb("rw", [P, EXPERTS]), sb("rb", [P, EXPERTS])
        self.b1_rows, self.b2 = sb("b1_rows", [EXPERTS * KB, P]), sb("b2", [P, EXPERTS * P])
        self.w1 = [sb(f"w1_{i}", [P, EXPERT_HIDDEN]) for i in range(2)]
        self.w2 = [sb(f"w2_{i}", [P, KB, P]) for i in range(2)]
        self.empty, self.zero = sb("empty", [P, SLOTS // P, ROW]), sb("zero", [P, TILES * P])
        self.slots = nc.dram_tensor("mo_slots", [SLOTS, ROW], F32).ap()
        self.answers = nc.dram_tensor("mo_answers", [2 * TOKENS, P], F32).ap()
        self.blank_ready, self.emptied, self.zeroed = (
            ctx.enter_context(nc.semaphore("mo_" + n)) for n in ("blank_ready", "emptied", "zeroed"))
        self.consts_loaded, *self.w1_loaded = (ctx.enter_context(nc.semaphore(n)) for n in ("mo_consts", "mo_w1_0", "mo_w1_1"))
        self.w2_loaded = [ctx.enter_context(nc.semaphore(f"mo_w2_{i}")) for i in range(2)]

    def load(self, sp, a):
        for dst, src in ((self.ident[:, :], a["c_ident"]), (self.rw[:, :], a["router_w"]), (self.tri32[:, :], a["tri"]),
                         (self.iota[:, :], a["iota"]), (self.tokens[:, :], a["tokens"]),
                         (self.rb[:, :], a["router_b"].partition_broadcast(P)),
                         (self.b1_rows[:, :], a["b1"].rearrange("e (k p) -> (e k) p", p=P)),
                         (self.b2[:, :], a["b2"].rearrange("e d -> (e d)").partition_broadcast(P))):
            sp.dma_start(dst, src).then_inc(self.consts_loaded, 16)
        for e in (At(0, 0), At(0, 1)):
            self.load_w1(sp, a, e)
            self.load_w2(sp, a, e)

    def make_blanks(self, g):
        g.memset(self.empty[:, :, 0:P + EXPERTS], 0.0).then_inc(self.blank_ready, 1)
        g.memset(self.empty[:, :, P + EXPERTS:ROW], FAR).then_inc(self.blank_ready, 1)
        g.memset(self.zero[:, :], 0.0).then_inc(self.blank_ready, 1)

    def clear(self, sp):
        sp.wait_ge(self.blank_ready, 3)
        sp.dma_start(self.slots.rearrange("(p a) d -> p (a d)", p=P),
                     self.empty[:, :, :].rearrange("p a d -> p (a d)")).then_inc(self.emptied, 16)
        for k in range(2):
            sp.dma_start(self.answers[k * TOKENS:(k + 1) * TOKENS, :].rearrange("(p a) d -> p (a d)", p=P),
                         self.zero[:, :]).then_inc(self.zeroed, 16)

    def load_w1(self, sp, a, e):
        sp.dma_start(self.w1[e.par][:, :], a["w1"][bass.ds(e.count(1), 1), :, :].rearrange("e p h -> (e p) h")).then_inc(
            self.w1_loaded[e.par], 16)

    def load_w2(self, sp, a, e):
        sp.dma_start(self.w2[e.par][:, :, :], a["w2"][bass.ds(e.count(1), 1), :, :].rearrange(
            "e (k p) d -> p (e k) d", p=P)).then_inc(self.w2_loaded[e.par], 16)


def moe_phase(nc, inputs, a, out, x_res, ln, sem_of):
    with ExitStack() as ctx:
        def sb(name, shape, dt=F32):
            return ctx.enter_context(nc.sbuf_tensor("mo_" + name, shape, dt))

        def bank(name):
            return ctx.enter_context(nc.psum_tensor("mo_" + name, [P, 512], F32))

        sem = sem_of("mo")
        slots, answers, emptied, zeroed = inputs.slots, inputs.answers, inputs.emptied, inputs.zeroed
        SPP = SLOTS // P
        ident, tri32, iota, tokens, rw, rb, b1_rows, b2, w1, w2 = (
            inputs.ident, inputs.tri32, inputs.iota, inputs.tokens, inputs.rw, inputs.rb, inputs.b1_rows, inputs.b2,
            inputs.w1, inputs.w2)
        consts_loaded, w1_loaded, w2_loaded = inputs.consts_loaded, inputs.w1_loaded, inputs.w2_loaded
        tri, ones = sb("tri", [P, P], BF16), sb("ones", [P, P], BF16)
        far_iota, slot_base = (sb(n, [P, EXPERTS]) for n in ("far_iota", "slot_base"))
        b1 = sb("b1", [P, EXPERTS * KB])
        rows = sb("rows", [P, TILES, ROW])
        xT = [sb(f"xT{i}", [P, CW]) for i in range(2)]
        wide = lambda n, dt=F32: sb(n, [P, TPC, EXPERTS], dt)
        logits, eq, cand, masked, prod, over, slot = (
            wide(n) for n in ("logits", "eq", "cand", "masked", "prod", "over", "slot"))
        hot = [wide(f"hot{k}") for k in range(2)]
        mask = sb("mask", [P, TILES, EXPERTS], BF16)
        top, denom, best, expert = (sb(n, [P, TPC]) for n in ("top", "denom", "best", "expert"))
        put = [sb(f"put{k}", [P, TILES], U32) for k in range(2)]
        xe, xeT = sb("xe", [P, SPP, P]), sb("xeT", [P, SLOTS])
        meta = sb("meta", [P, EXPERTS, 3, 2 * EXPERTS])
        to, gate = sb("to", [P, EXPERTS * 3], U32), sb("gate", [P, EXPERTS * 3])
        hT = [sb(f"hT{i}", [P, KB, CAPACITY]) for i in range(2)]
        ye = [sb(f"ye{i}", [P, 3, P]) for i in range(2)]
        got = sb("got", [P, 2, TILES, P])
        xt_bank, route_bank = bank("xt"), bank("route")
        h_bank = [bank(f"h{k}") for k in range(KB)]
        y_bank = [bank(f"y{i}") for i in range(2)]
        slot_banks = (xt_bank, route_bank)

        consts_ready = sem("consts_ready")
        xn_ready, tx_done, xT_ready, logits_done = sem("xn_ready"), sem("tx_done"), sem("xT_ready"), sem("logits_done")
        shifted, exp_ready, mask_ready, counts_done = sem("shifted"), sem("exp_ready"), sem("mask_ready"), sem("counts_done")
        b1_done, b1_ready = sem("b1_done"), sem("b1_ready")
        routed, scattered = sem("routed"), sem("scattered")
        xe_loaded, meta_loaded = [sem(f"xe_loaded{g}") for g in range(GROUPS)], sem("meta_loaded")
        te_done, xeT_ready, up_done, gelu_ready, down_done = (
            sem("te_done"), sem("xeT_ready"), sem("up_done"), sem("gelu_ready"), sem("down_done"))
        meta_read, y_read, ye_ready = sem("meta_read"), sem("y_read"), sem("ye_ready")
        ye_out = [sem(f"ye_out{i}") for i in range(2)]
        got_loaded = [sem(f"got_loaded{c}") for c in range(CHUNKS)]
        y_ready, stored = sem("y_ready"), sem("stored")
        chain = sem("chain")
        CONSTS = 16 * 8
        block = ctx.enter_context(nc.Block())
        out_tiles = out.rearrange("(a p) d -> p a d", p=P)

        @block.sync
        def _(sp):
            sp.wait_ge(scattered, 16 * 2 * TILES)
            for g in range(GROUPS):
                sp.dma_start(xe[:, g * GROUP:(g + 1) * GROUP, :],
                             slots[g * GROUP * P:(g + 1) * GROUP * P, 0:P].rearrange("(a p) d -> p a d", p=P)).then_inc(xe_loaded[g], 16)
            by_expert = slots[:, P:ROW].rearrange("(e s) d -> s e d", e=EXPERTS)
            for n, (at, r) in enumerate(SLOT_TILES):
                sp.dma_start(meta[0:r, :, n, :], by_expert[at:at + r, :, :]).then_inc(meta_loaded, 16)

            def body(e):
                sp.wait_ge(up_done, e.count(KB, KB))
                inputs.load_w1(sp, a, e + 2)
                sp.wait_ge(down_done, e.count(1, 1))
                inputs.load_w2(sp, a, e + 2)

            with sp.Fori(0, 3) as i:
                for c in (0, 1):
                    body(At(i, c))
            for i in range(2):
                sp.wait_ge(ye_out[i], 16 * 3 * (EXPERTS // 2))
            for c in range(CHUNKS):
                for k in range(2):
                    at = k * TOKENS + c * CW
                    sp.dma_start(got[:, k, c * TPC:(c + 1) * TPC, :],
                                 answers[at:at + CW, :].rearrange("(a p) d -> p a d", p=P)).then_inc(got_loaded[c], 16)

        @block.gpsimd
        def _(pool):
            g = nc.gpsimd
            g.memset(ones[:, :], 1.0).then_inc(consts_ready, 1)
            pool.wait_ge(consts_loaded, CONSTS)
            g.tensor_copy(tri[:, :], tri32[:, :]).then_inc(consts_ready, 1)
            g.tensor_scalar(far_iota[:, :], iota[:, :], float(EXPERTS), None, ALU.add).then_inc(consts_ready, 1)
            g.tensor_scalar(slot_base[:, :], iota[:, :], float(CAPACITY), -1.0, ALU.mult, ALU.add).then_inc(consts_ready, 1)
            pool.wait_ge(emptied, 16)
            for t in range(TILES):
                if t % TPC == 0:
                    pool.wait_ge(routed, 2 * (t // TPC + 1))
                for k in range(2):
                    g.indirect_dma_start(slots, bass.IndirectOffsetOnAxis(put[k][:, t:t + 1], 0), rows[:, t, :], None,
                                         bounds_check=SLOTS - 1, oob_is_err=False).then_inc(scattered, 16)
            pool.wait_ge(zeroed, 32)
            for e in range(EXPERTS):
                pool.wait_ge(ye_ready, e + 1)
                for n, (_, r) in enumerate(SLOT_TILES):
                    g.indirect_dma_start(answers, bass.IndirectOffsetOnAxis(to[0:r, 3 * e + n:3 * e + n + 1], 0), ye[e % 2][0:r, n, :],
                                         None, bounds_check=2 * TOKENS - 1, oob_is_err=False).then_inc(ye_out[e % 2], 16)

        @block.tensor
        def _(pe):
            mm = nc.tensor.matmul
            N = TPC * EXPERTS
            def route(c):
                pe.wait_ge(xn_ready, c + 1)
                pe.wait_ge(xT_ready, c)
                for n in range(TPC):
                    last = nc.tensor.transpose(xt_bank[:, n * P:(n + 1) * P], rows[:, c * TPC + n, 0:P], ident[:, :])
                last.then_inc(tx_done, 1)
                pe.wait_ge(xT_ready, c + 1)
                for n in range(TPC):
                    last = mm(route_bank[:, n * EXPERTS:(n + 1) * EXPERTS], xT[c % 2][:, n * P:(n + 1) * P], rw[:, :],
                              start=True, stop=True)
                last.then_inc(logits_done, 1)

            def count(c):
                pe.wait_ge(mask_ready, c + 1)
                place = y_bank[0][:, 0:N].rearrange("p (t e) -> p t e", e=EXPERTS)
                last = mm(place, tri[:, :], mask[:, c * TPC:(c + 1) * TPC, :], start=True, stop=False)
                for t in range((c + 1) * TPC - 1):
                    first = max(t - c * TPC + 1, 0)
                    width = [P, TPC - first, EXPERTS]
                    last = mm(place[:, first:TPC, :], ones[:, :], mask[:, t:t + 1, :].to_broadcast(width),
                              start=False, stop=t == (c + 1) * TPC - 2)
                last.then_inc(counts_done, 1)

            pe.wait_ge(consts_loaded, CONSTS)
            route(0)
            nc.tensor.transpose(h_bank[0][:, 0:EXPERTS * KB], b1_rows[:, :], ident[0:EXPERTS * KB, 0:EXPERTS * KB]).then_inc(b1_done, 1)
            pe.wait_ge(consts_ready, 4)
            for c in range(CHUNKS):
                if c < CHUNKS - 1:
                    pe.wait_ge(shifted, c + 1)
                    route(c + 1)
                count(c)

            def transpose_slots(g):
                pe.wait_ge(xe_loaded[g], 16)
                if g > 1:
                    pe.wait_ge(xeT_ready, g - 1)
                for n in range(GROUP):
                    last = nc.tensor.transpose(slot_banks[g % 2][:, n * P:(n + 1) * P], xe[:, g * GROUP + n, :], ident[:, :])
                last.then_inc(te_done, 1)

            def up(e):
                pe.wait_ge(w1_loaded[e.par], e.half(16, 16))
                for k in range(KB):
                    pe.wait_ge(gelu_ready, e.count(KB, k - KB + 1))
                    mm(h_bank[k][:, 0:CAPACITY], w1[e.par][:, k * P:(k + 1) * P], xeT[:, bass.ds(e.count(CAPACITY), CAPACITY)],
                       start=True, stop=True).then_inc(up_done, 1)

            def down(e):
                pe.wait_ge(y_read, e.count(1, -1))
                pe.wait_ge(gelu_ready, e.count(KB, KB))
                pe.wait_ge(w2_loaded[e.par], e.half(16, 16))
                for n, (at, r) in enumerate(SLOT_TILES):
                    for k in range(KB):
                        done = mm(y_bank[e.par][0:r, n * P:(n + 1) * P], hT[e.par][:, k, at:at + r], w2[e.par][:, k, :],
                                  start=k == 0, stop=k == KB - 1)
                done.then_inc(down_done, 1)

            def body(e, last=False):
                if not last:
                    up(e + 1)
                down(e)

            pe.wait_ge(b1_ready, 1)
            pe.wait_ge(routed, 2 * CHUNKS)
            for g in range(GROUPS):
                if g == 1:
                    pe.wait_ge(xeT_ready, 1)
                    up(At(0, 0))
                transpose_slots(g)
            pe.wait_ge(xeT_ready, GROUPS)
            body(At(0, 0))
            body(At(0, 1))
            with pe.Fori(0, 2) as i:
                for c in (2, 3):
                    body(At(i, c))
            body(At(0, 6))
            body(At(0, 7), last=True)

        @block.scalar
        def _(act):
            def copy_xT(c):
                act.wait_ge(tx_done, c + 1)
                nc.scalar.copy(xT[c % 2][:, :], xt_bank[:, :]).then_inc(xT_ready, 1)

            copy_xT(0)
            for c in range(CHUNKS):
                act.wait_ge(shifted, c + 1)
                nc.scalar.activation(logits[:, :, :], logits[:, :, :], ACT.Exp).then_inc(exp_ready, 1)
                if c < CHUNKS - 1:
                    copy_xT(c + 1)
            act.wait_ge(b1_done, 1)
            nc.scalar.copy(b1[:, :], h_bank[0][:, 0:EXPERTS * KB]).then_inc(b1_ready, 1)
            act.wait_ge(b1_ready, 1)

            def gelu(e):
                act.wait_ge(down_done, e.count(1, -1))
                for k in range(KB):
                    act.wait_ge(up_done, e.count(KB, k + 1))
                    nc.scalar.activation(hT[e.par][:, k, :], h_bank[k][:, 0:CAPACITY], ACT.Gelu,
                                         bias=b1[:, bass.ds(e.count(KB, k), 1)]).then_inc(gelu_ready, 1)

            for g in range(GROUPS):
                act.wait_ge(te_done, g + 1)
                nc.scalar.copy(xeT[:, g * GROUP * P:(g + 1) * GROUP * P], slot_banks[g % 2][:, :]).then_inc(xeT_ready, 1)
            gelu(At(0, 0))
            gelu(At(0, 1))
            with act.Fori(0, 3) as i:
                for c in (2, 3):
                    gelu(At(i, c))
            for c in range(CHUNKS):
                act.wait_ge(y_ready, c + 1)
                act.dma_start(out_tiles[:, c * TPC:(c + 1) * TPC, :],
                              x_res[:, c * CW:(c + 1) * CW].rearrange("p (a d) -> p a d", a=TPC)).then_inc(stored, 16)
            act.wait_ge(stored, 16 * CHUNKS)

        @block.vector
        def _(dve):
            v = nc.vector
            link = Chain(dve, chain)
            normalize_chunk(nc, x_res, ln, 0, rows[:, 0:TPC, :], xn_ready)
            layernorm_stats(nc, link, x_res, ln, 2 * TPC, TILES)

            shape = [P, TPC, EXPERTS]
            each = lambda t: t[:, :].unsqueeze(1).to_broadcast(shape)
            every = lambda t: t.unsqueeze(2).to_broadcast(shape)
            full = lambda t: t[:, :, :]
            tt = v.tensor_tensor

            def shift(c):
                dve.wait_ge(logits_done, c + 1)
                link(tt(full(logits), route_bank[:, 0:TPC * EXPERTS].rearrange("p (t e) -> p t e", e=EXPERTS), each(rb), ALU.add))
                link(v.reduce_max(top[:, :], full(logits), AX.X))
                tt(full(logits), full(logits), every(top[:, :]), ALU.subtract).then_inc(shifted, 1)

            def choose(c):
                dve.wait_ge(exp_ready, c + 1)
                gates = rows[:, c * TPC:(c + 1) * TPC, P:P + EXPERTS]
                link(v.reduce_sum(denom[:, :], full(logits), AX.X))
                link(v.reciprocal(denom[:, :], denom[:, :]))
                link(tt(gates, full(logits), every(denom[:, :]), ALU.mult))
                for k in range(2):
                    source = full(masked) if k else gates
                    link(v.reduce_max(best[:, :], source, AX.X))
                    link(tt(full(eq), source, every(best[:, :]), ALU.is_equal))
                    link(v.scalar_tensor_tensor(full(cand), full(eq), -float(EXPERTS), each(far_iota), ALU.mult, ALU.add))
                    link(v.tensor_reduce(expert[:, :], full(cand), AX.X, ALU.min))
                    link(tt(full(hot[k]), each(iota), every(expert[:, :]), ALU.is_equal))
                    if k == 0:
                        link(v.scalar_tensor_tensor(full(masked), full(hot[0]), -2.0, gates, ALU.mult, ALU.add))
                tt(mask[:, c * TPC:(c + 1) * TPC, :], full(hot[0]), full(hot[1]), ALU.add).then_inc(mask_ready, 1)
                link(v.scalar_tensor_tensor(rows[:, c * TPC:(c + 1) * TPC, P + EXPERTS:ROW], full(hot[1]), float(TOKENS),
                                            every(tokens[:, c * TPC:(c + 1) * TPC]), ALU.mult, ALU.add))

            def place(c):
                dve.wait_ge(counts_done, c + 1)
                places = y_bank[0][:, 0:TPC * EXPERTS].rearrange("p (t e) -> p t e", e=EXPERTS)
                link.done(v.tensor_scalar(full(over), places, float(CAPACITY), FAR, ALU.is_gt, ALU.mult))
                link(tt(full(slot), places, each(slot_base), ALU.add))
                link(tt(full(slot), full(slot), full(over), ALU.add))
                for k in range(2):
                    link(tt(full(prod), full(hot[k]), full(slot), ALU.mult))
                    link(v.reduce_sum(top[:, :], full(prod), AX.X))
                    v.tensor_copy(put[k][:, c * TPC:(c + 1) * TPC], top[:, :]).then_inc(routed, 1)
                    dve.wait_ge(routed, 2 * c + k + 1)

            dve.wait_ge(consts_ready, 4)
            for c in range(CHUNKS):
                shift(c)
                if c < CHUNKS - 1:
                    normalize_chunk(nc, x_res, ln, c + 1, rows[:, (c + 1) * TPC:(c + 2) * TPC, :], xn_ready)
                choose(c)
                place(c)

            dve.wait_ge(meta_loaded, 16 * 3)
            for e in range(EXPERTS):
                for q, dst in ((0, gate), (EXPERTS, to)):
                    for r, cols in ((P, slice(0, 2)), (64, slice(2, 3))):
                        last = v.tensor_copy(dst[0:r, 3 * e + cols.start:3 * e + cols.stop], meta[0:r, e, cols, q + e])
                last.then_inc(meta_read, 1)

            def body(e):
                dve.wait_ge(down_done, e.count(1, 1))
                dve.wait_ge(ye_out[e.par], e.half(48))
                bias = b2[:, bass.ds(e.count(P), P)]
                for n, (_, r) in enumerate(SLOT_TILES):
                    done = v.tensor_tensor(ye[e.par][0:r, n, :], y_bank[e.par][0:r, n * P:(n + 1) * P], bias[0:r, :], ALU.add)
                done.then_inc(y_read, 1)
                dve.wait_ge(y_read, e.count(1, 1))
                for n, (_, r) in enumerate(SLOT_TILES):
                    done = v.tensor_scalar(ye[e.par][0:r, n, :], ye[e.par][0:r, n, :], gate[0:r, bass.ds(e.count(3, n), 1)], None, ALU.mult)
                done.then_inc(ye_ready, 1)

            dve.wait_ge(meta_read, EXPERTS)
            body(At(0, 0))
            body(At(0, 1))
            with dve.Fori(0, 3) as i:
                for c in (2, 3):
                    body(At(i, c))

            for c in range(CHUNKS):
                dve.wait_ge(got_loaded[c], 32)
                x = x_res[:, c * CW:(c + 1) * CW]
                for k in range(2):
                    last = v.tensor_tensor(x, x, got[:, k, c * TPC:(c + 1) * TPC, :].rearrange("p a d -> p (a d)"), ALU.add)
                    if k == 0:
                        link(last)
                last.then_inc(y_ready, 1)


def attention_consts(np):
    pick = np.zeros((P, 3, 32), np.float32)
    for u in range(2):
        pick[:DV, u, 2 * u] = pick[DV:, u, 2 * u + 1] = 1
    pick[:, 2, 4:4 + P // DK] = np.repeat(np.eye(P // DK), DK, axis=0)
    sel = np.zeros((3 * HEADS, PAIRS, P), np.float32)
    for part in range(3):
        for h in range(HEADS):
            at = DV * (h % 2)
            sel[part * HEADS + h, h // 2, at:at + DV] = 1
    return {"ident": np.eye(P, dtype=np.float32), "pick": pick, "sel": sel}


def two_layer_program(nc, a, out):
    with ExitStack() as ctx:
        def sem_of(phase):
            return lambda name: ctx.enter_context(nc.semaphore(f"{phase}_{name}"))

        x_res = ctx.enter_context(nc.sbuf_tensor("x_res", [P, TILES * P], F32))
        parts = nc.dram_tensor("parts", [2, 3, 2 * HEADS * DK, T], BF16).ap()
        moe = {n: a["L1_ffn_" + n] for n in ("router_w", "router_b", "w1", "b1", "w2", "b2")}
        moe.update(c_ident=a["ident"], iota=a["iota"], tri=a["tri"], tokens=a["tokens"])
        ffn_inputs, wkv_inputs = FfnInputs(ctx, nc), WkvInputs(ctx, nc)

        ln_ffn, ln_wkv, ln_moe = (ln_tiles(lambda name, shape: ctx.enter_context(nc.sbuf_tensor(name + phase, shape, F32)))
                          for phase in ("_of_ffn", "_of_wkv", "_of_moe"))

        def load_ffn_and_wkv(sp):
            ffn_inputs.load(sp, a["L0_ffn_w_gate"], a["L0_ffn_w_up"], a["L0_ffn_w_down"], a["ident"])
            wkv_inputs.load(sp, a["L1_attn_W"], a["L1_attn_U"], [a["L1_attn_time_mix_" + m] for m in "kvr"],
                            [a["L1_attn_W" + m] for m in "kvro"], a["ident"])

        def load_moe(sp):
            moe_inputs.load(sp, moe)
            moe_inputs.clear(sp)

        attention_phase(nc, a["L0_attn_tokens"], a["L0_attn_Wq"], a["L0_attn_Wkv"], a["L0_attn_Wout"],
                        a["ident"], a["pick"], a["sel"], parts, x_res, sem_of, load_ffn_and_wkv, ffn_inputs.dequantise, ln_ffn)
        moe_inputs = MoeInputs(ctx, nc)
        ffn_phase(nc, ffn_inputs, x_res, ln_ffn, ln_wkv, sem_of, load_moe, moe_inputs.make_blanks)
        wkv_phase(nc, wkv_inputs, x_res, ln_wkv, ln_moe, sem_of)
        moe_phase(nc, moe_inputs, moe, out, x_res, ln_moe, sem_of)


def kernel(**inputs):
    import numpy as np
    import concourse.bacc as bacc
    from concourse.bass_utils import run_bass_kernel_spmd

    arrays = {}
    for name, a in inputs.items():
        a = np.asarray(a)
        if name.startswith(("L0_ffn_w_", "L1_attn_W")) and a.ndim == 2:
            a = a.T
        elif name.startswith("L1_attn_"):
            a = a.reshape(P, 1)
        arrays[name] = np.ascontiguousarray(a)
    arrays.update(attention_consts(np))
    arrays.update(moe_consts(np))
    nc = bacc.Bacc("TRN2", target_bir_lowering=False, num_devices=1)
    args = {name: nc.dram_tensor("in_" + name, a.shape, mybir.dt.from_np(a.dtype), kind="ExternalInput").ap()
            for name, a in arrays.items()}
    out = nc.dram_tensor("out", [BATCH, T, P], F32, kind="ExternalOutput").ap()
    two_layer_program(nc, args, out.rearrange("b t d -> (b t) d"))
    return run_bass_kernel_spmd(nc, [{"in_" + name: a for name, a in arrays.items()}], core_ids=[0]).results[0]["out"]
```
